# Optimizing a Trainium2 kernel written in Bass

```python
import numpy as np
import jax
import jax.numpy as jnp

def _softmax(x, axis=-1):
    return jax.nn.softmax(x, axis=axis)

def _gelu(x):
    return jax.nn.gelu(x, approximate=True)

def _silu(x):
    return jax.nn.silu(x)

def _sigmoid(x):
    return jax.nn.sigmoid(x)

def _layernorm(x, axis=-1, eps=1e-05):
    m = jnp.mean(x, axis=axis, keepdims=True)
    v = jnp.var(x, axis=axis, keepdims=True)
    return (x - m) / jnp.sqrt(v + eps)

def _scatter_add(tgt, idx, src, axis=0):
    return tgt.at[idx].add(src)

def _segment_sum(src, seg, n):
    return jax.ops.segment_sum(src, seg, n)
kernel_name = 'mk_vit_tower_postln_d2_tok_img1024_r4_4a0c2b'

def setup_inputs(seed: int=0):
    np.random.seed(seed)
    _w = jnp.asarray

    def _rec_inputs():
        import jax
        import jax.numpy as jnp
        _rk = jax.random.key(seed)
        x = -0.000169711 + 1.00022 * jax.random.normal(jax.random.fold_in(_rk, 1), (128, 3, 96, 96), jnp.float32)
        return x
    x = _rec_inputs()

    def _L0_tok_setup():
        import jax, jax.numpy as jnp
        import numpy as np
        C = 256
        H8 = 8
        DH = C // H8
        PS = 14
        CS = 3
        IMG = 168
        B = 4

        def _ln(x, g, b):
            mu = jnp.mean(x, axis=-1, keepdims=True)
            xc = x - mu
            var = jnp.mean(xc * xc, axis=-1, keepdims=True)
            return xc * jax.lax.rsqrt(var + 1e-05) * g + b

        def _forward(pixel_values, conv_w, class_emb, la_ln_q_g, la_ln_q_b, la_wq, la_ln_kv_g, la_ln_kv_b, la_wkv, la_proj_w, la_proj_b, ga_ln_q_g, ga_ln_q_b, ga_wq, ga_ln_kv_g, ga_ln_kv_b, ga_wkv, ga_proj_w, ga_proj_b, mod_w, mod_b):
            b = pixel_values.shape[0]
            pe = jax.lax.conv_general_dilated(pixel_values, conv_w, (PS, PS), 'VALID', dimension_numbers=('NCHW', 'OIHW', 'NCHW'))
            HP = pe.shape[2]
            h = HP // CS
            hw, N = (h * h, CS * CS)
            scale = C ** (-0.5)
            grid = pe.reshape(b, C, h, CS, h, CS)
            red = grid.mean(axis=(3, 5)).reshape(b, C, hw).transpose(0, 2, 1)
            win = grid.transpose(0, 2, 4, 3, 5, 1).reshape(b, hw, N, C)
            q = _ln(red, la_ln_q_g, la_ln_q_b) @ la_wq
            q = q.reshape(b, hw, H8, DH).transpose(0, 2, 1, 3)
            kv = _ln(win, la_ln_kv_g, la_ln_kv_b) @ la_wkv
            kv = kv.reshape(b, hw, N, 2, H8, DH).transpose(3, 0, 4, 1, 2, 5)
            k_, v_ = (kv[0], kv[1])
            attn = jax.nn.softmax(jnp.einsum('bhnd,bhnkd->bhnk', q * scale, k_), axis=-1)
            agg = jnp.einsum('bhnk,bhnkd->bhnd', attn, v_)
            agg = agg.transpose(0, 2, 1, 3).reshape(b, hw, C)
            local_out = red + agg @ la_proj_w + la_proj_b
            cls = jnp.broadcast_to(class_emb, (b, 1, C))
            gq = (_ln(cls, ga_ln_q_g, ga_ln_q_b) @ ga_wq).reshape(b, H8, DH)
            gkv = _ln(local_out, ga_ln_kv_g, ga_ln_kv_b) @ ga_wkv
            gkv = gkv.reshape(b, hw, 2, H8, DH).transpose(2, 0, 3, 1, 4)
            gk, gv = (gkv[0], gkv[1])
            gattn = jax.nn.softmax(jnp.einsum('bhd,bhnd->bhn', gq * scale, gk), axis=-1)
            gagg = jnp.einsum('bhn,bhnd->bhd', gattn, gv).reshape(b, 1, C)
            cls_out = cls + gagg @ ga_proj_w + ga_proj_b
            patch_out = local_out @ mod_w + mod_b
            return jnp.concatenate([patch_out, cls_out], axis=1)
        key = jax.random.key(seed)
        ks = jax.random.split(key, 16)
        nrm = lambda k, shape: jax.random.normal(k, shape, jnp.float32) * 0.02
        return {'pixel_values': jax.random.normal(ks[0], (B, 3, IMG, IMG), jnp.float32), 'pixel_masks': jnp.ones((B, 1, IMG, IMG), jnp.float32), 'conv_w': nrm(ks[1], (C, 3, PS, PS)), 'class_emb': nrm(ks[2], (C,)), 'la_ln_q_g': jnp.ones((C,)), 'la_ln_q_b': jnp.zeros((C,)), 'la_wq': nrm(ks[3], (C, C)), 'la_ln_kv_g': jnp.ones((C,)), 'la_ln_kv_b': jnp.zeros((C,)), 'la_wkv': nrm(ks[4], (C, 2 * C)), 'la_proj_w': nrm(ks[5], (C, C)), 'la_proj_b': jnp.zeros((C,)), 'ga_ln_q_g': jnp.ones((C,)), 'ga_ln_q_b': jnp.zeros((C,)), 'ga_wq': nrm(ks[6], (C, C)), 'ga_ln_kv_g': jnp.ones((C,)), 'ga_ln_kv_b': jnp.zeros((C,)), 'ga_wkv': nrm(ks[7], (C, 2 * C)), 'ga_proj_w': nrm(ks[8], (C, C)), 'ga_proj_b': jnp.zeros((C,)), 'mod_w': nrm(ks[9], (C, C)), 'mod_b': jnp.zeros((C,))}
    _L0_tok_all = _L0_tok_setup()
    _L0_tok_in = {k: v for k, v in _L0_tok_all.items() if k in ('pixel_masks', 'conv_w', 'class_emb', 'la_ln_q_g', 'la_ln_q_b', 'la_wq', 'la_ln_kv_g', 'la_ln_kv_b', 'la_wkv', 'la_proj_w', 'la_proj_b', 'ga_ln_q_g', 'ga_ln_q_b', 'ga_wq', 'ga_ln_kv_g', 'ga_ln_kv_b', 'ga_wkv', 'ga_proj_w', 'ga_proj_b', 'mod_w', 'mod_b')}
    del _L0_tok_all

    def _L0_attn_setup():
        import jax, jax.numpy as jnp
        import numpy as np
        import math
        H = 16
        N_EMBD = 256
        EPS = 1e-05
        key = jax.random.key(seed)
        ks = jax.random.split(key, 6)
        B, T, C = (2, 512, 256)
        x = jax.random.normal(ks[0], (B, T, C), dtype=jnp.float32)
        s = 0.02
        Wq = jax.random.normal(ks[1], (C, N_EMBD), dtype=jnp.float32) * s
        Wk = jax.random.normal(ks[2], (C, N_EMBD), dtype=jnp.float32) * s
        Wv = jax.random.normal(ks[3], (C, N_EMBD), dtype=jnp.float32) * s
        Wo = jax.random.normal(ks[4], (N_EMBD, C), dtype=jnp.float32) * s
        return {'x': x, 'Wq': Wq, 'bq': jnp.zeros((N_EMBD,), jnp.float32), 'Wk': Wk, 'bk': jnp.zeros((N_EMBD,), jnp.float32), 'Wv': Wv, 'bv': jnp.zeros((N_EMBD,), jnp.float32), 'Wo': Wo, 'bo': jnp.zeros((C,), jnp.float32), 'gamma': jnp.ones((C,), jnp.float32), 'beta': jnp.zeros((C,), jnp.float32)}
    _L0_attn_all = _L0_attn_setup()
    _L0_attn_in = {k: v for k, v in _L0_attn_all.items() if k in ('Wq', 'bq', 'Wk', 'bk', 'Wv', 'bv', 'Wo', 'bo', 'gamma', 'beta')}
    del _L0_attn_all

    def _L0_ffn_setup():
        import jax, jax.numpy as jnp
        import numpy as np
        B, S, H, E, K = (2, 512, 256, 8, 2)
        FF = 4 * H
        EPS = 1e-05
        key = jax.random.key(seed)
        ks = jax.random.split(key, 5)
        rn = lambda k, shape, scale: jax.random.normal(k, shape, dtype=jnp.float32) * scale
        return {'x': rn(ks[0], (B, S, H), 1.0), 'router_W': rn(ks[1], (H, E), H ** (-0.5)), 'router_b': jnp.zeros((E,), jnp.float32), 'ln_g': jnp.ones((E, H), jnp.float32), 'ln_b': jnp.zeros((E, H), jnp.float32), 'W1': rn(ks[2], (E, H, FF), H ** (-0.5)), 'b1': jnp.zeros((E, FF), jnp.float32), 'W2': rn(ks[3], (E, FF, H), FF ** (-0.5)), 'b2': jnp.zeros((E, H), jnp.float32)}
    _L0_ffn_all = _L0_ffn_setup()
    _L0_ffn_in = {k: v for k, v in _L0_ffn_all.items() if k in ('router_W', 'router_b', 'ln_g', 'ln_b', 'W1', 'b1', 'W2', 'b2')}
    del _L0_ffn_all

    def _L1_attn_setup():
        import jax, jax.numpy as jnp
        import numpy as np
        EPS = 1e-06
        HEADS = 8
        DIM_HEAD = 64
        SCALE = 16.0
        DIM = 256
        INNER = HEADS * DIM_HEAD

        def _l2norm(t):
            return t / jnp.clip(jnp.linalg.norm(t, axis=-1, keepdims=True), 1e-12)
        key = jax.random.key(seed)
        k1, k2, k3, k4 = jax.random.split(key, 4)
        b, n = (2, 1024)
        x = jax.random.normal(k1, (b, n, DIM), dtype=jnp.float32)
        Wq = jax.random.normal(k2, (DIM, INNER), dtype=jnp.float32) * 0.02
        Wkv = jax.random.normal(k3, (DIM, 2 * INNER), dtype=jnp.float32) * 0.02
        Wo = jax.random.normal(k4, (INNER, DIM), dtype=jnp.float32) * 0.02
        return {'x': x, 'Wq': Wq, 'Wkv': Wkv, 'Wo': Wo}
    _L1_attn_all = _L1_attn_setup()
    _L1_attn_in = {k: v for k, v in _L1_attn_all.items() if k in ('Wq', 'Wkv', 'Wo')}
    del _L1_attn_all

    def _L1_ffn_setup():
        import jax, jax.numpy as jnp
        import numpy as np
        B, S, D, H, E = (8, 512, 256, 1024, 16)
        key = jax.random.key(seed)
        ks = jax.random.split(key, 4)
        sd = 1.0 / np.sqrt(D).astype(np.float32)
        sh = 1.0 / np.sqrt(H).astype(np.float32)
        return {'x': jax.random.normal(ks[0], (B, S, D), jnp.float32), 'Wg': jax.random.normal(ks[1], (D, E), jnp.float32) * sd, 'bg': jnp.zeros((E,), jnp.float32), 'W1': jax.random.normal(ks[2], (E, D, H), jnp.float32) * sd, 'b1': jnp.zeros((E, H), jnp.float32), 'W2': jax.random.normal(ks[3], (E, H, D), jnp.float32) * sh, 'b2': jnp.zeros((E, D), jnp.float32)}
    _L1_ffn_all = _L1_ffn_setup()
    _L1_ffn_in = {k: v for k, v in _L1_ffn_all.items() if k in ('Wg', 'bg', 'W1', 'b1', 'W2', 'b2')}
    del _L1_ffn_all
    return {'x': x, 'L0_tok_pixel_masks': _L0_tok_in['pixel_masks'], 'L0_tok_conv_w': _L0_tok_in['conv_w'], 'L0_tok_class_emb': _L0_tok_in['class_emb'], 'L0_tok_la_ln_q_g': _L0_tok_in['la_ln_q_g'], 'L0_tok_la_ln_q_b': _L0_tok_in['la_ln_q_b'], 'L0_tok_la_wq': _L0_tok_in['la_wq'], 'L0_tok_la_ln_kv_g': _L0_tok_in['la_ln_kv_g'], 'L0_tok_la_ln_kv_b': _L0_tok_in['la_ln_kv_b'], 'L0_tok_la_wkv': _L0_tok_in['la_wkv'], 'L0_tok_la_proj_w': _L0_tok_in['la_proj_w'], 'L0_tok_la_proj_b': _L0_tok_in['la_proj_b'], 'L0_tok_ga_ln_q_g': _L0_tok_in['ga_ln_q_g'], 'L0_tok_ga_ln_q_b': _L0_tok_in['ga_ln_q_b'], 'L0_tok_ga_wq': _L0_tok_in['ga_wq'], 'L0_tok_ga_ln_kv_g': _L0_tok_in['ga_ln_kv_g'], 'L0_tok_ga_ln_kv_b': _L0_tok_in['ga_ln_kv_b'], 'L0_tok_ga_wkv': _L0_tok_in['ga_wkv'], 'L0_tok_ga_proj_w': _L0_tok_in['ga_proj_w'], 'L0_tok_ga_proj_b': _L0_tok_in['ga_proj_b'], 'L0_tok_mod_w': _L0_tok_in['mod_w'], 'L0_tok_mod_b': _L0_tok_in['mod_b'], 'L0_attn_Wq': _L0_attn_in['Wq'], 'L0_attn_bq': _L0_attn_in['bq'], 'L0_attn_Wk': _L0_attn_in['Wk'], 'L0_attn_bk': _L0_attn_in['bk'], 'L0_attn_Wv': _L0_attn_in['Wv'], 'L0_attn_bv': _L0_attn_in['bv'], 'L0_attn_Wo': _L0_attn_in['Wo'], 'L0_attn_bo': _L0_attn_in['bo'], 'L0_attn_gamma': _L0_attn_in['gamma'], 'L0_attn_beta': _L0_attn_in['beta'], 'L0_ffn_router_W': _L0_ffn_in['router_W'], 'L0_ffn_router_b': _L0_ffn_in['router_b'], 'L0_ffn_ln_g': _L0_ffn_in['ln_g'], 'L0_ffn_ln_b': _L0_ffn_in['ln_b'], 'L0_ffn_W1': _L0_ffn_in['W1'], 'L0_ffn_b1': _L0_ffn_in['b1'], 'L0_ffn_W2': _L0_ffn_in['W2'], 'L0_ffn_b2': _L0_ffn_in['b2'], 'L1_attn_Wq': _L1_attn_in['Wq'], 'L1_attn_Wkv': _L1_attn_in['Wkv'], 'L1_attn_Wo': _L1_attn_in['Wo'], 'L1_ffn_Wg': _L1_ffn_in['Wg'], 'L1_ffn_bg': _L1_ffn_in['bg'], 'L1_ffn_W1': _L1_ffn_in['W1'], 'L1_ffn_b1': _L1_ffn_in['b1'], 'L1_ffn_W2': _L1_ffn_in['W2'], 'L1_ffn_b2': _L1_ffn_in['b2']}

def reference(x, L0_tok_pixel_masks, L0_tok_conv_w, L0_tok_class_emb, L0_tok_la_ln_q_g, L0_tok_la_ln_q_b, L0_tok_la_wq, L0_tok_la_ln_kv_g, L0_tok_la_ln_kv_b, L0_tok_la_wkv, L0_tok_la_proj_w, L0_tok_la_proj_b, L0_tok_ga_ln_q_g, L0_tok_ga_ln_q_b, L0_tok_ga_wq, L0_tok_ga_ln_kv_g, L0_tok_ga_ln_kv_b, L0_tok_ga_wkv, L0_tok_ga_proj_w, L0_tok_ga_proj_b, L0_tok_mod_w, L0_tok_mod_b, L0_attn_Wq, L0_attn_bq, L0_attn_Wk, L0_attn_bk, L0_attn_Wv, L0_attn_bv, L0_attn_Wo, L0_attn_bo, L0_attn_gamma, L0_attn_beta, L0_ffn_router_W, L0_ffn_router_b, L0_ffn_ln_g, L0_ffn_ln_b, L0_ffn_W1, L0_ffn_b1, L0_ffn_W2, L0_ffn_b2, L1_attn_Wq, L1_attn_Wkv, L1_attn_Wo, L1_ffn_Wg, L1_ffn_bg, L1_ffn_W1, L1_ffn_b1, L1_ffn_W2, L1_ffn_b2):
    import jax
    import jax.numpy as jnp

    def _L0_tok_ref(pixel_values, pixel_masks, conv_w, class_emb, la_ln_q_g, la_ln_q_b, la_wq, la_ln_kv_g, la_ln_kv_b, la_wkv, la_proj_w, la_proj_b, ga_ln_q_g, ga_ln_q_b, ga_wq, ga_ln_kv_g, ga_ln_kv_b, ga_wkv, ga_proj_w, ga_proj_b, mod_w, mod_b):
        import jax, jax.numpy as jnp
        import numpy as np
        C = 256
        H8 = 8
        DH = C // H8
        PS = 14
        CS = 3
        IMG = 168
        B = 4

        def _ln(x, g, b):
            mu = jnp.mean(x, axis=-1, keepdims=True)
            xc = x - mu
            var = jnp.mean(xc * xc, axis=-1, keepdims=True)
            return xc * jax.lax.rsqrt(var + 1e-05) * g + b

        def _forward(pixel_values, conv_w, class_emb, la_ln_q_g, la_ln_q_b, la_wq, la_ln_kv_g, la_ln_kv_b, la_wkv, la_proj_w, la_proj_b, ga_ln_q_g, ga_ln_q_b, ga_wq, ga_ln_kv_g, ga_ln_kv_b, ga_wkv, ga_proj_w, ga_proj_b, mod_w, mod_b):
            b = pixel_values.shape[0]
            pe = jax.lax.conv_general_dilated(pixel_values, conv_w, (PS, PS), 'VALID', dimension_numbers=('NCHW', 'OIHW', 'NCHW'))
            HP = pe.shape[2]
            h = HP // CS
            hw, N = (h * h, CS * CS)
            scale = C ** (-0.5)
            grid = pe.reshape(b, C, h, CS, h, CS)
            red = grid.mean(axis=(3, 5)).reshape(b, C, hw).transpose(0, 2, 1)
            win = grid.transpose(0, 2, 4, 3, 5, 1).reshape(b, hw, N, C)
            q = _ln(red, la_ln_q_g, la_ln_q_b) @ la_wq
            q = q.reshape(b, hw, H8, DH).transpose(0, 2, 1, 3)
            kv = _ln(win, la_ln_kv_g, la_ln_kv_b) @ la_wkv
            kv = kv.reshape(b, hw, N, 2, H8, DH).transpose(3, 0, 4, 1, 2, 5)
            k_, v_ = (kv[0], kv[1])
            attn = jax.nn.softmax(jnp.einsum('bhnd,bhnkd->bhnk', q * scale, k_), axis=-1)
            agg = jnp.einsum('bhnk,bhnkd->bhnd', attn, v_)
            agg = agg.transpose(0, 2, 1, 3).reshape(b, hw, C)
            local_out = red + agg @ la_proj_w + la_proj_b
            cls = jnp.broadcast_to(class_emb, (b, 1, C))
            gq = (_ln(cls, ga_ln_q_g, ga_ln_q_b) @ ga_wq).reshape(b, H8, DH)
            gkv = _ln(local_out, ga_ln_kv_g, ga_ln_kv_b) @ ga_wkv
            gkv = gkv.reshape(b, hw, 2, H8, DH).transpose(2, 0, 3, 1, 4)
            gk, gv = (gkv[0], gkv[1])
            gattn = jax.nn.softmax(jnp.einsum('bhd,bhnd->bhn', gq * scale, gk), axis=-1)
            gagg = jnp.einsum('bhn,bhnd->bhd', gattn, gv).reshape(b, 1, C)
            cls_out = cls + gagg @ ga_proj_w + ga_proj_b
            patch_out = local_out @ mod_w + mod_b
            return jnp.concatenate([patch_out, cls_out], axis=1)
        del pixel_masks
        return _forward(pixel_values, conv_w, class_emb, la_ln_q_g, la_ln_q_b, la_wq, la_ln_kv_g, la_ln_kv_b, la_wkv, la_proj_w, la_proj_b, ga_ln_q_g, ga_ln_q_b, ga_wq, ga_ln_kv_g, ga_ln_kv_b, ga_wkv, ga_proj_w, ga_proj_b, mod_w, mod_b)

    def _L0_attn_ref(x, Wq, bq, Wk, bk, Wv, bv, Wo, bo, gamma, beta):
        import jax, jax.numpy as jnp
        import numpy as np
        import math
        H = 16
        N_EMBD = 256
        EPS = 1e-05
        B, T, _ = x.shape
        Dh = N_EMBD // H

        def split_heads(y):
            return y.reshape(B, T, H, Dh).transpose(0, 2, 1, 3)
        q = split_heads(x @ Wq + bq)
        k = split_heads(x @ Wk + bk)
        v = split_heads(x @ Wv + bv)
        att = jnp.einsum('bhtd,bhsd->bhts', q, k) * (1.0 / math.sqrt(Dh))
        causal = jnp.tril(jnp.ones((T, T), dtype=bool))
        att = jnp.where(causal[None, None], att, -jnp.inf)
        att = jax.nn.softmax(att, axis=-1)
        o = jnp.einsum('bhts,bhsd->bhtd', att, v)
        o = o.transpose(0, 2, 1, 3).reshape(B, T, N_EMBD)
        y = o @ Wo + bo
        mu = jnp.mean(y, axis=-1, keepdims=True)
        var = jnp.var(y, axis=-1, keepdims=True)
        return (y - mu) * jax.lax.rsqrt(var + EPS) * gamma + beta

    def _L0_ffn_ref(x, router_W, router_b, ln_g, ln_b, W1, b1, W2, b2):
        import jax, jax.numpy as jnp
        import numpy as np
        B, S, H, E, K = (2, 512, 256, 8, 2)
        FF = 4 * H
        EPS = 1e-05
        logits = x @ router_W + router_b
        w, idx = jax.lax.top_k(logits, K)
        w = jax.nn.softmax(w, axis=-1)
        gates = jnp.einsum('bske,bsk->bse', jax.nn.one_hot(idx, E, dtype=x.dtype), w)
        mu = jnp.mean(x, axis=-1, keepdims=True)
        var = jnp.mean(jnp.square(x - mu), axis=-1, keepdims=True)
        xhat = (x - mu) * jax.lax.rsqrt(var + EPS)
        h = xhat[:, :, None, :] * ln_g + ln_b
        a = jax.nn.gelu(jnp.einsum('bseh,ehf->bsef', h, W1) + b1, approximate=False)
        y = jnp.einsum('bsef,efh->bseh', a, W2) + b2
        y = y + x[:, :, None, :]
        out = jnp.einsum('bseh,bse->bsh', y, gates)
        return out

    def _L1_attn_ref(x, Wq, Wkv, Wo):
        import jax, jax.numpy as jnp
        import numpy as np
        EPS = 1e-06
        HEADS = 8
        DIM_HEAD = 64
        SCALE = 16.0
        DIM = 256
        INNER = HEADS * DIM_HEAD

        def _l2norm(t):
            return t / jnp.clip(jnp.linalg.norm(t, axis=-1, keepdims=True), 1e-12)
        b, n, _ = x.shape
        q = (x @ Wq).reshape(b, n, HEADS, DIM_HEAD).transpose(0, 2, 1, 3)
        kv = x @ Wkv
        k = kv[..., :INNER].reshape(b, n, HEADS, DIM_HEAD).transpose(0, 2, 1, 3)
        v = kv[..., INNER:].reshape(b, n, HEADS, DIM_HEAD).transpose(0, 2, 1, 3)
        q = _l2norm(q)
        k = _l2norm(k)
        logits = jnp.einsum('bhid,bhjd->bhij', q, k) * SCALE - SCALE
        p = jnp.exp(logits)
        row_sums = jnp.clip(p.sum(axis=-1, keepdims=True), EPS)
        out = jnp.einsum('bhij,bhjd->bhid', p, v) / row_sums
        out = out.transpose(0, 2, 1, 3).reshape(b, n, INNER)
        return out @ Wo

    def _L1_ffn_ref(x, Wg, bg, W1, b1, W2, b2):
        import jax, jax.numpy as jnp
        import numpy as np
        B, S, D, H, E = (8, 512, 256, 1024, 16)
        d = x.shape[-1]
        xf = x.reshape(-1, d)
        n_tok = xf.shape[0]
        n_exp = Wg.shape[1]
        cap = -(-n_tok // n_exp)
        score = jax.nn.softmax(xf @ Wg + bg, axis=-1)
        gate = jnp.max(score, axis=-1)
        idx = jnp.argmax(score, axis=-1)
        onehot = jax.nn.one_hot(idx, n_exp, dtype=jnp.int32)
        pos = jnp.sum((jnp.cumsum(onehot, axis=0) - 1) * onehot, axis=-1)
        keep = pos < cap
        safe_pos = jnp.where(keep, pos, cap - 1)
        buf = jnp.zeros((n_exp, cap, d), x.dtype).at[idx, safe_pos].add(jnp.where(keep[:, None], xf, 0.0))
        h = jax.nn.relu(jnp.einsum('ecd,edh->ech', buf, W1) + b1[:, None, :])
        y = jnp.einsum('ech,ehd->ecd', h, W2) + b2[:, None, :]
        out = y[idx, safe_pos] * gate[:, None]
        out = jnp.where(keep[:, None], out, 0.0)
        return out.reshape(x.shape)
    h = _L0_tok_ref(x, L0_tok_pixel_masks, L0_tok_conv_w, L0_tok_class_emb, L0_tok_la_ln_q_g, L0_tok_la_ln_q_b, L0_tok_la_wq, L0_tok_la_ln_kv_g, L0_tok_la_ln_kv_b, L0_tok_la_wkv, L0_tok_la_proj_w, L0_tok_la_proj_b, L0_tok_ga_ln_q_g, L0_tok_ga_ln_q_b, L0_tok_ga_wq, L0_tok_ga_ln_kv_g, L0_tok_ga_ln_kv_b, L0_tok_ga_wkv, L0_tok_ga_proj_w, L0_tok_ga_proj_b, L0_tok_mod_w, L0_tok_mod_b)
    h = _layernorm(h + _L0_attn_ref(h, L0_attn_Wq, L0_attn_bq, L0_attn_Wk, L0_attn_bk, L0_attn_Wv, L0_attn_bv, L0_attn_Wo, L0_attn_bo, L0_attn_gamma, L0_attn_beta), axis=-1)
    h = _layernorm(h + _L0_ffn_ref(h, L0_ffn_router_W, L0_ffn_router_b, L0_ffn_ln_g, L0_ffn_ln_b, L0_ffn_W1, L0_ffn_b1, L0_ffn_W2, L0_ffn_b2), axis=-1)
    h = _layernorm(h + _L1_attn_ref(h, L1_attn_Wq, L1_attn_Wkv, L1_attn_Wo), axis=-1)
    h = _layernorm(h + _L1_ffn_ref(h, L1_ffn_Wg, L1_ffn_bg, L1_ffn_W1, L1_ffn_b1, L1_ffn_W2, L1_ffn_b2), axis=-1)
    return h

_drawn_inputs = setup_inputs


def setup_inputs(seed=0):
    import zlib

    import numpy as np

    out = dict(_drawn_inputs(seed))
    spreads = {'L0_tok_pixel_masks': (1.0, 0.2),
     'L0_tok_la_ln_q_g': (1.0, 0.6),
     'L0_tok_la_ln_q_b': (0.0, 0.8),
     'L0_tok_la_ln_kv_g': (1.0, 0.6),
     'L0_tok_la_ln_kv_b': (0.0, 0.1),
     'L0_tok_la_proj_b': (0.0, 0.1),
     'L0_tok_ga_ln_q_g': (1.0, 0.6),
     'L0_tok_ga_ln_q_b': (0.0, 2.0),
     'L0_tok_ga_ln_kv_g': (1.0, 0.2),
     'L0_tok_ga_ln_kv_b': (0.0, 0.1),
     'L0_tok_ga_proj_b': (0.0, 0.1),
     'L0_tok_mod_b': (0.0, 0.1),
     'L0_attn_bq': (0.0, 2.0),
     'L0_attn_bk': (0.0, 2.0),
     'L0_attn_bv': (0.0, 0.1),
     'L0_attn_bo': (0.0, 0.1),
     'L0_attn_gamma': (1.0, 0.2),
     'L0_attn_beta': (0.0, 0.1),
     'L0_ffn_router_b': (0.0, 0.1),
     'L0_ffn_ln_g': (1.0, 0.2),
     'L0_ffn_ln_b': (0.0, 0.34),
     'L0_ffn_b1': (0.0, 0.338),
     'L0_ffn_b2': (0.0, 0.1),
     'L1_ffn_bg': (0.0, 0.462),
     'L1_ffn_b1': (0.0, 0.8),
     'L1_ffn_b2': (0.0, 0.8)}
    factors = {'L0_tok_la_wq': 8.0, 'L0_tok_ga_wq': 20.453, 'L0_attn_Wq': 43.917, 'L0_attn_Wk': 22.221}
    for name, (base, spread) in spreads.items():
        noise = np.random.default_rng([zlib.crc32(name.encode()), seed]).standard_normal(out[name].shape)
        drawn = base * np.exp(spread * noise) if base else spread * noise
        out[name] = jnp.asarray(drawn.astype(out[name].dtype))
    for name, factor in factors.items():
        out[name] = (out[name] * factor).astype(out[name].dtype)
    return out
```

```python
from contextlib import ExitStack

import concourse.bass as bass
from concourse import mybir

ALU = mybir.AluOpType
ACT = mybir.ActivationFunctionType
AX = mybir.AxisListType
F32 = mybir.dt.float32
I32 = mybir.dt.int32
U32 = mybir.dt.uint32
P = 128


def reuse(w, p, per):
    n = w * per + p + CREDIT
    return n if p == 0 else n - 2 if p == 1 else n - 1


CREDIT = 3


class Steps:

    def __init__(self, eng, sem):
        self.eng, self.sem, self.n = eng, sem, 0

    def __call__(self, ins):
        ins.then_inc(self.sem, 1)
        self.n = self.n + 1
        self.eng.wait_ge(self.sem, self.n)

    def loop(self, base, trip, per):
        self.n = base + trip * per


def build_program(nc, x, conv_w, class_emb, tok_vecs, la_wq, la_wkv, la_proj_w, la_proj_b, ga_wq, ga_wkv,
                  ga_proj_w, ga_proj_b, mod_w, mod_b, a0_w, a0_b, a0_wo, a0_bo, a0_gamma, a0_beta,
                  f0_router_w, f0_router_b, f0_ln_g, f0_ln_b, f0_w1, f0_b1, f0_w2, f0_b2,
                  a1_wq, a1_wkv, a1_wo, f1_wg, f1_bg, f1_w1, f1_b1, f1_w2, f1_b2, out):
    B, CH, IH, IW = x.shape
    C, _, PS, _ = conv_w.shape
    assert B == P and C == 2 * P
    KC = C // P
    CS = 3
    G = IH // PS // CS
    NW = G * G
    NP = CS * CS
    T = NW + 1
    ROWS = G * CS * PS
    KP = CH * PS * PS
    NCH = -(-KP // P)
    KT = KP - (NCH - 1) * P
    H8 = 8
    DH = C // H8
    SCALE = float(C) ** -0.5
    LN_EPS = 1e-5

    H0 = 16
    D0 = C // H0
    E0, _, F0 = f0_w1.shape
    FC = F0 // P
    NT0 = (2 * T * P - E0) // P + E0
    H1 = 8
    INNER = a1_wq.shape[1]
    D1 = INNER // H1
    KI = INNER // P
    E1 = f1_w1.shape[0]
    CAP = -(-T * P // E1)
    SLOT = 64
    NPAIR = E1 // 2
    assert CAP < SLOT and F0 == f1_w1.shape[2]

    xs0 = nc.dram_tensor("xs0", [NT0 * P, C], F32, kind="Internal").ap()
    ys0 = nc.dram_tensor("ys0", [NT0 * P, C], F32, kind="Internal").ap()
    xs1 = nc.dram_tensor("xs1", [E1 * SLOT + T * P, C], F32, kind="Internal").ap()
    ys1 = nc.dram_tensor("ys1", [E1 * SLOT, C], F32, kind="Internal").ap()

    ctx = ExitStack()
    with ctx:
        def sb(name, shape, dt=F32):
            return ctx.enter_context(nc.sbuf_tensor(name, shape, dt))

        def sem(name):
            return ctx.enter_context(nc.semaphore(name))

        IMG = CH * ROWS * IW
        AR = 45400
        arena = sb("arena", [P, AR])
        top = {}

        def at(off, size, pat=None, /, **kw):
            a = arena[:, off:off + size]
            return a.rearrange(pat, **kw) if pat else a

        img = at(0, IMG, "p (c i j) -> p c i j", c=CH, i=ROWS)
        o = IMG
        packed = at(o, 2 * KP, "p (s k) -> p s k", s=2); o += 2 * KP
        patchT = at(o, 2 * NCH * P, "p (s k n) -> p s k n", s=2, k=NCH); o += 2 * NCH * P
        pe_raw = at(o, NP * C, "p (n c) -> p n c", n=NP); o += NP * C
        xhat = at(o, NP * C, "p (n c) -> p n c", n=NP); o += NP * C
        kvw = at(o, NP * 2 * C, "p (n c) -> p n c", n=NP)
        convw_raw = at(o, KC * KP, "p (h k) -> p h k", h=KC)
        vec_raw = at(o + KC * KP, C)
        b1_raw = at(o + KC * KP + C, F0); o += NP * 2 * C
        kvnT = at(o, 2 * KC * P, "p (s k n) -> p s k n", s=2, k=KC); o += 2 * KC * P
        redT = at(o, KC * P, "p (k n) -> p k n", k=KC); o += KC * P
        q_sb = at(o, C); o += C
        agg = at(o, NW * C, "p (n c) -> p n c", n=NW); o += NW * C
        redb = at(o, NW * C, "p (n c) -> p n c", n=NW); o += NW * C
        red = at(o, C); o += C
        redhat = at(o, C); o += C
        convT = at(o, NCH * C, "p (k c) -> p k c", k=NCH); o += NCH * C

        def wt(n):
            nonlocal o
            a = at(o, KC * n, "p (k n) -> p k n", k=KC)
            o += KC * n
            return a
        wq_s, wkv_s, proj_s, gwq_s, gwkv_s, gproj_s, mod_s = wt(C), wt(2 * C), wt(C), wt(C), wt(2 * C), wt(C), wt(C)
        assert o <= AR, o

        o = 0
        a0w_s = at(0, KC * 3 * C, "p (k n) -> p k n", k=KC); o += KC * 3 * C
        a0wo_s = at(o, KC * C, "p (k n) -> p k n", k=KC); o += KC * C
        qkv0 = at(o, T * 3 * C, "p (t n) -> p t n", t=T); o += T * 3 * C
        prod0 = at(o, T * C); o += T * C
        local = at(o, NW * C, "p (n c) -> p n c", n=NW); o += NW * C
        lhat = at(o, NW * C, "p (n c) -> p n c", n=NW); o += NW * C
        gkv = at(o, NW * 2 * C, "p (n c) -> p n c", n=NW); o += NW * 2 * C
        gprod = at(o, NW * C, "p (n c) -> p n c", n=NW); o += NW * C
        gagg = at(o, C); o += C
        attn0 = at(o, T * C, "p (t c) -> p t c", t=T); o += T * C
        yln = at(o, T * C, "p (t c) -> p t c", t=T); o += T * C
        assert o <= 16384, o
        w1_1 = [at(i * 4 * KC * F0, 2 * KC * F0, "p (e k f) -> p e k f", e=2, k=KC) for i in range(2)]
        w2_1 = [at(i * 4 * KC * F0 + 2 * KC * F0, 2 * FC * C, "p (e f c) -> p e f c", e=2, f=FC) for i in range(2)]
        w1_0 = [at(16384 + i * 2 * KC * F0, KC * F0, "p (k f) -> p k f", k=KC) for i in range(2)]
        w2_0 = [at(16384 + i * 2 * KC * F0 + KC * F0, FC * C, "p (f c) -> p f c", f=FC) for i in range(2)]
        o = 24576
        hA = at(o, T * C, "p (t c) -> p t c", t=T); o += T * C
        hB = at(o, T * C, "p (t c) -> p t c", t=T); o += T * C
        hX = at(o, T * C, "p (t c) -> p t c", t=T); o += T * C
        XT = at(o, KC * T * P, "p (k n) -> p k n", k=KC); o += KC * T * P
        XT2 = at(o, KC * T * P, "p (k n) -> p k n", k=KC); o += KC * T * P
        OT = at(o - 2 * KC * T * P, KI * T * P, "p (k n) -> p k n", k=KI)
        assert KI == 2 * KC
        a1w_s = at(o, KC * 3 * INNER, "p (k n) -> p k n", k=KC); o += KC * 3 * INNER
        a1wo_s = at(o, KI * C, "p (k n) -> p k n", k=KI); o += KI * C
        assert o <= IMG + 2 * KP + 2 * NCH * P + 2 * NP * C + NP * 2 * C, o
        work = o
        qkv1 = at(o, T * 3 * INNER, "p (t n) -> p t n", t=T); o += T * 3 * INNER
        prod1 = at(16384, 2 * T * INNER)
        assert o <= AR, o
        o = work
        xrow = at(o, 2 * C, "p (s c) -> p s c", s=2); o += 2 * C
        xTs = at(o, 2 * KC * P, "p (s k n) -> p s k n", s=2, k=KC); o += 2 * KC * P
        h_sb = at(o, F0); o += F0
        hb = at(o, F0); o += F0
        hTs = at(o, FC * P, "p (f n) -> p f n", f=FC); o += FC * P
        y_sb = at(o, 2 * C, "p (s c) -> p s c", s=2); o += 2 * C
        b2_r = at(o, 2 * C, "p (s c) -> p s c", s=2); o += 2 * C
        yg = at(o, 2 * T * C, "p (k t c) -> p k t c", k=2, t=T); o += 2 * T * C
        assert o <= AR, o

        rows_sb = sb("rows_sb", [P, 3 * C + 3 * C + 3 * C + C + E0 + E1])
        o = 0

        def row(n):
            nonlocal o
            o += n
            return rows_sb[:, o - n:o]
        projb_r, gprojb_r, modb_r, bqkv_r, bo_r, gamma_r, beta_r, cls_r, rb_r, bg_r = (
            row(C), row(C), row(C), row(3 * C), row(C), row(C), row(C), row(C), row(E0), row(E1))
        ident = sb("ident", [P, P])
        ones_sb = sb("ones_sb", [P, P])
        upper = sb("upper", [P, P])
        vecT = sb("vecT", [P, KC, 24])
        b1T = sb("b1T", [P, FC, 24])
        eps_sb = sb("eps_sb", [P, 1])
        gq_sb = sb("gq_sb", [P, C])
        stats = sb("stats", [P, NP, 6])
        mv = sb("mv", [P, NP, 2])
        sd = sb("sd", [P, NP])
        rs = sb("rs", [P, NP])
        sc = sb("sc", [P, NP, H8])
        ex = sb("ex", [P, NP, H8])
        hx = sb("hx", [P, 4, H8])

        zeros = sb("zeros", [P, C])
        S0 = sb("S0", [P, T, H0, T])
        S1 = sb("S1", [P, T, H1, T])
        hs = sb("hs", [P, 3, T * H0])
        ssq = sb("ssq", [P, T, 2 * H1])
        rnorm = sb("rnorm", [P, T, 2 * H1])
        neg16 = sb("neg16", [P, 1])
        rw_s = sb("rw_s", [P, KC, E0])
        wg_s = sb("wg_s", [P, KC, E1])
        iota_e = sb("iota_e", [P, E1])
        iota_t = sb("iota_t", [1, NT0 + 1])
        trash = sb("trash", [P, T])
        lg = sb("lg", [P, T, E1])
        lg2 = sb("lg2", [P, T, E1])
        best = sb("best", [P, T, 8])
        besti = sb("besti", [P, T, 8], U32)
        bestf = sb("bestf", [P, T, 2])
        oh = sb("oh", [P, 2, T, E1])
        msum = sb("msum", [P, T, E1])
        mcum = sb("mcum", [P, T, E1])
        rk = sb("rk", [P, T, E1])
        cnt = sb("cnt", [P, E0])
        ntile = sb("ntile", [P, E0])
        incl = sb("incl", [P, E0])
        basee = sb("basee", [P, E0])
        slotf = sb("slotf", [P, 2, T])
        slotu = sb("slotu", [P, 2, T], U32)
        gslotu = sb("gslotu", [P, T], U32)
        cmp_t = sb("cmp_t", [1, NT0, E0])
        eidf = sb("eidf", [1, NT0])
        eid = sb("eid", [1, NT0], I32)
        gate = sb("gate", [P, 4, T])
        tab = sb("tab", [P, E0, 2 * KC + FC])
        cur = sb("cur", [P, 2, 2 * KC + FC])

        bank = [ctx.enter_context(nc.psum_tensor(f"bank{i}", [P, 512], F32)) for i in range(8)]
        b_top, b_tail, b_conv, b_kvT, b_kv, b_q = bank[0], bank[1], bank[2:4], bank[4], bank[5:7], bank[7]
        b_turn, b_mm = bank[0:2], bank[2:6]
        b_x, b_h, b_hT, b_y = bank[0], bank[1:3], bank[3:5], bank[5]

        convw_loaded = sem("convw_loaded")
        img_rows = [sem(f"img_rows{i}") for i in range(CS)]
        vecs_loaded = sem("vecs_loaded")
        tokw_loaded = sem("tokw_loaded")
        rows_loaded = sem("rows_loaded")
        consts_made = sem("consts_made")
        setup_turned = sem("setup_turned")
        setup_copied = sem("setup_copied")
        patch_packed = sem("patch_packed")
        patch_turned = sem("patch_turned")
        patchT_ready = sem("patchT_ready")
        conv_ready = sem("conv_ready")
        conv_copied = sem("conv_copied")
        var_ready = sem("var_ready")
        std_ready = sem("std_ready")
        xhat_ready = sem("xhat_ready")
        kvn_turned = sem("kvn_turned")
        kvnT_ready = sem("kvnT_ready")
        kv_ready = sem("kv_ready")
        kv_copied = sem("kv_copied")
        redhat_ready = sem("redhat_ready")
        red_turned = sem("red_turned")
        redT_ready = sem("redT_ready")
        q_ready = sem("q_ready")
        q_copied = sem("q_copied")
        scores_shifted = sem("scores_shifted")
        exps_ready = sem("exps_ready")
        agg_ready = sem("agg_ready")
        dve_step = sem("dve_step")
        act_step = sem("act_step")
        pool_step = sem("pool_step")
        turned = sem("turned")
        turned_copied = sem("turned_copied")
        product_ready = sem("product_ready")
        product_read = sem("product_read")
        rows_ready = sem("rows_ready")
        out_stored = sem("out_stored")
        a0w_loaded = sem("a0w_loaded")
        a1w_loaded = sem("a1w_loaded")
        gatew_loaded = sem("gatew_loaded")
        scratch_zeroed = sem("scratch_zeroed")
        logits_shifted = sem("logits_shifted")
        attn_exps = sem("attn_exps")
        squares_ready = sem("squares_ready")
        norms_ready = sem("norms_ready")
        table_ready = sem("table_ready")
        route_ready = sem("route_ready")
        gathered = sem("gathered")

        class Ffn:

            def __init__(self, name):
                def s(what):
                    return sem(f"{name}_{what}")
                self.scattered = s("scattered")
                self.x_loaded = [s(f"x_loaded{i}") for i in range(2)]
                self.w1_loaded = [s(f"w1_loaded{i}") for i in range(2)]
                self.w2_loaded = [s(f"w2_loaded{i}") for i in range(2)]
                self.x_turned = s("x_turned")
                self.xT_ready = s("xT_ready")
                self.up_ready = s("up_ready")
                self.h_copied = s("h_copied")
                self.h_turned = s("h_turned")
                self.biased = s("biased")
                self.active = s("active")
                self.down_ready = s("down_ready")
                self.y_ready = s("y_ready")
                self.cur_ready = s("cur_ready")
                self.y_stored = s("y_stored")
                self.y_free = s("y_free")
        ff0, ff1 = Ffn("ff0"), Ffn("ff1")

        block = ctx.enter_context(nc.Block())

        N_VEC, N_TOKW, N_ROWS = 12, 7, 12
        N_CONST = 10
        R0 = 2 * NW + 1
        N_OUT = R0 + 2 + 6 * T
        AHEAD = 2

        def tiles(eng, count, body, parts=2):
            with eng.Fori(0, count // 2) as i:
                for s in range(2):
                    body(i * 2 + s, s, i)
            if count % 2:
                body(count - 1, 0, count // 2)

        @block.sync
        def _(sp):
            sp.dma_start(convw_raw, conv_w.rearrange("(h p) c i j -> p h (c i j)", p=P)).then_inc(convw_loaded, 16)

            def image_rows(wr, pr):
                r = (wr * CS + pr) * PS
                if wr:
                    sp.wait_ge(img_rows[pr], 16 * wr)
                sp.dma_start(img[:, :, r:r + PS, :], x[:, :, r:r + PS, :]).then_inc(img_rows[pr], 16)
            image_rows(0, 0)
            for i, v in enumerate(tok_vecs):
                sp.dma_start(vec_raw[i:i + 1, :], v.rearrange("(a c) -> a c", a=1)).then_inc(vecs_loaded, 16)
            sp.dma_start(vec_raw[8:16, :], f0_ln_g).then_inc(vecs_loaded, 16)
            sp.dma_start(vec_raw[16:24, :], f0_ln_b).then_inc(vecs_loaded, 16)
            sp.dma_start(b1_raw[0:E0, :], f0_b1).then_inc(vecs_loaded, 16)
            sp.dma_start(b1_raw[E0:E0 + E1, :], f1_b1).then_inc(vecs_loaded, 16)
            image_rows(0, 1)
            for dst, src in ((wq_s, la_wq), (wkv_s, la_wkv), (gwq_s, ga_wq), (proj_s, la_proj_w),
                             (gwkv_s, ga_wkv), (gproj_s, ga_proj_w), (mod_s, mod_w)):
                sp.dma_start(dst, src.rearrange("(k p) n -> p k n", p=P)).then_inc(tokw_loaded, 16)
            image_rows(0, 2)
            for dst, src in ((projb_r, la_proj_b), (gprojb_r, ga_proj_b), (modb_r, mod_b),
                             (bqkv_r[:, 0:C], a0_b[0]), (bqkv_r[:, C:2 * C], a0_b[1]), (bqkv_r[:, 2 * C:3 * C], a0_b[2]),
                             (bo_r, a0_bo), (gamma_r, a0_gamma), (beta_r, a0_beta), (cls_r, class_emb),
                             (rb_r, f0_router_b), (bg_r, f1_bg)):
                sp.dma_start(dst, src.partition_broadcast(P)).then_inc(rows_loaded, 16)
            for pr in range(CS):
                image_rows(1, pr)
            sp.dma_start(rw_s[:, :, :], f0_router_w.rearrange("(k p) e -> p k e", p=P)).then_inc(gatew_loaded, 16)
            sp.dma_start(wg_s[:, :, :], f1_wg.rearrange("(k p) e -> p k e", p=P)).then_inc(gatew_loaded, 16)
            sp.wait_ge(consts_made, N_CONST)
            for dst in (xs0, xs1):
                n = dst.shape[0] // P
                sp.dma_start(dst.rearrange("(n p) c -> p n c", p=P), zeros[:, :].unsqueeze(1).to_broadcast([P, n, C]))\
                    .then_inc(scratch_zeroed, 16)
            sp.wait_ge(patch_packed, NW * NP)
            for i in range(3):
                sp.dma_start(a0w_s[:, :, i * C:(i + 1) * C], a0_w[i].rearrange("(k p) n -> p k n", p=P)).then_inc(a0w_loaded, 16)
            sp.dma_start(a0wo_s, a0_wo.rearrange("(k p) n -> p k n", p=P)).then_inc(a0w_loaded, 16)
            sp.wait_ge(agg_ready, NW + 1)
            sp.dma_start(a1w_s[:, :, 0:INNER], a1_wq.rearrange("(k p) n -> p k n", p=P)).then_inc(a1w_loaded, 16)
            sp.dma_start(a1w_s[:, :, INNER:3 * INNER], a1_wkv.rearrange("(k p) n -> p k n", p=P)).then_inc(a1w_loaded, 16)
            sp.dma_start(a1wo_s, a1_wo.rearrange("(k p) n -> p k n", p=P)).then_inc(a1w_loaded, 16)

            def load_tile(ff, j, s, i, xs, w1, w1_src, w2, w2_src, b2_src):
                sp.wait_ge(ff.x_turned, j + 1)
                sp.dma_start(xrow[:, s, :], xs[bass.ds(j * P, P), :]).then_inc(ff.x_loaded[s], 16)
                sp.wait_ge(ff.up_ready, j + 1)
                sp.dma_start(w1, w1_src).then_inc(ff.w1_loaded[s], 16)
                sp.wait_ge(ff.down_ready, j + 1)
                sp.dma_start(w2, w2_src).then_inc(ff.w2_loaded[s], 16)
                sp.wait_ge(ff.y_ready, j + 1)
                for dst, src in b2_src:
                    sp.dma_start(dst, src).then_inc(ff.w2_loaded[s], 16)

            sp.wait_ge(route_ready, 1)
            sp.wait_ge(ff0.scattered, 16 * 2 * T)
            with sp.register("tile_expert") as expert:
                def load0(j, s, i):
                    sp.reg_load(expert, eid[0:1, bass.ds(j, 1)])
                    e = sp.snap(expert, min_val=0, max_val=E0 - 1)
                    load_tile(ff0, j, s, i, xs0, w1_0[s], f0_w1[bass.ds(e, 1)].rearrange("e (k p) f -> p (e k) f", p=P),
                              w2_0[s], f0_w2[bass.ds(e, 1)].rearrange("e (f p) c -> p (e f) c", p=P),
                              [(b2_r[:, s, :], f0_b2[bass.ds(e, 1), :].rearrange("e c -> (e c)").partition_broadcast(P))])
                tiles(sp, NT0, load0)
            sp.wait_ge(ff1.scattered, 16 * T)

            def load1(j, s, i):
                load_tile(ff1, j, s, i, xs1,
                          w1_1[s], f1_w1[bass.ds(j * 2, 2)].rearrange("e (k p) f -> p e k f", p=P),
                          w2_1[s], f1_w2[bass.ds(j * 2, 2)].rearrange("e (f p) c -> p e f c", p=P),
                          [(b2_r[e * SLOT:(e + 1) * SLOT, s, :],
                            f1_b2[bass.ds(j * 2 + e, 1), :].rearrange("e c -> (e c)").partition_broadcast(SLOT)) for e in range(2)])
            tiles(sp, NPAIR, load1)
            sp.wait_ge(rows_ready, N_OUT)
            sp.dma_start(out, hA).then_inc(out_stored, 16)
            sp.wait_ge(out_stored, 16)
        @block.gpsimd
        def _(pool):
            step = Steps(pool, pool_step)
            step(pool.memset(ident[:, :], 0.0))
            pool.affine_select(out=ident[:, :], in_=ident[:, :], compare_op=ALU.not_equal, fill=1.0, base=0,
                               pattern=[[-1, P]], channel_multiplier=1).then_inc(consts_made, 1)
            step(pool.memset(upper[:, :], 1.0))
            pool.affine_select(out=upper[:, :], in_=upper[:, :], compare_op=ALU.is_gt, fill=0.0, base=0,
                               pattern=[[1, P]], channel_multiplier=-1).then_inc(consts_made, 1)
            pool.memset(ones_sb[:, :], 1.0).then_inc(consts_made, 1)
            pool.memset(eps_sb[:, :], LN_EPS).then_inc(consts_made, 1)
            pool.memset(neg16[:, :], -16.0).then_inc(consts_made, 1)
            pool.memset(zeros[:, :], 0.0).then_inc(consts_made, 1)
            pool.memset(S0[:, :, :, :], -1e30).then_inc(consts_made, 1)
            pool.iota(iota_e[:, :], [[1, E1]], base=0, channel_multiplier=0,
                      allow_small_or_imprecise_dtypes=True).then_inc(consts_made, 1)
            pool.iota(iota_t[:, :], [[1, NT0 + 1]], base=0, channel_multiplier=0,
                      allow_small_or_imprecise_dtypes=True).then_inc(consts_made, 1)
            pool.iota(trash[:, :], [[P, T]], base=E1 * SLOT, channel_multiplier=1,
                      allow_small_or_imprecise_dtypes=True).then_inc(consts_made, 1)
            with pool.Fori(0, G) as wr:
                with pool.Fori(0, G) as wc:
                    w = wr * G + wc
                    for p in range(NP):
                        pr, pc = divmod(p, CS)
                        pool.wait_ge(img_rows[pr], wr * 16 + 16)
                        pool.wait_ge(patch_turned, reuse(w, p, NP))
                        src = img[:, :, bass.ds(wr * (CS * PS) + pr * PS, PS), bass.ds(wc * (CS * PS) + pc * PS, PS)]
                        pool.tensor_copy(packed[:, p % 2, :].rearrange("p (c i j) -> p c i j", c=CH, i=PS), src)\
                            .then_inc(patch_packed, 1)

            def store_tile(ff, ys):
                def store(j, s, i):
                    pool.wait_ge(ff.y_ready, j + 1 + AHEAD)
                    pool.dma_start(ys[bass.ds(j * P, P), :], y_sb[:, s, :]).then_inc(ff.y_stored, 16)
                    pool.wait_ge(ff.y_stored, j * 16 + 16)
                    pool.sem_inc(ff.y_free, 1)
                return store

            for q in (ff0.y_free, ff1.y_free):
                pool.sem_inc(q, AHEAD)
            pool.wait_ge(route_ready, 1)
            pool.wait_ge(scratch_zeroed, 32)
            for k in range(2):
                for t in range(T):
                    pool.indirect_dma_start(xs0, bass.IndirectOffsetOnAxis(ap=slotu[:, k, t:t + 1], axis=0),
                                            hX[:, t, :], None).then_inc(ff0.scattered, 16)
            tiles(pool, NT0, store_tile(ff0, ys0))
            for k in range(2):
                for t in range(T):
                    pool.indirect_dma_start(yg[:, k, t, :], None, ys0,
                                            bass.IndirectOffsetOnAxis(ap=slotu[:, k, t:t + 1], axis=0)).then_inc(gathered, 16)
            pool.wait_ge(route_ready, 2)
            for t in range(T):
                pool.indirect_dma_start(xs1, bass.IndirectOffsetOnAxis(ap=slotu[:, 0, t:t + 1], axis=0),
                                        hB[:, t, :], None).then_inc(ff1.scattered, 16)
            tiles(pool, NPAIR, store_tile(ff1, ys1))
            for t in range(T):
                pool.indirect_dma_start(yg[:, 0, t, :], None, ys1,
                                        bass.IndirectOffsetOnAxis(ap=gslotu[:, t:t + 1], axis=0)).then_inc(gathered, 16)

        @block.tensor
        def _(pe):
            pe.wait_ge(consts_made, N_CONST)
            pe.wait_ge(convw_loaded, 16)
            for k in range(NCH):
                kn = P if k < NCH - 1 else KT
                if k >= 2:
                    pe.wait_ge(setup_copied, k - 1)
                for h in range(KC):
                    ins = pe.transpose(bank[k % 2][0:kn, h * P:(h + 1) * P], convw_raw[:, h, k * P:k * P + kn], ident[:, :])
                ins.then_inc(setup_turned, 1)
            pe.wait_ge(vecs_loaded, 16 * N_VEC)
            for k in range(KC):
                ins = pe.transpose(bank[4][:, k * 24:(k + 1) * 24], vec_raw[0:24, k * P:(k + 1) * P], ident[0:24, 0:24])
            ins.then_inc(setup_turned, 1)
            for f in range(FC):
                ins = pe.transpose(bank[5][:, f * 24:(f + 1) * 24], b1_raw[0:24, f * P:(f + 1) * P], ident[0:24, 0:24])
            ins.then_inc(setup_turned, 1)
            pe.wait_ge(redhat_ready, 1)
            for k in range(KC):
                ins = pe.transpose(b_q[:, k * P:(k + 1) * P], redhat[:, k * P:(k + 1) * P], ident[:, :])
            ins.then_inc(red_turned, 1)
            pe.wait_ge(redT_ready, 1)
            pe.wait_ge(tokw_loaded, 16 * N_TOKW)
            for k in range(KC):
                ins = pe.matmul(b_q[:, C:2 * C], redT[:, k, :], gwq_s[:, k, :], start=(k == 0), stop=(k == KC - 1))
            ins.then_inc(q_ready, 1)
            pe.wait_ge(setup_copied, NCH + 2)
            for s in (patch_turned, conv_ready, kv_ready):
                pe.sem_inc(s, CREDIT)

            def turn_patch(w, p):
                g = w * NP + p
                pe.wait_ge(patch_packed, g + 1)
                pe.wait_ge(patchT_ready, g + 1)
                for k in range(NCH - 1):
                    pe.transpose(b_top[:, k * P:(k + 1) * P], packed[:, p % 2, k * P:(k + 1) * P], ident[:, :])
                pe.transpose(b_tail[0:KT, 0:P], packed[:, p % 2, (NCH - 1) * P:KP], ident[:, :]).then_inc(patch_turned, 1)

            def project_patch(w, p):
                pe.wait_ge(patchT_ready, w * NP + p + 2)
                pe.wait_ge(conv_copied, reuse(w, p, NP))
                for k in range(NCH):
                    kn = P if k < NCH - 1 else KT
                    ins = pe.matmul(b_conv[p % 2][:, 0:C], patchT[0:kn, p % 2, k, :], convT[0:kn, k, :],
                                    start=(k == 0), stop=(k == NCH - 1))
                ins.then_inc(conv_ready, 1)

            def turn_normed(w, p):
                g = w * NP + p
                pe.wait_ge(xhat_ready, g + 2)
                pe.wait_ge(kvnT_ready, g + 1)
                for k in range(KC):
                    ins = pe.transpose(b_kvT[:, k * P:(k + 1) * P], xhat[:, p, k * P:(k + 1) * P], ident[:, :])
                ins.then_inc(kvn_turned, 1)

            def key_value(w, p):
                pe.wait_ge(kvnT_ready, w * NP + p + 2)
                pe.wait_ge(kv_copied, reuse(w, p, NP))
                for k in range(KC):
                    ins = pe.matmul(b_kv[p % 2][:, :], kvnT[:, p % 2, k, :], wkv_s[:, k, :],
                                    start=(k == 0), stop=(k == KC - 1))
                ins.then_inc(kv_ready, 1)

            with pe.Fori(0, NW) as w:
                turn_patch(w, 0)
                for p in range(NP):
                    if p + 1 < NP:
                        turn_patch(w, p + 1)
                    project_patch(w, p)
                turn_normed(w, 0)
                for p in range(NP):
                    if p + 1 < NP:
                        turn_normed(w, p + 1)
                    key_value(w, p)
                    if p == 5:
                        pe.wait_ge(redhat_ready, w + 2)
                        pe.wait_ge(q_copied, w + 1)
                        for k in range(KC):
                            ins = pe.transpose(b_q[:, k * P:(k + 1) * P], redhat[:, k * P:(k + 1) * P], ident[:, :])
                        ins.then_inc(red_turned, 1)
                    if p == 6:
                        pe.wait_ge(redT_ready, w + 2)
                        for k in range(KC):
                            ins = pe.matmul(b_q[:, C:2 * C], redT[:, k, :], wq_s[:, k, :],
                                            start=(k == 0), stop=(k == KC - 1))
                        ins.then_inc(q_ready, 1)
            pe.wait_ge(kv_copied, NW * NP + CREDIT)
            pe.wait_ge(q_copied, NW + 1)

            n_turn, n_mm = [0], [0]

            def turn_rows(src, chunks=KC):
                n = n_turn[0]
                n_turn[0] += 1
                if n >= 2:
                    pe.wait_ge(turned_copied, n - 1)
                for k in range(chunks):
                    ins = pe.transpose(b_turn[n % 2][:, k * P:(k + 1) * P], src[:, k * P:(k + 1) * P], ident[:, :])
                ins.then_inc(turned, 1)

            def project(xt, t, w_s, lo, hi, copied, chunks=KC):
                n = n_mm[0]
                n_mm[0] += 1
                pe.wait_ge(turned_copied, copied)
                if n >= 4:
                    pe.wait_ge(product_read, n - 3)
                for k in range(chunks):
                    ins = pe.matmul(b_mm[n % 4][:, 0:hi - lo], xt[:, k, t * P:(t + 1) * P], w_s[:, k, lo:hi],
                                    start=(k == 0), stop=(k == chunks - 1))
                ins.then_inc(product_ready, 1)

            pe.wait_ge(agg_ready, NW + 1)
            for n in range(NW):
                turn_rows(agg[:, n, :])
            for n in range(NW):
                project(XT, n, proj_s, 0, C, n + 1)
            for n in range(NW):
                pe.wait_ge(rows_ready, n + 1)
                turn_rows(local[:, n, :])
            for n in range(NW):
                project(XT2, n, mod_s, 0, C, NW + n + 1)
            for n in range(NW):
                pe.wait_ge(rows_ready, NW + n + 1)
                turn_rows(lhat[:, n, :])
            for n in range(NW):
                project(XT, n, gwkv_s, 0, 2 * C, 2 * NW + n + 1)
            n = 3 * NW
            pe.wait_ge(product_read, 2 * NW)
            for t in range(NW):
                turn_rows(hA[:, t, :])
            pe.wait_ge(a0w_loaded, 64)
            for t in range(2):
                project(XT2, t, a0w_s, 0, 2 * C, n + t + 1)
                project(XT2, t, a0w_s, 2 * C, 3 * C, n + t + 1)
            pe.wait_ge(rows_ready, 2 * NW + 1)
            turn_rows(gagg)
            project(XT, 0, gproj_s, 0, C, n + NW + 1)
            for t in range(2, NW):
                project(XT2, t, a0w_s, 0, 2 * C, n + t + 1)
                project(XT2, t, a0w_s, 2 * C, 3 * C, n + t + 1)
            pe.wait_ge(product_read, 3 * NW + 5)
            turn_rows(hA[:, NW, :])
            n += NW + 2
            project(XT2, NW, a0w_s, 0, 2 * C, n)
            project(XT2, NW, a0w_s, 2 * C, 3 * C, n)
            for t in range(T):
                pe.wait_ge(rows_ready, R0 + t + 1)
                turn_rows(attn0[:, t, :])
            for t in range(T):
                project(XT, t, a0wo_s, 0, C, n + t + 1)
            n += T

            def rank(rhs_own, rhs_all, width, totals=None):
                m = n_mm[0]
                n_mm[0] += 1
                pe.wait_ge(product_read, m - 3)
                b = b_mm[m % 4]
                ins = pe.matmul(b[:, 0:width], upper[:, :], rhs_own, start=True, stop=rhs_all is None)
                if rhs_all is not None:
                    ins = pe.matmul(b[:, 0:width], ones_sb[:, :], rhs_all, start=False, stop=True)
                if totals is not None:
                    for i, r in enumerate(totals):
                        ins = pe.matmul(b[:, 256:256 + E0], ones_sb[:, :], r, start=(i == 0), stop=(i == len(totals) - 1))
                ins.then_inc(product_ready, 1)

            def turn_x(ff, j, s, i):
                pe.wait_ge(ff.x_loaded[s], i * 16 + 16)
                pe.wait_ge(ff.xT_ready, j + AHEAD)
                for k in range(KC):
                    ins = pe.transpose(b_x[:, k * P:(k + 1) * P], xrow[:, s, k * P:(k + 1) * P], ident[:, :])
                ins.then_inc(ff.x_turned, 1)

            def turn_h(ff, j):
                pe.wait_ge(ff.h_copied, j + 1 + AHEAD)
                pe.wait_ge(ff.biased, j + AHEAD)
                for f in range(FC):
                    ins = pe.transpose(b_hT[f // 4][:, f % 4 * P:(f % 4 + 1) * P], h_sb[:, f * P:(f + 1) * P], ident[:, :])
                ins.then_inc(ff.h_turned, 1)

            def before_up(ff, j, s, i):
                pe.wait_ge(ff.xT_ready, j + 1 + AHEAD)
                pe.wait_ge(ff.w1_loaded[s], i * 16 + 16)
                pe.wait_ge(ff.h_copied, j + AHEAD)

            def before_down(ff, j, s, i, loads):
                pe.wait_ge(ff.active, j + 1 + AHEAD)
                pe.wait_ge(ff.w2_loaded[s], i * (16 * loads) + 16 * loads)
                pe.wait_ge(ff.y_ready, j + AHEAD)

            def up0(j, s, i):
                before_up(ff0, j, s, i)
                for n in range(2):
                    for k in range(KC):
                        ins = pe.matmul(b_h[n][:, :], xTs[:, s, k, :], w1_0[s][:, k, n * 512:(n + 1) * 512],
                                        start=(k == 0), stop=(k == KC - 1))
                ins.then_inc(ff0.up_ready, 1)

            def down0(j, s, i):
                before_down(ff0, j, s, i, 2)
                for f in range(FC):
                    ins = pe.matmul(b_y[:, 0:C], hTs[:, f, :], w2_0[s][:, f, :], start=(f == 0), stop=(f == FC - 1))
                ins.then_inc(ff0.down_ready, 1)

            def up1(j, s, i):
                before_up(ff1, j, s, i)
                for n in range(2):
                    for k in range(KC):
                        for e in range(2):
                            own = slice(e * SLOT, (e + 1) * SLOT)
                            ins = pe.matmul(b_h[n][own, :], xTs[:, s, k, own], w1_1[s][:, e, k, n * 512:(n + 1) * 512],
                                            start=(k == 0), stop=(k == KC - 1))
                ins.then_inc(ff1.up_ready, 1)

            def down1(j, s, i):
                before_down(ff1, j, s, i, 3)
                for f in range(FC):
                    for e in range(2):
                        own = slice(e * SLOT, (e + 1) * SLOT)
                        ins = pe.matmul(b_y[own, 0:C], hTs[:, f, own], w2_1[s][:, e, f, :], start=(f == 0), stop=(f == FC - 1))
                ins.then_inc(ff1.down_ready, 1)

            def expert_tiles(ff, count, up, down):
                for q in (ff.x_turned, ff.up_ready, ff.h_turned, ff.down_ready):
                    pe.sem_inc(q, AHEAD)
                turn_x(ff, 0, 0, 0)
                up(0, 0, 0)
                turn_x(ff, 1, 1, 0)
                turn_h(ff, 0)

                def body(j, s, i):
                    up(j + 1, 1 - s, i + s)
                    turn_x(ff, j + 2, s, i + 1)
                    down(j, s, i)
                    turn_h(ff, j + 1)
                trips = (count - 2) // 2
                with pe.Fori(0, trips) as i:
                    for s in range(2):
                        body(i * 2 + s, s, i)
                for j in range(2 * trips, count):
                    if j + 1 < count:
                        up(j + 1, (j + 1) % 2, (j + 1) // 2)
                    if j + 2 < count:
                        turn_x(ff, j + 2, j % 2, j // 2 + 1)
                    down(j, j % 2, j // 2)
                    if j + 1 < count:
                        turn_h(ff, j + 1)

            for t in range(T):
                pe.wait_ge(rows_ready, R0 + T + t + 1)
                turn_rows(hB[:, t, :])
            pe.wait_ge(gatew_loaded, 32)
            for t in range(T):
                project(XT2, t, rw_s, 0, E0, n + t + 1)
            n += T
            pe.wait_ge(rows_ready, R0 + 2 * T + 1)
            rank(msum[:, :, 0:E0], mcum[:, :, 0:E0], T * E0, (mcum[:, T - 1, 0:E0], msum[:, T - 1, 0:E0]))
            pe.wait_ge(product_read, n_mm[0])
            pe.wait_ge(turned_copied, n_turn[0])
            expert_tiles(ff0, NT0, up0, down0)
            pe.wait_ge(ff0.y_ready, NT0 + AHEAD)
            for t in range(T):
                pe.wait_ge(rows_ready, R0 + 1 + 2 * T + t + 1)
                turn_rows(hA[:, t, :])
            pe.wait_ge(a1w_loaded, 48)
            for t in range(T):
                for i in range(3):
                    project(XT, t, a1w_s, i * INNER, (i + 1) * INNER, n + t + 1)
            n += T
            for t in range(T):
                pe.wait_ge(rows_ready, R0 + 1 + 3 * T + t + 1)
                turn_rows(qkv1[:, t, 0:INNER], KI)
            for t in range(T):
                project(OT, t, a1wo_s, 0, C, n + t + 1, KI)
            n += T
            for t in range(T):
                pe.wait_ge(rows_ready, R0 + 1 + 4 * T + t + 1)
                turn_rows(hB[:, t, :])
            for t in range(T):
                project(XT, t, wg_s, 0, E1, n + t + 1)
            n += T
            pe.wait_ge(rows_ready, R0 + 1 + 5 * T + 1)
            rank(msum[:, 0, :], None, E1)
            pe.wait_ge(product_read, n_mm[0])
            pe.wait_ge(turned_copied, n_turn[0])
            expert_tiles(ff1, NPAIR, up1, down1)

        @block.scalar
        def _(act):
            step = Steps(act, act_step)
            for k in range(NCH):
                kn = P if k < NCH - 1 else KT
                act.wait_ge(setup_turned, k + 1)
                act.activation(convT[0:kn, k, :], bank[k % 2][0:kn, 0:C], ACT.Copy).then_inc(setup_copied, 1)
            act.wait_ge(setup_turned, NCH + 1)
            act.activation(vecT[:, :, :].rearrange("p k v -> p (k v)"), bank[4][:, 0:KC * 24], ACT.Copy).then_inc(setup_copied, 1)
            act.wait_ge(setup_turned, NCH + 2)
            act.activation(b1T[:, :, :].rearrange("p k v -> p (k v)"), bank[5][:, 0:FC * 24], ACT.Copy).then_inc(setup_copied, 1)
            act.wait_ge(setup_copied, NCH + 2)
            for s in (conv_copied, kv_copied):
                act.sem_inc(s, CREDIT)
            for s in (patchT_ready, kvnT_ready):
                act.sem_inc(s, 1)

            def vec(v, k):
                return vecT[:, k, v:v + 1]

            def std(lo, hi, n):
                act.wait_ge(var_ready, n)
                act.activation(sd[:, lo:hi], mv[:, lo:hi, 1], ACT.Sqrt, bias=eps_sb[:, 0:1]).then_inc(std_ready, 1)

            def affine_turned(dst, src, g, b):
                for k in range(KC):
                    ins = act.activation(dst[:, k, :], src[:, k * P:(k + 1) * P], ACT.Identity,
                                         scale=vec(g, k), bias=vec(b, k))
                return ins

            std(0, 1, 1)
            act.wait_ge(red_turned, 1)
            affine_turned(redT, b_q, 4, 5).then_inc(redT_ready, 1)
            act.wait_ge(q_ready, 1)
            act.activation(gq_sb[:, :], b_q[:, C:2 * C], ACT.Copy, scale=SCALE).then_inc(q_copied, 1)

            def patch_copied(w, p):
                act.wait_ge(patch_turned, w * NP + p + 1 + CREDIT)
                act.wait_ge(conv_ready, reuse(w, p, NP))
                act.activation(patchT[:, p % 2, 0:NCH - 1, :].rearrange("p k n -> p (k n)"), b_top[:, :], ACT.Copy)
                act.activation(patchT[0:KT, p % 2, NCH - 1, :], b_tail[0:KT, 0:P], ACT.Copy).then_inc(patchT_ready, 1)

            def raw_copied(w, p):
                act.wait_ge(conv_ready, w * NP + p + 1 + CREDIT)
                act.wait_ge(xhat_ready, w * NP + 1)
                act.activation(pe_raw[:, p, :], b_conv[p % 2][:, 0:C], ACT.Copy).then_inc(conv_copied, 1)

            def normed_copied(w, p):
                act.wait_ge(kvn_turned, w * NP + p + 1)
                act.wait_ge(kv_ready, reuse(w, p, NP))
                affine_turned(kvnT[:, p % 2], b_kvT, 2, 3).then_inc(kvnT_ready, 1)

            def kv_stored(w, p):
                act.wait_ge(kv_ready, w * NP + p + 1 + CREDIT)
                act.wait_ge(agg_ready, w + 1)
                act.activation(kvw[:, p, :], b_kv[p % 2][:, :], ACT.Copy).then_inc(kv_copied, 1)

            with act.Fori(0, NW) as w:
                patch_copied(w, 0)
                for p in range(NP):
                    if p + 1 < NP:
                        patch_copied(w, p + 1)
                    raw_copied(w, p)
                    if p in (3, 6):
                        std(p - 3, p, w * 4 + p // 3 + 1)
                normed_copied(w, 0)
                for p in range(NP):
                    if p + 1 < NP:
                        normed_copied(w, p + 1)
                    kv_stored(w, p)
                    if p == 0:
                        std(6, 9, w * 4 + 4)
                    if p == 1:
                        std(0, 1, w * 4 + 5)
                    if p == 5:
                        act.wait_ge(red_turned, w + 2)
                        affine_turned(redT, b_q, 0, 1).then_inc(redT_ready, 1)
                    if p == 6:
                        act.wait_ge(q_ready, w + 2)
                        act.wait_ge(agg_ready, w + 1)
                        act.activation(q_sb, b_q[:, C:2 * C], ACT.Copy, scale=SCALE).then_inc(q_copied, 1)
                act.wait_ge(scores_shifted, w + 1)
                act.activation(ex[:, :, :], sc[:, :, :], ACT.Exp).then_inc(exps_ready, 1)

            n_turn = [0]

            def rows_turned(dst, t, g=None, b=None, chunks=KC):
                n = n_turn[0]
                n_turn[0] += 1
                act.wait_ge(turned, n + 1)
                d = dst[:, :, t * P:(t + 1) * P]
                if g is None:
                    act.activation(d, b_turn[n % 2][:, 0:chunks * P].rearrange("p (k n) -> p k n", k=chunks), ACT.Copy)\
                        .then_inc(turned_copied, 1)
                else:
                    affine_turned(d, b_turn[n % 2], g, b).then_inc(turned_copied, 1)

            for n in range(NW):
                rows_turned(XT, n)
            for n in range(NW):
                rows_turned(XT2, n)
            std(0, NW, NW * 4 + 2)
            act.wait_ge(product_ready, NW)
            for n in range(NW):
                rows_turned(XT, n, 6, 7)
            act.wait_ge(scores_shifted, NW + 1)
            act.activation(ex[:, 0:NW, :], sc[:, 0:NW, :], ACT.Exp).then_inc(exps_ready, 1)
            act.wait_ge(product_ready, 3 * NW)
            for t in range(NW):
                rows_turned(XT2, t)
            rows_turned(XT, 0)
            rows_turned(XT2, NW)
            act.wait_ge(logits_shifted, 1)
            act.activation(S0[:, :, :, :], S0[:, :, :, :], ACT.Exp, scale=float(D0) ** -0.5).then_inc(attn_exps, 1)
            act.wait_ge(product_ready, 3 * NW + 5)
            for t in range(T):
                rows_turned(XT, t)
            for i in range(2):
                std(0, T, 4 * NW + 3 + i)
            act.wait_ge(product_ready, 3 * NW + 1 + 2 * T)
            for t in range(T):
                rows_turned(XT2, t)
            std(0, T, 4 * NW + 5)
            act.wait_ge(logits_shifted, 2)
            act.activation(gate[:, 1, :], gate[:, 0, :], ACT.Exp).then_inc(attn_exps, 1)

            def x_copied(ff, j, s, affine):
                act.wait_ge(ff.x_turned, j + 1 + AHEAD)
                act.wait_ge(ff.up_ready, j + 1)
                if affine:
                    act.wait_ge(ff.cur_ready, j + 1 + AHEAD)
                    for k in range(KC):
                        ins = act.activation(xTs[:, s, k, :], b_x[:, k * P:(k + 1) * P], ACT.Identity,
                                             scale=cur[:, s, k:k + 1], bias=cur[:, s, KC + k:KC + k + 1])
                else:
                    ins = act.activation(xTs[:, s, :, :].rearrange("p k n -> p (k n)"), b_x[:, 0:C], ACT.Copy)
                ins.then_inc(ff.xT_ready, 1)

            def h_stored(ff, j):
                act.wait_ge(ff.up_ready, j + 1 + AHEAD)
                act.wait_ge(ff.h_turned, j + AHEAD)
                for n in range(2):
                    ins = act.activation(h_sb[:, n * 512:(n + 1) * 512], b_h[n][:, :], ACT.Copy)
                ins.then_inc(ff.h_copied, 1)

            def activated(ff, j, func):
                act.wait_ge(ff.biased, j + 1 + AHEAD)
                act.wait_ge(ff.down_ready, j + AHEAD)
                act.activation(hTs.rearrange("p f n -> p (f n)"), hb, func).then_inc(ff.active, 1)

            def expert_tiles(ff, count, affine, func):
                for q in (ff.xT_ready, ff.h_copied, ff.active):
                    act.sem_inc(q, AHEAD)
                x_copied(ff, 0, 0, affine)
                h_stored(ff, 0)
                x_copied(ff, 1, 1, affine)
                activated(ff, 0, func)
                trips = (count - 2) // 2
                with act.Fori(0, trips) as i:
                    for s in range(2):
                        j = i * 2 + s
                        h_stored(ff, j + 1)
                        x_copied(ff, j + 2, s, affine)
                        activated(ff, j + 1, func)
                for j in range(2 * trips, count - 1):
                    h_stored(ff, j + 1)
                    if j + 2 < count:
                        x_copied(ff, j + 2, j % 2, affine)
                    activated(ff, j + 1, func)

            expert_tiles(ff0, NT0, True, ACT.Gelu)
            std(0, T, 4 * NW + 6)
            for t in range(T):
                rows_turned(XT, t)
            base = 3 * NW + 1 + 2 * T + T + T + 1
            act.wait_ge(product_read, base + 3 * T)
            act.activation(prod1[:, 0:T * 2 * INNER].rearrange("p (t n) -> p t n", t=T), qkv1[:, :, 0:2 * INNER], ACT.Square)\
                .then_inc(squares_ready, 1)
            act.wait_ge(norms_ready, 1)
            act.activation(rnorm[:, :, :], ssq[:, :, :], ACT.Sqrt).then_inc(norms_ready, 1)
            act.wait_ge(logits_shifted, 3)
            act.activation(S1[:, :, :, :], S1[:, :, :, :], ACT.Exp, scale=16.0, bias=neg16[:, 0:1]).then_inc(attn_exps, 1)
            for t in range(T):
                rows_turned(OT, t, chunks=KI)
            std(0, T, 4 * NW + 7)
            act.wait_ge(product_ready, base + 4 * T)
            for t in range(T):
                rows_turned(XT, t)
            act.wait_ge(logits_shifted, 4)
            act.activation(lg2[:, :, :], lg[:, :, :], ACT.Exp).then_inc(attn_exps, 1)
            expert_tiles(ff1, NPAIR, False, ACT.Relu)
            std(0, T, 4 * NW + 8)

        @block.vector
        def _(dve):
            step = Steps(dve, dve_step)

            def rstd(lo, hi, n):
                dve.wait_ge(std_ready, n)
                step(dve.reciprocal(rs[:, lo:hi], sd[:, lo:hi]))

            def normed(dst, src, i):
                return dve.tensor_scalar(dst, src, mv[:, i, 0:1], rs[:, i:i + 1], ALU.subtract, ALU.mult)

            dve.wait_ge(rows_loaded, 16 * N_ROWS)
            dve.wait_ge(consts_made, N_CONST)
            step(dve.bn_stats(stats[:, 0, :], cls_r))
            dve.bn_aggr(mv[:, 0, :], stats[:, 0, :]).then_inc(var_ready, 1)
            rstd(0, 1, 1)
            normed(redhat, cls_r, 0).then_inc(redhat_ready, 1)
            dve.sem_inc(xhat_ready, 1)
            dve.sem_inc(agg_ready, 1)

            PER = 22
            base = step.n

            def finish(lo, w):
                rstd(lo, lo + 3, w * 4 + lo // 3 + 2)
                for p in range(lo, lo + 3):
                    normed(xhat[:, p, :], pe_raw[:, p, :], p).then_inc(xhat_ready, 1)

            with dve.Fori(0, NW) as w:
                step.loop(base, w, PER)
                for p in range(NP):
                    dve.wait_ge(conv_copied, w * NP + p + 1 + CREDIT)
                    ins = dve.bn_stats(stats[:, p, :], pe_raw[:, p, :])
                    if p % 3 == 2:
                        step(ins)
                    if p in (5, 8):
                        finish(p - 5, w)
                    if p in (3, 5, 8):
                        batch = {3: 0, 5: 3, 8: 6}[p]
                        for i in range(batch, batch + 3):
                            ins = dve.bn_aggr(mv[:, i, :], stats[:, i, :])
                        ins.then_inc(var_ready, 1)
                step(dve.tensor_reduce(redhat, pe_raw.rearrange("p n c -> p c n"), AX.X, ALU.add))
                step(dve.tensor_scalar(red, redhat, 1.0 / NP, None, ALU.mult))
                step(dve.tensor_tensor(redb[:, bass.ds(w, 1), :].rearrange("p a c -> p (a c)"), red, projb_r, ALU.add))
                step(dve.bn_stats(stats[:, 0, :], red))
                finish(6, w)
                dve.bn_aggr(mv[:, 0, :], stats[:, 0, :]).then_inc(var_ready, 1)
                rstd(0, 1, w * 4 + 5)
                normed(redhat, red, 0).then_inc(redhat_ready, 1)
                dve.wait_ge(q_copied, w + 2)
                for r in range(3):
                    dve.wait_ge(kv_copied, w * NP + 3 * r + 3 + CREDIT)
                    keys = kvw[:, 3 * r:3 * r + 3, 0:C]
                    step(dve.tensor_tensor(keys, keys, q_sb.unsqueeze(1).to_broadcast([P, 3, C]), ALU.mult))
                    step(dve.tensor_reduce(sc[:, 3 * r:3 * r + 3, :],
                                           keys.rearrange("p n (h d) -> p n h d", h=H8), AX.X, ALU.add))
                step(dve.tensor_reduce(hx[:, 0, :], sc[:, :, :].rearrange("p n h -> p h n"), AX.X, ALU.max))
                dve.tensor_tensor(sc[:, :, :], sc[:, :, :], hx[:, 0, :].unsqueeze(1).to_broadcast([P, NP, H8]),
                                  ALU.subtract).then_inc(scores_shifted, 1)
                dve.wait_ge(exps_ready, w + 1)
                step(dve.tensor_reduce(hx[:, 1, :], ex[:, :, :].rearrange("p n h -> p h n"), AX.X, ALU.add))
                step(dve.reciprocal(hx[:, 2, :], hx[:, 1, :]))
                step(dve.tensor_tensor(ex[:, :, :], ex[:, :, :], hx[:, 2, :].unsqueeze(1).to_broadcast([P, NP, H8]), ALU.mult))
                vals = kvw[:, :, C:2 * C]
                step(dve.tensor_tensor(vals.rearrange("p n (h d) -> p n h d", h=H8), vals.rearrange("p n (h d) -> p n h d", h=H8),
                                       ex[:, :, :].unsqueeze(3).to_broadcast([P, NP, H8, DH]), ALU.mult))
                dve.tensor_reduce(agg[:, bass.ds(w, 1), :].rearrange("p a c -> p (a c)"), vals.rearrange("p n c -> p c n"),
                                  AX.X, ALU.add).then_inc(agg_ready, 1)
            step.loop(base, NW, PER)

            n_mm = [0]

            def product():
                n = n_mm[0]
                n_mm[0] += 1
                dve.wait_ge(product_ready, n + 1)
                return b_mm[n % 4]

            for n in range(NW):
                b = product()
                dve.tensor_tensor(local[:, n, :], b[:, 0:C], redb[:, n, :], ALU.add).then_inc(product_read, 1)
                dve.wait_ge(product_read, n + 1)
                dve.bn_stats(stats[:, n, :], local[:, n, :]).then_inc(rows_ready, 1)
            dve.wait_ge(rows_ready, NW)
            for n in range(NW):
                ins = dve.bn_aggr(mv[:, n, :], stats[:, n, :])
            ins.then_inc(var_ready, 1)
            for n in range(NW):
                b = product()
                dve.tensor_tensor(hA[:, n, :], b[:, 0:C], modb_r, ALU.add).then_inc(product_read, 1)
            rstd(0, NW, NW * 4 + 2)
            for n in range(NW):
                normed(lhat[:, n, :], local[:, n, :], n).then_inc(rows_ready, 1)
            for n in range(NW):
                b = product()
                dve.tensor_copy(gkv[:, n, :], b[:, :]).then_inc(product_read, 1)
            dve.wait_ge(product_read, 3 * NW)
            step(dve.tensor_tensor(gprod, gkv[:, :, 0:C], gq_sb[:, :].unsqueeze(1).to_broadcast([P, NW, C]), ALU.mult))
            step(dve.tensor_reduce(sc[:, 0:NW, :], gprod.rearrange("p n (h d) -> p n h d", h=H8), AX.X, ALU.add))
            step(dve.tensor_reduce(hx[:, 0, :], sc[:, 0:NW, :].rearrange("p n h -> p h n"), AX.X, ALU.max))
            dve.tensor_tensor(sc[:, 0:NW, :], sc[:, 0:NW, :], hx[:, 0, :].unsqueeze(1).to_broadcast([P, NW, H8]),
                              ALU.subtract).then_inc(scores_shifted, 1)
            dve.wait_ge(exps_ready, NW + 1)
            step(dve.tensor_reduce(hx[:, 1, :], ex[:, 0:NW, :].rearrange("p n h -> p h n"), AX.X, ALU.add))
            step(dve.reciprocal(hx[:, 2, :], hx[:, 1, :]))
            step(dve.tensor_tensor(ex[:, 0:NW, :], ex[:, 0:NW, :], hx[:, 2, :].unsqueeze(1).to_broadcast([P, NW, H8]), ALU.mult))
            step(dve.tensor_tensor(gprod.rearrange("p n (h d) -> p n h d", h=H8),
                                   gkv[:, :, C:2 * C].rearrange("p n (h d) -> p n h d", h=H8),
                                   ex[:, 0:NW, :].unsqueeze(3).to_broadcast([P, NW, H8, DH]), ALU.mult))
            dve.tensor_reduce(gagg, gprod.rearrange("p n c -> p c n"), AX.X, ALU.add).then_inc(rows_ready, 1)
            dve.wait_ge(rows_ready, 2 * NW + 1)
            step(dve.tensor_tensor(gprod[:, 0, :], cls_r, gprojb_r, ALU.add))

            def read_product(dst, row_):
                b = product()
                width = dst.free_size()
                if row_ is None:
                    dve.tensor_copy(dst, b[:, 0:width]).then_inc(product_read, 1)
                else:
                    dve.tensor_tensor(dst, b[:, 0:width], row_, ALU.add).then_inc(product_read, 1)

            def qkv_read(t):
                read_product(qkv0[:, t, 0:2 * C], bqkv_r[:, 0:2 * C])
                read_product(qkv0[:, t, 2 * C:3 * C], bqkv_r[:, 2 * C:3 * C])

            qkv_read(0)
            qkv_read(1)
            b = product()
            dve.tensor_tensor(hA[:, NW, :], b[:, 0:C], gprod[:, 0, :], ALU.add).then_inc(product_read, 1)
            for t in range(2, T):
                qkv_read(t)

            def spread(a, n, where):
                shape = list(a.shape)
                shape.insert(where, n)
                return a.unsqueeze(where).to_broadcast(shape)

            dve.wait_ge(product_read, n_mm[0])
            for t in range(T):
                pr = prod0[:, 0:(t + 1) * C].rearrange("p (s c) -> p s c", s=t + 1)
                step(dve.tensor_tensor(pr, qkv0[:, 0:t + 1, C:2 * C], spread(qkv0[:, t, 0:C], t + 1, 1), ALU.mult))
                step(dve.tensor_reduce(S0[:, t, :, 0:t + 1].rearrange("p h s -> p s h"),
                                       pr.rearrange("p s (h d) -> p s h d", h=H0), AX.X, ALU.add))
            flat0 = S0[:, :, :, :].rearrange("p t h s -> p (t h) s")
            step(dve.tensor_reduce(hs[:, 0, :], flat0, AX.X, ALU.max))
            dve.tensor_tensor(flat0, flat0, spread(hs[:, 0, :], T, 2), ALU.subtract).then_inc(logits_shifted, 1)
            dve.wait_ge(attn_exps, 1)
            step(dve.tensor_reduce(hs[:, 1, :], flat0, AX.X, ALU.add))
            step(dve.reciprocal(hs[:, 2, :], hs[:, 1, :]))
            step(dve.tensor_tensor(flat0, flat0, spread(hs[:, 2, :], T, 2), ALU.mult))
            for t in range(T):
                pr = prod0[:, 0:(t + 1) * C].rearrange("p (s h d) -> p s h d", s=t + 1, h=H0)
                step(dve.tensor_tensor(pr, qkv0[:, 0:t + 1, 2 * C:3 * C].rearrange("p s (h d) -> p s h d", h=H0),
                                       spread(S0[:, t, :, 0:t + 1].rearrange("p h s -> p s h"), D0, 3), ALU.mult))
                dve.tensor_reduce(attn0[:, t, :], prod0[:, 0:(t + 1) * C].rearrange("p (s c) -> p c s", s=t + 1),
                                  AX.X, ALU.add).then_inc(rows_ready, 1)
                dve.wait_ge(rows_ready, R0 + t + 1)

            n_std = [NW * 4 + 2]

            def row_stats(src):
                for t in range(T):
                    ins = dve.bn_stats(stats[:, t, :], src[:, t, :])
                step(ins)
                for t in range(T):
                    ins = dve.bn_aggr(mv[:, t, :], stats[:, t, :])
                ins.then_inc(var_ready, 1)
                n_std[0] += 1
                rstd(0, T, n_std[0])

            for t in range(T):
                read_product(yln[:, t, :], bo_r)
            dve.wait_ge(product_read, n_mm[0])
            row_stats(yln)
            for t in range(T):
                ins = normed(yln[:, t, :], yln[:, t, :], t)
            step(ins)
            step(dve.tensor_tensor(yln, yln, spread(gamma_r, T, 1), ALU.mult))
            step(dve.tensor_tensor(yln, yln, spread(beta_r, T, 1), ALU.add))
            step(dve.tensor_tensor(yln, yln, hA, ALU.add))
            row_stats(yln)
            for t in range(T):
                normed(hB[:, t, :], yln[:, t, :], t).then_inc(rows_ready, 1)
            dve.wait_ge(rows_ready, R0 + 2 * T)
            row_stats(hB)
            for t in range(T):
                ins = normed(hX[:, t, :], hB[:, t, :], t)
            step(ins)
            for t in range(T):
                read_product(lg[:, t, 0:E0], rb_r)
            dve.wait_ge(product_read, n_mm[0])
            for t in range(T):
                ins = dve.max(best[:, t, :], lg[:, t, 0:E0])
            step(ins)
            for t in range(T):
                ins = dve.max_index(besti[:, t, :], best[:, t, :], lg[:, t, 0:E0])
            step(ins)
            dve.tensor_tensor(gate[:, 0, :], best[:, :, 1], best[:, :, 0], ALU.subtract).then_inc(logits_shifted, 1)
            step(dve.tensor_copy(bestf[:, :, :], besti[:, :, 0:2]))
            for k in range(2):
                step(dve.tensor_tensor(oh[:, k, :, 0:E0], spread(iota_e[:, 0:E0], T, 1),
                                       spread(bestf[:, :, k], E0, 2), ALU.is_equal))
            step(dve.tensor_tensor(msum[:, :, 0:E0], oh[:, 0, :, 0:E0], oh[:, 1, :, 0:E0], ALU.add))

            def tiles_before(width):
                step(dve.memset(mcum[:, 0, 0:width], 0.0))
                for t in range(1, T):
                    step(dve.tensor_tensor(mcum[:, t, 0:width], mcum[:, t - 1, 0:width],
                                           (msum if width == E0 else oh[:, 0])[:, t - 1, 0:width], ALU.add))
            tiles_before(E0)
            dve.sem_inc(rows_ready, 1)
            b = product()
            ins = dve.tensor_copy(cnt[:, :], b[:, 256:256 + E0])
            step(ins)
            dve.tensor_copy(rk[:, :, 0:E0], b[:, 0:T * E0].rearrange("p (t e) -> p t e", t=T)).then_inc(product_read, 1)
            step(dve.tensor_scalar(ntile[:, :], cnt[:, :], 0.0, None, ALU.is_gt))
            for i in range(1, T):
                step(dve.scalar_tensor_tensor(ntile[:, :], cnt[:, :], float(i * P), ntile[:, :], ALU.is_gt, ALU.add))
            step(dve.tensor_tensor_scan(incl[:, :], ones_sb[:, 0:E0], ntile[:, :], 0.0, ALU.mult, ALU.add))
            step(dve.tensor_tensor(basee[:, :], incl[:, :], ntile[:, :], ALU.subtract))
            step(dve.tensor_scalar(basee[:, :], basee[:, :], float(P), None, ALU.mult))
            dve.wait_ge(product_read, n_mm[0])
            step(dve.tensor_tensor(rk[:, :, 0:E0], rk[:, :, 0:E0], spread(basee[:, :], T, 1), ALU.add))
            for k in range(2):
                step(dve.tensor_tensor(oh[:, k, :, 0:E0], oh[:, k, :, 0:E0], rk[:, :, 0:E0], ALU.mult))
                step(dve.tensor_reduce(slotf[:, k, :], oh[:, k, :, 0:E0], AX.X, ALU.add))
            step(dve.tensor_copy(slotu[:, :, :], slotf[:, :, :]))
            step(dve.tensor_tensor(cmp_t[:, :, :], spread(iota_t[:, 0:NT0], E0, 2), spread(incl[0:1, :], NT0, 1), ALU.is_ge))
            step(dve.tensor_reduce(eidf[:, :], cmp_t[:, :, :], AX.X, ALU.add))
            step(dve.tensor_scalar(eidf[:, :], eidf[:, :], float(E0 - 1), None, ALU.min))
            dve.tensor_copy(eid[:, :], eidf[:, :]).then_inc(route_ready, 1)
            dve.wait_ge(setup_copied, NCH + 2)
            for k in range(KC):
                dve.tensor_copy(tab[:, :, k], vecT[:, k, 8:8 + E0])
                dve.tensor_copy(tab[:, :, KC + k], vecT[:, k, 16:16 + E0])
            step(dve.tensor_copy(tab[:, :, 2 * KC:].rearrange("p e f -> p f e"), b1T[:, :, 0:E0]))
            dve.wait_ge(attn_exps, 2)
            step(dve.tensor_scalar(gate[:, 0, :], gate[:, 1, :], 1.0, None, ALU.add))
            step(dve.reciprocal(gate[:, 2, :], gate[:, 0, :]))
            step(dve.tensor_tensor(gate[:, 3, :], gate[:, 1, :], gate[:, 2, :], ALU.mult))
            step(dve.tensor_tensor(gate[:, 0, :], gate[:, 2, :], gate[:, 3, :], ALU.add))
            step(dve.tensor_scalar(gate[:, 0, :], gate[:, 0, :], 1.0, None, ALU.add))
            dve.wait_ge(route_ready, 1)

            def biased0(ff, j, s):
                dve.wait_ge(ff.h_turned, j + 1 + AHEAD)
                dve.wait_ge(ff.active, j + AHEAD)
                for n in range(2):
                    ins = dve.tensor_tensor(hb[:, n * 512:(n + 1) * 512].rearrange("p (f n) -> p f n", f=4),
                                            b_hT[n][:, :].rearrange("p (f n) -> p f n", f=4),
                                            spread(cur[:, s, 2 * KC + 4 * n:2 * KC + 4 * n + 4], P, 2), ALU.add)
                ins.then_inc(ff.biased, 1)

            def biased1(ff, j, s):
                dve.wait_ge(ff.h_turned, j + 1 + AHEAD)
                dve.wait_ge(ff.active, j + AHEAD)
                for n in range(2):
                    bias = b1T[:, 4 * n:4 * n + 4, bass.ds(j * 2 + E0, 2)]
                    ins = dve.tensor_tensor(hb[:, n * 512:(n + 1) * 512].rearrange("p (f e n) -> p f e n", f=4, e=2),
                                            b_hT[n][:, :].rearrange("p (f e n) -> p f e n", f=4, e=2),
                                            spread(bias, SLOT, 3), ALU.add)
                ins.then_inc(ff.biased, 1)

            def y_read(ff, j, s, i, loads):
                dve.wait_ge(ff.down_ready, j + 1 + AHEAD)
                dve.wait_ge(ff.w2_loaded[s], i * (16 * loads) + 16 * loads)
                dve.wait_ge(ff.y_free, j + 1)
                dve.tensor_tensor(y_sb[:, s, :], b_y[:, 0:C], b2_r[:, s, :], ALU.add).then_inc(ff.y_ready, 1)

            def expert_tiles(ff, count, cur_read, biased, loads):
                for q in (ff.cur_ready, ff.biased, ff.y_ready):
                    dve.sem_inc(q, AHEAD)
                cur_read(0, 0)
                cur_read(1, 1)
                biased(ff, 0, 0)
                trips = (count - 2) // 2
                with dve.Fori(0, trips) as i:
                    for s in range(2):
                        j = i * 2 + s
                        cur_read(j + 2, s)
                        y_read(ff, j, s, i, loads)
                        biased(ff, j + 1, 1 - s)
                for j in range(2 * trips, count):
                    if j + 2 < count:
                        cur_read(j + 2, j % 2)
                    y_read(ff, j, j % 2, j // 2, loads)
                    if j + 1 < count:
                        biased(ff, j + 1, (j + 1) % 2)

            with dve.register("tile_expert") as expert:
                def cur_read(j, s):
                    dve.reg_load(expert, eid[0:1, bass.ds(j, 1)])
                    e = dve.snap(expert, min_val=0, max_val=E0 - 1)
                    dve.wait_ge(ff0.xT_ready, j + 1)
                    dve.wait_ge(ff0.biased, j + 1)
                    dve.tensor_copy(cur[:, s, :].unsqueeze(1), tab[:, bass.ds(e, 1), :]).then_inc(ff0.cur_ready, 1)
                expert_tiles(ff0, NT0, cur_read, biased0, 2)

            dve.wait_ge(gathered, 16 * 2 * T)
            for t in range(T):
                ins = dve.tensor_scalar(hX[:, t, :], hB[:, t, :], gate[:, 0, t:t + 1], None, ALU.mult)
            step(ins)
            for k in range(2):
                for t in range(T):
                    ins = dve.scalar_tensor_tensor(hX[:, t, :], yg[:, k, t, :], gate[:, 2 + k, t:t + 1], hX[:, t, :],
                                                   ALU.mult, ALU.add)
                step(ins)
            row_stats(hX)
            for t in range(T):
                normed(hA[:, t, :], hX[:, t, :], t).then_inc(rows_ready, 1)

            for t in range(T):
                for i in range(3):
                    read_product(qkv1[:, t, i * INNER:(i + 1) * INNER], None)
            dve.wait_ge(squares_ready, 1)
            dve.tensor_reduce(ssq[:, :, :], prod1[:, 0:T * 2 * INNER].rearrange("p (t h d) -> p t h d", t=T, h=2 * H1),
                              AX.X, ALU.add).then_inc(norms_ready, 1)
            dve.wait_ge(norms_ready, 2)
            step(dve.tensor_scalar(ssq[:, :, :], rnorm[:, :, :], 1e-12, None, ALU.max))
            step(dve.reciprocal(rnorm[:, :, :], ssq[:, :, :]))
            for t in range(T):
                pr = prod1[:, 0:T * INNER].rearrange("p (s c) -> p s c", s=T)
                step(dve.tensor_tensor(pr, qkv1[:, :, INNER:2 * INNER], spread(qkv1[:, t, 0:INNER], T, 1), ALU.mult))
                step(dve.tensor_reduce(S1[:, t, :, :].rearrange("p h s -> p s h"),
                                       pr.rearrange("p s (h d) -> p s h d", h=H1), AX.X, ALU.add))
            step(dve.tensor_tensor(S1[:, :, :, :], S1[:, :, :, :], spread(rnorm[:, :, 0:H1], T, 3), ALU.mult))
            dve.tensor_tensor(S1[:, :, :, :], S1[:, :, :, :], spread(rnorm[:, :, H1:].rearrange("p s h -> p h s"), T, 1),
                              ALU.mult).then_inc(logits_shifted, 1)
            dve.wait_ge(attn_exps, 3)
            flat1 = S1[:, :, :, :].rearrange("p t h s -> p (t h) s")
            hs1 = hs[:, :, 0:T * H1]
            step(dve.tensor_reduce(hs1[:, 0, :], flat1, AX.X, ALU.add))
            step(dve.tensor_scalar(hs1[:, 1, :], hs1[:, 0, :], 1e-6, None, ALU.max))
            step(dve.reciprocal(hs1[:, 2, :], hs1[:, 1, :]))
            step(dve.tensor_tensor(flat1, flat1, spread(hs1[:, 2, :], T, 2), ALU.mult))
            for t in range(T):
                pr = prod1[:, 0:T * INNER].rearrange("p (s h d) -> p s h d", s=T, h=H1)
                step(dve.tensor_tensor(pr, qkv1[:, :, 2 * INNER:].rearrange("p s (h d) -> p s h d", h=H1),
                                       spread(S1[:, t, :, :].rearrange("p h s -> p s h"), D1, 3), ALU.mult))
                dve.tensor_reduce(qkv1[:, t, 0:INNER], prod1[:, 0:T * INNER].rearrange("p (s c) -> p c s", s=T),
                                  AX.X, ALU.add).then_inc(rows_ready, 1)
                dve.wait_ge(rows_ready, R0 + 1 + 3 * T + t + 1)
            for t in range(T):
                b = product()
                dve.tensor_tensor(hX[:, t, :], b[:, 0:C], hA[:, t, :], ALU.add).then_inc(product_read, 1)
            dve.wait_ge(product_read, n_mm[0])
            row_stats(hX)
            for t in range(T):
                normed(hB[:, t, :], hX[:, t, :], t).then_inc(rows_ready, 1)

            for t in range(T):
                read_product(lg[:, t, :], bg_r)
            dve.wait_ge(product_read, n_mm[0])
            step(dve.tensor_reduce(gate[:, 0, :], lg[:, :, :], AX.X, ALU.max))
            dve.tensor_tensor(lg[:, :, :], lg[:, :, :], spread(gate[:, 0, :], E1, 2), ALU.subtract).then_inc(logits_shifted, 1)
            dve.wait_ge(attn_exps, 4)
            for t in range(T):
                ins = dve.max(best[:, t, :], lg2[:, t, :])
            step(ins)
            for t in range(T):
                ins = dve.max_index(besti[:, t, :], best[:, t, :], lg2[:, t, :])
            step(ins)
            step(dve.tensor_copy(bestf[:, :, :], besti[:, :, 0:2]))
            step(dve.tensor_tensor(oh[:, 0, :, :], spread(iota_e[:, :], T, 1), spread(bestf[:, :, 0], E1, 2), ALU.is_equal))
            dve.tensor_reduce(msum[:, 0, :], oh[:, 0, :, :].rearrange("p t e -> p e t"), AX.X, ALU.add).then_inc(rows_ready, 1)
            tiles_before(E1)
            step(dve.tensor_reduce(gate[:, 1, :], lg2[:, :, :], AX.X, ALU.add))
            step(dve.reciprocal(gate[:, 2, :], gate[:, 1, :]))
            b = product()
            dve.tensor_tensor(rk[:, :, :], mcum[:, :, :], spread(b[:, 0:E1], T, 1), ALU.add).then_inc(product_read, 1)
            dve.wait_ge(product_read, n_mm[0])
            step(dve.tensor_tensor(oh[:, 0, :, :], oh[:, 0, :, :], rk[:, :, :], ALU.mult))
            step(dve.tensor_reduce(slotf[:, 0, :], oh[:, 0, :, :], AX.X, ALU.add))
            step(dve.tensor_scalar(gate[:, 0, :], slotf[:, 0, :], float(CAP), None, ALU.is_lt))
            step(dve.tensor_scalar(slotf[:, 1, :], slotf[:, 0, :], float(CAP), None, ALU.min))
            step(dve.scalar_tensor_tensor(slotf[:, 1, :], bestf[:, :, 0], float(SLOT), slotf[:, 1, :], ALU.mult, ALU.add))
            step(dve.tensor_copy(gslotu[:, :], slotf[:, 1, :]))
            step(dve.tensor_tensor(slotf[:, 1, :], slotf[:, 1, :], trash[:, :], ALU.subtract))
            step(dve.tensor_tensor(slotf[:, 1, :], slotf[:, 1, :], gate[:, 0, :], ALU.mult))
            step(dve.tensor_tensor(slotf[:, 1, :], slotf[:, 1, :], trash[:, :], ALU.add))
            dve.tensor_copy(slotu[:, 0, :], slotf[:, 1, :]).then_inc(route_ready, 1)
            step(dve.tensor_tensor(gate[:, 3, :], gate[:, 0, :], gate[:, 2, :], ALU.mult))
            expert_tiles(ff1, NPAIR, lambda j, s: None, biased1, 3)
            dve.wait_ge(gathered, 16 * 3 * T)
            for t in range(T):
                ins = dve.scalar_tensor_tensor(hX[:, t, :], yg[:, 0, t, :], gate[:, 3, t:t + 1], hB[:, t, :],
                                               ALU.mult, ALU.add)
            step(ins)
            row_stats(hX)
            for t in range(T):
                ins = normed(hA[:, t, :], hX[:, t, :], t).then_inc(rows_ready, 1)


TOK, A0, FF0, A1, FF1 = "L0_tok_", "L0_attn_", "L0_ffn_", "L1_attn_", "L1_ffn_"


def kernel(**inputs):
    import numpy as _np
    import concourse.bacc as _bacc
    from concourse import mybir as _mybir
    from concourse.bass_utils import run_bass_kernel_spmd as _run

    nc = _bacc.Bacc("TRN2", target_bir_lowering=False, num_devices=1)
    arrays = {}

    def arg(name):
        a = _np.ascontiguousarray(inputs[name])
        arrays[f"in_{name}_dram"] = a
        return nc.dram_tensor(f"in_{name}_dram", a.shape, _mybir.dt.from_np(a.dtype), kind="ExternalInput").ap()

    vecs = [arg(TOK + n) for n in ("la_ln_q_g", "la_ln_q_b", "la_ln_kv_g", "la_ln_kv_b",
                                   "ga_ln_q_g", "ga_ln_q_b", "ga_ln_kv_g", "ga_ln_kv_b")]
    B, T, C = inputs["x"].shape[0], 5, inputs[A0 + "Wo"].shape[1]
    out = nc.dram_tensor("out_0_dram", (B, T, C), _mybir.dt.float32, kind="ExternalOutput").ap()
    build_program(
        nc, arg("x"), arg(TOK + "conv_w"), arg(TOK + "class_emb"), vecs, arg(TOK + "la_wq"), arg(TOK + "la_wkv"),
        arg(TOK + "la_proj_w"), arg(TOK + "la_proj_b"), arg(TOK + "ga_wq"), arg(TOK + "ga_wkv"),
        arg(TOK + "ga_proj_w"), arg(TOK + "ga_proj_b"), arg(TOK + "mod_w"), arg(TOK + "mod_b"),
        [arg(A0 + n) for n in ("Wq", "Wk", "Wv")], [arg(A0 + n) for n in ("bq", "bk", "bv")],
        arg(A0 + "Wo"), arg(A0 + "bo"), arg(A0 + "gamma"), arg(A0 + "beta"),
        arg(FF0 + "router_W"), arg(FF0 + "router_b"), arg(FF0 + "ln_g"), arg(FF0 + "ln_b"),
        arg(FF0 + "W1"), arg(FF0 + "b1"), arg(FF0 + "W2"), arg(FF0 + "b2"),
        arg(A1 + "Wq"), arg(A1 + "Wkv"), arg(A1 + "Wo"),
        arg(FF1 + "Wg"), arg(FF1 + "bg"), arg(FF1 + "W1"), arg(FF1 + "b1"), arg(FF1 + "W2"), arg(FF1 + "b2"), out)
    r = _run(nc, [arrays], core_ids=[0])
    return r.results[0]["out_0_dram"]
```

```python
from contextlib import ExitStack

import concourse.bass as bass
from concourse import mybir

ALU = mybir.AluOpType
ACT = mybir.ActivationFunctionType
AX = mybir.AxisListType
F32 = mybir.dt.float32
I32 = mybir.dt.int32
U32 = mybir.dt.uint32
P = 128


def reuse(w, p, per):
    n = w * per + p + CREDIT
    return n if p == 0 else n - 2 if p == 1 else n - 1


CREDIT = 3


class Steps:

    def __init__(self, eng, sem):
        self.eng, self.sem, self.n = eng, sem, 0

    def __call__(self, ins):
        ins.then_inc(self.sem, 1)
        self.n = self.n + 1
        self.eng.wait_ge(self.sem, self.n)

    def loop(self, base, trip, per):
        self.n = base + trip * per


def build_program(nc, x, conv_w, class_emb, tok_vecs, la_wq, la_wkv, la_proj_w, la_proj_b, ga_wq, ga_wkv,
                  ga_proj_w, ga_proj_b, mod_w, mod_b, a0_w, a0_b, a0_wo, a0_bo, a0_gamma, a0_beta,
                  f0_router_w, f0_router_b, f0_ln_g, f0_ln_b, f0_w1, f0_b1, f0_w2, f0_b2,
                  a1_wq, a1_wkv, a1_wo, f1_wg, f1_bg, f1_w1, f1_b1, f1_w2, f1_b2, out):
    B, CH, IH, IW = x.shape
    C, _, PS, _ = conv_w.shape
    assert B == P and C == 2 * P
    KC = C // P
    CS = 3
    G = IH // PS // CS
    NW = G * G
    NP = CS * CS
    T = NW + 1
    ROWS = G * CS * PS
    KP = CH * PS * PS
    NCH = -(-KP // P)
    KT = KP - (NCH - 1) * P
    H8 = 8
    DH = C // H8
    SCALE = float(C) ** -0.5
    LN_EPS = 1e-5

    H0 = 16
    D0 = C // H0
    E0, _, F0 = f0_w1.shape
    FC = F0 // P
    NT0 = (2 * T * P - E0) // P + E0
    H1 = 8
    INNER = a1_wq.shape[1]
    D1 = INNER // H1
    KI = INNER // P
    E1 = f1_w1.shape[0]
    CAP = -(-T * P // E1)
    SLOT = 64
    NPAIR = E1 // 2
    assert CAP < SLOT and F0 == f1_w1.shape[2]

    xs0 = nc.dram_tensor("xs0", [NT0 * P, C], F32, kind="Internal").ap()
    ys0 = nc.dram_tensor("ys0", [NT0 * P, C], F32, kind="Internal").ap()
    xs1 = nc.dram_tensor("xs1", [E1 * SLOT + T * P, C], F32, kind="Internal").ap()
    ys1 = nc.dram_tensor("ys1", [E1 * SLOT, C], F32, kind="Internal").ap()

    ctx = ExitStack()
    with ctx:
        def sb(name, shape, dt=F32):
            return ctx.enter_context(nc.sbuf_tensor(name, shape, dt))

        def sem(name):
            return ctx.enter_context(nc.semaphore(name))

        IMG = CH * ROWS * IW
        AR = 45400
        arena = sb("arena", [P, AR])

        def at(off, size, pat=None, /, **kw):
            a = arena[:, off:off + size]
            return a.rearrange(pat, **kw) if pat else a

        img = at(0, IMG, "p (c i j) -> p c i j", c=CH, i=ROWS)
        o = IMG
        packed = at(o, 2 * KP, "p (s k) -> p s k", s=2); o += 2 * KP
        patchT = at(o, 2 * NCH * P, "p (s k n) -> p s k n", s=2, k=NCH); o += 2 * NCH * P
        pe_raw = at(o, NP * C, "p (n c) -> p n c", n=NP); o += NP * C
        xhat = at(o, NP * C, "p (n c) -> p n c", n=NP); o += NP * C
        kvw = at(o, NP * 2 * C, "p (n c) -> p n c", n=NP)
        convw_raw = at(o, KC * KP, "p (h k) -> p h k", h=KC)
        vec_raw = at(o + KC * KP, C)
        b1_raw = at(o + KC * KP + C, F0); o += NP * 2 * C
        kvnT = at(o, 2 * KC * P, "p (s k n) -> p s k n", s=2, k=KC); o += 2 * KC * P
        redT = at(o, KC * P, "p (k n) -> p k n", k=KC); o += KC * P
        q_sb = at(o, C); o += C
        agg = at(o, NW * C, "p (n c) -> p n c", n=NW); o += NW * C
        redb = at(o, NW * C, "p (n c) -> p n c", n=NW); o += NW * C
        red = at(o, C); o += C
        redhat = at(o, C); o += C
        convT = at(o, NCH * C, "p (k c) -> p k c", k=NCH); o += NCH * C

        def wt(n):
            nonlocal o
            a = at(o, KC * n, "p (k n) -> p k n", k=KC)
            o += KC * n
            return a
        wq_s, wkv_s, proj_s, gwq_s, gwkv_s, gproj_s, mod_s = wt(C), wt(2 * C), wt(C), wt(C), wt(2 * C), wt(C), wt(C)
        assert o <= AR, o

        o = 0
        a0w_s = at(0, KC * 3 * C, "p (k n) -> p k n", k=KC); o += KC * 3 * C
        a0wo_s = at(o, KC * C, "p (k n) -> p k n", k=KC); o += KC * C
        qkv0 = at(o, T * 3 * C, "p (t n) -> p t n", t=T); o += T * 3 * C
        prod0 = at(o, T * C, "p (s c) -> p s c", s=T); o += T * C
        weighted0 = [prod0, qkv0[:, :, 0:C], qkv0[:, :, C:2 * C]]
        local = at(o, NW * C, "p (n c) -> p n c", n=NW); o += NW * C
        lhat = at(o, NW * C, "p (n c) -> p n c", n=NW); o += NW * C
        gkv = at(o, NW * 2 * C, "p (n c) -> p n c", n=NW); o += NW * 2 * C
        gprod = at(o, NW * C, "p (n c) -> p n c", n=NW); o += NW * C
        gagg = at(o, C); o += C
        residual = at(o, T * C, "p (t c) -> p t c", t=T); o += T * C
        yln = at(o, T * C, "p (t c) -> p t c", t=T); o += T * C
        assert o <= 16384, o
        PAIR = 2 * KC * F0
        up_at = [0, 2 * PAIR, 4 * PAIR]
        down_at = [o_ + PAIR for o_ in up_at]
        w1_0 = [at(16384 + i * 2 * KC * F0, KC * F0, "p (k f) -> p k f", k=KC) for i in range(2)]
        w2_0 = [at(16384 + i * 2 * KC * F0 + KC * F0, FC * C, "p (f c) -> p f c", f=FC) for i in range(2)]
        o = 24576
        hB = at(o, T * C, "p (t c) -> p t c", t=T)
        squares = at(o, 2 * INNER); o += T * C
        assert 2 * INNER <= T * C
        down_at.append(o)
        hA = at(o, T * C, "p (t c) -> p t c", t=T); o += T * C
        hX = at(o, T * C, "p (t c) -> p t c", t=T); o += T * C
        XT = at(o, KC * T * P, "p (k n) -> p k n", k=KC); o += KC * T * P
        XT2 = at(o, KC * T * P, "p (k n) -> p k n", k=KC); o += KC * T * P
        OT = at(o - 2 * KC * T * P, KI * T * P, "p (k n) -> p k n", k=KI)
        assert KI == 2 * KC
        assert o - down_at[3] >= PAIR
        up_at.append(o)
        a1w_s = at(o, KC * 3 * INNER, "p (k n) -> p k n", k=KC); o += KC * 3 * INNER
        a1wo_s = at(o, KI * C, "p (k n) -> p k n", k=KI); o += KI * C
        assert o <= IMG + 2 * KP + 2 * NCH * P + 2 * NP * C + NP * 2 * C, o
        assert o - up_at[3] >= PAIR
        w1_1 = [at(i, PAIR, "p (e k f) -> p e k f", e=2, k=KC) for i in up_at]
        w2_1 = [at(i, PAIR, "p (e f c) -> p e f c", e=2, f=FC) for i in down_at]
        work = o
        qkv1 = at(o, T * 3 * INNER, "p (t n) -> p t n", t=T); o += T * 3 * INNER
        prod1 = at(o, T * INNER, "p (s c) -> p s c", s=T); o += T * INNER
        weighted1 = [prod1, qkv1[:, :, 0:INNER], qkv1[:, :, INNER:2 * INNER]]
        assert o <= AR, o
        o = work
        SLOTS1 = 4
        xrow = at(o, SLOTS1 * C, "p (s c) -> p s c", s=SLOTS1); o += SLOTS1 * C
        xTs = at(o, SLOTS1 * KC * P, "p (s k n) -> p s k n", s=SLOTS1, k=KC); o += SLOTS1 * KC * P
        h_sb = at(o, F0); o += F0
        hb = at(o, F0); o += F0
        hTs = at(o, FC * P, "p (f n) -> p f n", f=FC); o += FC * P
        y_sb = at(o, SLOTS1 * C, "p (s c) -> p s c", s=SLOTS1); o += SLOTS1 * C
        b2_r = at(o, SLOTS1 * C, "p (s c) -> p s c", s=SLOTS1); o += SLOTS1 * C
        yg = at(o, 2 * T * C, "p (k t c) -> p k t c", k=2, t=T); o += 2 * T * C
        assert o <= AR, o

        rows_sb = sb("rows_sb", [P, 3 * C + 3 * C + 3 * C + C + E0 + E1])
        o = 0

        def row(n):
            nonlocal o
            o += n
            return rows_sb[:, o - n:o]
        projb_r, gprojb_r, modb_r, bqkv_r, bo_r, gamma_r, beta_r, cls_r, rb_r, bg_r = (
            row(C), row(C), row(C), row(3 * C), row(C), row(C), row(C), row(C), row(E0), row(E1))
        ident = sb("ident", [P, P])
        ones_sb = sb("ones_sb", [P, P])
        upper = sb("upper", [P, P])
        vecT = sb("vecT", [P, KC, 24])
        b1T = sb("b1T", [P, FC, 24])
        eps_sb = sb("eps_sb", [P, 1])
        gq_sb = sb("gq_sb", [P, C])
        stats = sb("stats", [P, NP, 6])
        mv = sb("mv", [P, NP, 2])
        sd = sb("sd", [P, NP])
        rs = sb("rs", [P, NP])
        sc = sb("sc", [P, NP, H8])
        ex = sb("ex", [P, NP, H8])
        hx = sb("hx", [P, 4, H8])

        zeros = sb("zeros", [P, C])
        S0 = sb("S0", [P, T, H0, T])
        S1 = sb("S1", [P, T, H1, T])
        hs = sb("hs", [P, 3, T * H0])
        ssq = sb("ssq", [P, T, 2 * H1])
        rnorm = sb("rnorm", [P, T, 2 * H1])
        neg16 = sb("neg16", [P, 1])
        rw_s = sb("rw_s", [P, KC, E0])
        wg_s = sb("wg_s", [P, KC, E1])
        iota_e = sb("iota_e", [P, E1])
        iota_t = sb("iota_t", [1, NT0 + 1])
        trash = sb("trash", [P, T])
        lg = sb("lg", [P, T, E1])
        lg2 = sb("lg2", [P, T, E1])
        best = sb("best", [P, T, 8])
        besti = sb("besti", [P, T, 8], U32)
        bestf = sb("bestf", [P, T, 2])
        oh = sb("oh", [P, 2, T, E1])
        msum = sb("msum", [P, T, E1])
        mcum = sb("mcum", [P, T, E1])
        rk = sb("rk", [P, T, E1])
        cnt = sb("cnt", [P, E0])
        ntile = sb("ntile", [P, E0])
        incl = sb("incl", [P, E0])
        basee = sb("basee", [P, E0])
        slotf = sb("slotf", [P, 2, T])
        slotu = sb("slotu", [P, 2, T], U32)
        gslotu = sb("gslotu", [P, T], U32)
        cmp_t = sb("cmp_t", [1, NT0, E0])
        eidf = sb("eidf", [1, NT0])
        eid = sb("eid", [1, NT0], I32)
        gate = sb("gate", [P, 4, T])
        tab = sb("tab", [P, E0, 2 * KC + FC])
        cur = sb("cur", [P, 2, 2 * KC + FC])

        bank = [ctx.enter_context(nc.psum_tensor(f"bank{i}", [P, 512], F32)) for i in range(8)]
        b_top, b_tail, b_conv, b_kvT, b_kv, b_q = bank[0], bank[1], bank[2:4], bank[4], bank[5:7], bank[7]
        b_turn, b_mm = bank[0:2], bank[2:6]
        b_x, b_h, b_hT, b_y = bank[0], bank[1:3], bank[3:5], bank[5]

        convw_loaded = sem("convw_loaded")
        img_rows = [sem(f"img_rows{i}") for i in range(CS)]
        vecs_loaded = sem("vecs_loaded")
        cls_loaded = sem("cls_loaded")
        gwq_loaded = sem("gwq_loaded")
        tokw_loaded = sem("tokw_loaded")
        rows_loaded = sem("rows_loaded")
        consts_made = sem("consts_made")
        setup_turned = sem("setup_turned")
        setup_copied = sem("setup_copied")
        patch_packed = sem("patch_packed")
        patch_turned = sem("patch_turned")
        patchT_ready = sem("patchT_ready")
        conv_ready = sem("conv_ready")
        conv_copied = sem("conv_copied")
        var_ready = sem("var_ready")
        std_ready = sem("std_ready")
        xhat_ready = sem("xhat_ready")
        kvn_turned = sem("kvn_turned")
        kvnT_ready = sem("kvnT_ready")
        kv_ready = sem("kv_ready")
        kv_copied = sem("kv_copied")
        redhat_ready = sem("redhat_ready")
        red_turned = sem("red_turned")
        redT_ready = sem("redT_ready")
        q_ready = sem("q_ready")
        q_copied = sem("q_copied")
        scores_shifted = sem("scores_shifted")
        exps_ready = sem("exps_ready")
        agg_ready = sem("agg_ready")
        dve_step = sem("dve_step")
        act_step = sem("act_step")
        pool_step = sem("pool_step")
        turned = sem("turned")
        turned_copied = sem("turned_copied")
        product_ready = sem("product_ready")
        product_read = sem("product_read")
        rows_ready = sem("rows_ready")
        out_stored = sem("out_stored")
        a0w_loaded = sem("a0w_loaded")
        a1w_loaded = sem("a1w_loaded")
        gatew_loaded = sem("gatew_loaded")
        scratch_zeroed = sem("scratch_zeroed")
        logits_shifted = sem("logits_shifted")
        attn_exps = sem("attn_exps")
        squares_ready = sem("squares_ready")
        norms_ready = sem("norms_ready")
        table_ready = sem("table_ready")
        route_ready = sem("route_ready")
        gathered = [sem(f"gathered{t}") for t in range(T)]

        class Ffn:

            def __init__(self, name, slots, scatters):
                self.slots = slots

                def s(what):
                    return sem(f"{name}_{what}")
                self.scattered = s("scattered")
                self.scatters = scatters
                self.x_loaded = [s(f"x_loaded{i}") for i in range(slots)]
                self.w1_loaded = [s(f"w1_loaded{i}") for i in range(slots)]
                self.w2_loaded = [s(f"w2_loaded{i}") for i in range(slots)]
                self.x_turned = s("x_turned")
                self.xT_ready = s("xT_ready")
                self.up_ready = s("up_ready")
                self.h_copied = s("h_copied")
                self.h_turned = s("h_turned")
                self.biased = s("biased")
                self.active = s("active")
                self.down_ready = s("down_ready")
                self.y_ready = s("y_ready")
                self.cur_ready = s("cur_ready")
                self.y_stored = [s(f"y_stored{i}") for i in range(slots)]
                self.y_free = s("y_free")
        ff0, ff1 = Ffn("ff0", 2, 2 * T), Ffn("ff1", SLOTS1, T)

        block = ctx.enter_context(nc.Block())

        PRODUCTS_1 = 3 * NW + 1 + 2 * T + T + T + 1
        OUT_1 = PRODUCTS_1 + 4 * T
        TURNED_0 = 4 * NW + 2
        TURNED_1 = TURNED_0 + 3 * T
        N_VEC, N_TOKW, N_ROWS = 12, 6, 11
        N_CONST = 10
        R0 = 2 * NW + 1
        N_OUT = R0 + 2 + 6 * T
        def tiles(eng, lo, hi, slots, body):
            trips = (hi - 1 - lo) // slots
            if trips:
                with eng.Fori(0, trips) as i:
                    for s in range(slots):
                        body(i * slots + lo + s, s, i + lo // slots)
            for j in range(lo + trips * slots, hi):
                body(j, j % slots, j // slots)

        @block.sync
        def _(sp):
            sp.dma_start(convw_raw, conv_w.rearrange("(h p) c i j -> p h (c i j)", p=P)).then_inc(convw_loaded, 16)

            def image_rows(wr, pr):
                r = (wr * CS + pr) * PS
                if wr:
                    sp.wait_ge(img_rows[pr], 16 * wr)
                sp.dma_start(img[:, :, r:r + PS, :], x[:, :, r:r + PS, :]).then_inc(img_rows[pr], 16)
            sp.dma_start(cls_r, class_emb.partition_broadcast(P)).then_inc(cls_loaded, 16)
            image_rows(0, 0)
            sp.dma_start(gwq_s, ga_wq.rearrange("(k p) n -> p k n", p=P)).then_inc(gwq_loaded, 16)
            for i, v in enumerate(tok_vecs):
                sp.dma_start(vec_raw[i:i + 1, :], v.rearrange("(a c) -> a c", a=1)).then_inc(vecs_loaded, 16)
            sp.dma_start(vec_raw[8:16, :], f0_ln_g).then_inc(vecs_loaded, 16)
            sp.dma_start(vec_raw[16:24, :], f0_ln_b).then_inc(vecs_loaded, 16)
            sp.dma_start(b1_raw[0:E0, :], f0_b1).then_inc(vecs_loaded, 16)
            sp.dma_start(b1_raw[E0:E0 + E1, :], f1_b1).then_inc(vecs_loaded, 16)
            image_rows(0, 1)
            for dst, src in ((wq_s, la_wq), (wkv_s, la_wkv), (proj_s, la_proj_w),
                             (gwkv_s, ga_wkv), (gproj_s, ga_proj_w), (mod_s, mod_w)):
                sp.dma_start(dst, src.rearrange("(k p) n -> p k n", p=P)).then_inc(tokw_loaded, 16)
            image_rows(0, 2)
            for dst, src in ((projb_r, la_proj_b), (gprojb_r, ga_proj_b), (modb_r, mod_b),
                             (bqkv_r[:, 0:C], a0_b[0]), (bqkv_r[:, C:2 * C], a0_b[1]), (bqkv_r[:, 2 * C:3 * C], a0_b[2]),
                             (bo_r, a0_bo), (gamma_r, a0_gamma), (beta_r, a0_beta),
                             (rb_r, f0_router_b), (bg_r, f1_bg)):
                sp.dma_start(dst, src.partition_broadcast(P)).then_inc(rows_loaded, 16)
            for pr in range(CS):
                image_rows(1, pr)
            sp.dma_start(rw_s[:, :, :], f0_router_w.rearrange("(k p) e -> p k e", p=P)).then_inc(gatew_loaded, 16)
            sp.dma_start(wg_s[:, :, :], f1_wg.rearrange("(k p) e -> p k e", p=P)).then_inc(gatew_loaded, 16)
            sp.wait_ge(consts_made, N_CONST)
            for dst in (xs0, xs1):
                n = dst.shape[0] // P
                sp.dma_start(dst.rearrange("(n p) c -> p n c", p=P), zeros[:, :].unsqueeze(1).to_broadcast([P, n, C]))\
                    .then_inc(scratch_zeroed, 16)
            sp.wait_ge(patch_packed, NW * NP)
            for i in range(3):
                sp.dma_start(a0w_s[:, :, i * C:(i + 1) * C], a0_w[i].rearrange("(k p) n -> p k n", p=P)).then_inc(a0w_loaded, 16)
            sp.dma_start(a0wo_s, a0_wo.rearrange("(k p) n -> p k n", p=P)).then_inc(a0w_loaded, 16)
            sp.wait_ge(agg_ready, NW + 1)
            sp.dma_start(a1w_s[:, :, 0:INNER], a1_wq.rearrange("(k p) n -> p k n", p=P)).then_inc(a1w_loaded, 16)
            sp.dma_start(a1w_s[:, :, INNER:3 * INNER], a1_wkv.rearrange("(k p) n -> p k n", p=P)).then_inc(a1w_loaded, 16)
            sp.dma_start(a1wo_s, a1_wo.rearrange("(k p) n -> p k n", p=P)).then_inc(a1w_loaded, 16)

            def load_x(ff, j, s, xs):
                sp.wait_ge(ff.x_turned, j + 1)
                sp.dma_start(xrow[:, s, :], xs[bass.ds(j * P, P), :]).then_inc(ff.x_loaded[s], 16)

            def load_up(ff, j, s, w1, src):
                sp.wait_ge(ff.up_ready, j + 1)
                sp.dma_start(w1, src).then_inc(ff.w1_loaded[s], 16)

            def load_down(ff, j, s, w2, src):
                sp.wait_ge(ff.down_ready, j + 1)
                sp.dma_start(w2, src).then_inc(ff.w2_loaded[s], 16)

            def load_biases(ff, j, s, biases):
                sp.wait_ge(ff.y_ready, j + 1)
                for dst, src in biases:
                    sp.dma_start(dst, src).then_inc(ff.w2_loaded[s], 16)

            def load_tiles(ff, count, weights, xs, ahead):
                n = ff.slots
                for j in range(ahead):
                    up, down, biases = weights(j, j)
                    if ff is ff1 and j == n - 1:
                        sp.wait_ge(product_ready, OUT_1)
                    up(j)
                    if ff is ff1 and j == n - 1:
                        sp.wait_ge(product_ready, OUT_1 + T)
                    down(j)
                sp.wait_ge(ff.scattered, ff.scatters * 16)
                for j in range(ahead):
                    load_x(ff, j, j, xs)
                    weights(j, j)[2](j)
                for j in range(ahead, n):
                    up, down, biases = weights(j, j)
                    load_x(ff, j, j, xs)
                    up(j)
                    down(j)
                    biases(j)
                load_x(ff, n, 0, xs)

                def body(j, s, i):
                    up, down, biases = weights(j, s)
                    up(j)
                    if not isinstance(j, int) or j + 1 < count:
                        load_x(ff, j + 1, (s + 1) % n, xs)
                    down(j)
                    biases(j)
                tiles(sp, n, count, n, body)

            sp.wait_ge(route_ready, 1)
            with sp.register("tile_expert") as expert:
                def weights0(j, s):
                    sp.reg_load(expert, eid[0:1, bass.ds(j, 1)])
                    e = sp.snap(expert, min_val=0, max_val=E0 - 1)
                    return (lambda j: load_up(ff0, j, s, w1_0[s], f0_w1[bass.ds(e, 1)].rearrange("e (k p) f -> p (e k) f", p=P)),
                            lambda j: load_down(ff0, j, s, w2_0[s], f0_w2[bass.ds(e, 1)].rearrange("e (f p) c -> p (e f) c", p=P)),
                            lambda j: load_biases(ff0, j, s,
                                                  [(b2_r[:, s, :], f0_b2[bass.ds(e, 1), :].rearrange("e c -> (e c)").partition_broadcast(P))]))
                load_tiles(ff0, NT0, weights0, xs0, 1)
            sp.wait_ge(ff0.y_ready, NT0 + ff0.slots)
            for t in range(T):
                sp.wait_ge(gathered[t], 16 * 2)
            def weights1(j, s):
                return (lambda j: load_up(ff1, j, s, w1_1[s], f1_w1[bass.ds(j * 2, 2)].rearrange("e (k p) f -> p e k f", p=P)),
                        lambda j: load_down(ff1, j, s, w2_1[s], f1_w2[bass.ds(j * 2, 2)].rearrange("e (f p) c -> p e f c", p=P)),
                        lambda j: load_biases(ff1, j, s,
                                              [(b2_r[e * SLOT:(e + 1) * SLOT, s, :],
                                              f1_b2[bass.ds(j * 2 + e, 1), :].rearrange("e c -> (e c)").partition_broadcast(SLOT))
                                             for e in range(2)]))
            load_tiles(ff1, NPAIR, weights1, xs1, ff1.slots)
            for t in range(T):
                sp.wait_ge(rows_ready, N_OUT - T + t + 1)
                sp.dma_start(out[:, t, :], hA[:, t, :]).then_inc(out_stored, 16)
            sp.wait_ge(out_stored, 16 * T)
        @block.gpsimd
        def _(pool):
            step = Steps(pool, pool_step)
            step(pool.memset(ident[:, :], 0.0))
            pool.affine_select(out=ident[:, :], in_=ident[:, :], compare_op=ALU.not_equal, fill=1.0, base=0,
                               pattern=[[-1, P]], channel_multiplier=1).then_inc(consts_made, 1)
            step(pool.memset(upper[:, :], 1.0))
            pool.affine_select(out=upper[:, :], in_=upper[:, :], compare_op=ALU.is_gt, fill=0.0, base=0,
                               pattern=[[1, P]], channel_multiplier=-1).then_inc(consts_made, 1)
            pool.memset(ones_sb[:, :], 1.0).then_inc(consts_made, 1)
            pool.memset(eps_sb[:, :], LN_EPS).then_inc(consts_made, 1)
            pool.memset(neg16[:, :], -16.0).then_inc(consts_made, 1)
            pool.memset(zeros[:, :], 0.0).then_inc(consts_made, 1)
            pool.memset(S0[:, :, :, :], -1e30).then_inc(consts_made, 1)
            pool.iota(iota_e[:, :], [[1, E1]], base=0, channel_multiplier=0,
                      allow_small_or_imprecise_dtypes=True).then_inc(consts_made, 1)
            pool.iota(iota_t[:, :], [[1, NT0 + 1]], base=0, channel_multiplier=0,
                      allow_small_or_imprecise_dtypes=True).then_inc(consts_made, 1)
            pool.iota(trash[:, :], [[P, T]], base=E1 * SLOT, channel_multiplier=1,
                      allow_small_or_imprecise_dtypes=True).then_inc(consts_made, 1)
            with pool.Fori(0, G) as wr:
                with pool.Fori(0, G) as wc:
                    w = wr * G + wc
                    for p in range(NP):
                        pr, pc = divmod(p, CS)
                        pool.wait_ge(img_rows[pr], wr * 16 + 16)
                        pool.wait_ge(patch_turned, reuse(w, p, NP))
                        src = img[:, :, bass.ds(wr * (CS * PS) + pr * PS, PS), bass.ds(wc * (CS * PS) + pc * PS, PS)]
                        pool.tensor_copy(packed[:, p % 2, :].rearrange("p (c i j) -> p c i j", c=CH, i=PS), src)\
                            .then_inc(patch_packed, 1)

            def store_tiles(ff, ys, count):
                n = ff.slots

                def store(j, s, i):
                    if not isinstance(j, int) or j:
                        pool.wait_ge(ff.y_stored[(s - 1) % n], i * 16 + (16 if s else 0))
                        pool.sem_inc(ff.y_free, 1)
                    pool.wait_ge(ff.y_ready, j + 1 + n)
                    pool.dma_start(ys[bass.ds(j * P, P), :], y_sb[:, s, :]).then_inc(ff.y_stored[s], 16)
                for j in range(n):
                    store(j, j, 0)
                tiles(pool, n, count, n, store)
                pool.wait_ge(ff.y_stored[(count - 1) % n], (count - 1) // n * 16 + 16)

            for ff in (ff0, ff1):
                pool.sem_inc(ff.y_free, ff.slots)
            pool.wait_ge(route_ready, 1)
            pool.wait_ge(scratch_zeroed, 32)
            for k in range(2):
                for t in range(T):
                    pool.indirect_dma_start(xs0, bass.IndirectOffsetOnAxis(ap=slotu[:, k, t:t + 1], axis=0),
                                            hX[:, t, :], None).then_inc(ff0.scattered, 16)
            store_tiles(ff0, ys0, NT0)
            for t in range(T):
                for k in range(2):
                    pool.indirect_dma_start(yg[:, k, t, :], None, ys0,
                                            bass.IndirectOffsetOnAxis(ap=slotu[:, k, t:t + 1], axis=0)).then_inc(gathered[t], 16)
            pool.wait_ge(route_ready, 2)
            for t in range(T):
                pool.indirect_dma_start(xs1, bass.IndirectOffsetOnAxis(ap=slotu[:, 0, t:t + 1], axis=0),
                                        hB[:, t, :], None).then_inc(ff1.scattered, 16)
            store_tiles(ff1, ys1, NPAIR)
            for t in range(T):
                pool.indirect_dma_start(yg[:, 0, t, :], None, ys1,
                                        bass.IndirectOffsetOnAxis(ap=gslotu[:, t:t + 1], axis=0)).then_inc(gathered[t], 16)

        @block.tensor
        def _(pe):
            pe.wait_ge(consts_made, N_CONST)
            pe.wait_ge(convw_loaded, 16)
            for k in range(NCH):
                kn = P if k < NCH - 1 else KT
                if k >= 2:
                    pe.wait_ge(setup_copied, k - 1)
                for h in range(KC):
                    ins = pe.transpose(bank[k % 2][0:kn, h * P:(h + 1) * P], convw_raw[:, h, k * P:k * P + kn], ident[:, :])
                ins.then_inc(setup_turned, 1)
            pe.wait_ge(setup_copied, NCH)
            for s in (patch_turned, conv_ready, kv_ready):
                pe.sem_inc(s, CREDIT)
            for ff in (ff0, ff1):
                for s in (ff.x_turned, ff.up_ready, ff.h_turned, ff.down_ready):
                    pe.sem_inc(s, ff.slots)

            def turn_patch(w, p):
                g = w * NP + p
                pe.wait_ge(patch_packed, g + 1)
                pe.wait_ge(patchT_ready, g + 1)
                for k in range(NCH - 1):
                    pe.transpose(b_top[:, k * P:(k + 1) * P], packed[:, p % 2, k * P:(k + 1) * P], ident[:, :])
                pe.transpose(b_tail[0:KT, 0:P], packed[:, p % 2, (NCH - 1) * P:KP], ident[:, :]).then_inc(patch_turned, 1)

            def project_patch(w, p):
                pe.wait_ge(patchT_ready, w * NP + p + 2)
                pe.wait_ge(conv_copied, reuse(w, p, NP))
                for k in range(NCH):
                    kn = P if k < NCH - 1 else KT
                    ins = pe.matmul(b_conv[p % 2][:, 0:C], patchT[0:kn, p % 2, k, :], convT[0:kn, k, :],
                                    start=(k == 0), stop=(k == NCH - 1))
                ins.then_inc(conv_ready, 1)

            def turn_normed(w, p):
                g = w * NP + p
                pe.wait_ge(xhat_ready, g + 2)
                pe.wait_ge(kvnT_ready, g + 1)
                for k in range(KC):
                    ins = pe.transpose(b_kvT[:, k * P:(k + 1) * P], xhat[:, p, k * P:(k + 1) * P], ident[:, :])
                ins.then_inc(kvn_turned, 1)

            def key_value(w, p):
                pe.wait_ge(kvnT_ready, w * NP + p + 2)
                pe.wait_ge(kv_copied, reuse(w, p, NP))
                for k in range(KC):
                    ins = pe.matmul(b_kv[p % 2][:, :], kvnT[:, p % 2, k, :], wkv_s[:, k, :],
                                    start=(k == 0), stop=(k == KC - 1))
                ins.then_inc(kv_ready, 1)

            def turn_vectors():
                pe.wait_ge(vecs_loaded, 16 * N_VEC)
                for k in range(KC):
                    ins = pe.transpose(bank[4][:, k * 24:(k + 1) * 24], vec_raw[0:24, k * P:(k + 1) * P], ident[0:24, 0:24])
                ins.then_inc(setup_turned, 1)
                for f in range(FC):
                    ins = pe.transpose(bank[5][:, f * 24:(f + 1) * 24], b1_raw[0:24, f * P:(f + 1) * P], ident[0:24, 0:24])
                ins.then_inc(setup_turned, 1)
                pe.wait_ge(redhat_ready, 1)
                for k in range(KC):
                    ins = pe.transpose(b_q[:, k * P:(k + 1) * P], redhat[:, k * P:(k + 1) * P], ident[:, :])
                ins.then_inc(red_turned, 1)

            def class_query():
                pe.wait_ge(redT_ready, 1)
                pe.wait_ge(gwq_loaded, 16)
                for k in range(KC):
                    ins = pe.matmul(b_q[:, C:2 * C], redT[:, k, :], gwq_s[:, k, :], start=(k == 0), stop=(k == KC - 1))
                ins.then_inc(q_ready, 1)

            def window(w, first=False, last=False):
                for p in range(NP):
                    if p + 1 < NP:
                        turn_patch(w, p + 1)
                    else:
                        if first:
                            pe.wait_ge(setup_copied, NCH + 2)
                        turn_normed(w, 0)
                    project_patch(w, p)
                    if first and p == 5:
                        turn_vectors()
                    if first and p == 6:
                        class_query()
                pe.wait_ge(tokw_loaded, 16 * N_TOKW)
                for p in range(NP):
                    if p + 1 < NP:
                        turn_normed(w, p + 1)
                    elif not last:
                        turn_patch(w + 1, 0)
                    key_value(w, p)
                    if p == 5:
                        pe.wait_ge(redhat_ready, w + 2)
                        pe.wait_ge(q_copied, w + 1)
                        for k in range(KC):
                            ins = pe.transpose(b_q[:, k * P:(k + 1) * P], redhat[:, k * P:(k + 1) * P], ident[:, :])
                        ins.then_inc(red_turned, 1)
                    if p == 6:
                        pe.wait_ge(redT_ready, w + 2)
                        for k in range(KC):
                            ins = pe.matmul(b_q[:, C:2 * C], redT[:, k, :], wq_s[:, k, :],
                                            start=(k == 0), stop=(k == KC - 1))
                        ins.then_inc(q_ready, 1)
            turn_patch(0, 0)
            window(0, first=True)
            with pe.Fori(1, NW - 1) as w:
                window(w)
            window(NW - 1, last=True)
            pe.wait_ge(kv_copied, NW * NP + CREDIT)
            pe.wait_ge(q_copied, NW + 1)

            n_turn, n_mm = [0], [0]

            def turn_rows(src, chunks=KC):
                n = n_turn[0]
                n_turn[0] += 1
                if n >= 2:
                    pe.wait_ge(turned_copied, n - 1)
                for k in range(chunks):
                    ins = pe.transpose(b_turn[n % 2][:, k * P:(k + 1) * P], src[:, k * P:(k + 1) * P], ident[:, :])
                ins.then_inc(turned, 1)

            def project(xt, t, w_s, lo, hi, copied, chunks=KC):
                n = n_mm[0]
                n_mm[0] += 1
                pe.wait_ge(turned_copied, copied)
                if n >= 4:
                    pe.wait_ge(product_read, n - 3)
                for k in range(chunks):
                    ins = pe.matmul(b_mm[n % 4][:, 0:hi - lo], xt[:, k, t * P:(t + 1) * P], w_s[:, k, lo:hi],
                                    start=(k == 0), stop=(k == chunks - 1))
                ins.then_inc(product_ready, 1)

            def sum_turned(parts, chunks):
                m = n_turn[0]
                n_turn[0] += 1
                pe.wait_ge(turned_copied, m - 1)
                for k in range(chunks):
                    for i, part in enumerate(parts):
                        ins = pe.matmul(b_turn[m % 2][:, k * P:(k + 1) * P], part[:, k * P:(k + 1) * P], ident[:, :],
                                        start=(i == 0), stop=(i == len(parts) - 1))
                ins.then_inc(turned, 1)

            pe.wait_ge(agg_ready, NW + 1)
            for n in range(NW):
                turn_rows(agg[:, n, :])
            for n in range(NW):
                project(XT, n, proj_s, 0, C, n + 1)
            for n in range(NW):
                pe.wait_ge(rows_ready, n + 1)
                turn_rows(local[:, n, :])
            for n in range(NW):
                project(XT2, n, mod_s, 0, C, NW + n + 1)
            for n in range(NW):
                pe.wait_ge(rows_ready, NW + n + 1)
                turn_rows(lhat[:, n, :])
            for n in range(NW):
                project(XT, n, gwkv_s, 0, 2 * C, 2 * NW + n + 1)
            n = 3 * NW
            pe.wait_ge(product_read, 2 * NW)
            for t in range(NW):
                turn_rows(hA[:, t, :])
            pe.wait_ge(a0w_loaded, 64)
            for t in range(2):
                project(XT2, t, a0w_s, 0, 2 * C, n + t + 1)
                project(XT2, t, a0w_s, 2 * C, 3 * C, n + t + 1)
            pe.wait_ge(rows_ready, 2 * NW + 1)
            turn_rows(gagg)
            project(XT, 0, gproj_s, 0, C, n + NW + 1)
            for t in range(2, NW):
                project(XT2, t, a0w_s, 0, 2 * C, n + t + 1)
                project(XT2, t, a0w_s, 2 * C, 3 * C, n + t + 1)
            pe.wait_ge(product_read, 3 * NW + 5)
            turn_rows(hA[:, NW, :])
            n += NW + 2
            project(XT2, NW, a0w_s, 0, 2 * C, n)
            project(XT2, NW, a0w_s, 2 * C, 3 * C, n)
            assert n_turn[0] == TURNED_0
            for t in range(T):
                pe.wait_ge(rows_ready, R0 + t + 1)
                sum_turned([weighted0[t % 3][:, i, :] for i in range(t + 1)], KC)
                if t >= 1:
                    project(XT, t - 1, a0wo_s, 0, C, n + t)
            project(XT, T - 1, a0wo_s, 0, C, n + T)
            n += T

            def rank(rhs_own, rhs_all, width, totals=None):
                m = n_mm[0]
                n_mm[0] += 1
                pe.wait_ge(product_read, m - 3)
                b = b_mm[m % 4]
                ins = pe.matmul(b[:, 0:width], upper[:, :], rhs_own, start=True, stop=rhs_all is None)
                if rhs_all is not None:
                    ins = pe.matmul(b[:, 0:width], ones_sb[:, :], rhs_all, start=False, stop=True)
                if totals is not None:
                    for i, r in enumerate(totals):
                        ins = pe.matmul(b[:, 256:256 + E0], ones_sb[:, :], r, start=(i == 0), stop=(i == len(totals) - 1))
                ins.then_inc(product_ready, 1)

            def turn_x(ff, j, s, i):
                pe.wait_ge(ff.x_loaded[s], i * 16 + 16)
                pe.wait_ge(ff.xT_ready, j + ff.slots)
                for k in range(KC):
                    ins = pe.transpose(b_x[:, k * P:(k + 1) * P], xrow[:, s, k * P:(k + 1) * P], ident[:, :])
                ins.then_inc(ff.x_turned, 1)

            def turn_h(ff, j):
                pe.wait_ge(ff.h_copied, j + 1 + ff.slots)
                pe.wait_ge(ff.biased, j + ff.slots)
                for f in range(FC):
                    ins = pe.transpose(b_hT[f // 4][:, f % 4 * P:(f % 4 + 1) * P], h_sb[:, f * P:(f + 1) * P], ident[:, :])
                ins.then_inc(ff.h_turned, 1)

            def before_up(ff, j, s, i):
                pe.wait_ge(ff.xT_ready, j + 1 + ff.slots)
                pe.wait_ge(ff.w1_loaded[s], i * 16 + 16)
                pe.wait_ge(ff.h_copied, j + ff.slots)

            def before_down(ff, j, s, i, loads):
                pe.wait_ge(ff.active, j + 1 + ff.slots)
                pe.wait_ge(ff.w2_loaded[s], i * (16 * loads) + 16 * loads)
                pe.wait_ge(ff.y_ready, j + ff.slots)

            def up0(j, s, i):
                before_up(ff0, j, s, i)
                for n in range(2):
                    for k in range(KC):
                        ins = pe.matmul(b_h[n][:, :], xTs[:, s, k, :], w1_0[s][:, k, n * 512:(n + 1) * 512],
                                        start=(k == 0), stop=(k == KC - 1))
                ins.then_inc(ff0.up_ready, 1)

            def down0(j, s, i):
                before_down(ff0, j, s, i, 2)
                for f in range(FC):
                    ins = pe.matmul(b_y[:, 0:C], hTs[:, f, :], w2_0[s][:, f, :], start=(f == 0), stop=(f == FC - 1))
                ins.then_inc(ff0.down_ready, 1)

            def up1(j, s, i):
                before_up(ff1, j, s, i)
                for n in range(2):
                    for k in range(KC):
                        for e in range(2):
                            own = slice(e * SLOT, (e + 1) * SLOT)
                            ins = pe.matmul(b_h[n][own, :], xTs[:, s, k, own], w1_1[s][:, e, k, n * 512:(n + 1) * 512],
                                            start=(k == 0), stop=(k == KC - 1))
                ins.then_inc(ff1.up_ready, 1)

            def down1(j, s, i):
                before_down(ff1, j, s, i, 3)
                for f in range(FC):
                    for e in range(2):
                        own = slice(e * SLOT, (e + 1) * SLOT)
                        ins = pe.matmul(b_y[own, 0:C], hTs[:, f, own], w2_1[s][:, e, f, :], start=(f == 0), stop=(f == FC - 1))
                ins.then_inc(ff1.down_ready, 1)

            def expert_tiles(ff, count, up, down):
                n = ff.slots
                turn_x(ff, 0, 0, 0)
                up(0, 0, 0)
                turn_x(ff, 1, 1, 0)
                turn_h(ff, 0)

                def body(j, s, i, left=3):
                    if left > 1:
                        up(j + 1, (s + 1) % n, i + (s + 1) // n)
                    if left > 2:
                        turn_x(ff, j + 2, (s + 2) % n, i + (s + 2) // n)
                    down(j, s, i)
                    if left > 1:
                        turn_h(ff, j + 1)
                trips = (count - 2) // n
                with pe.Fori(0, trips) as i:
                    for s in range(n):
                        body(i * n + s, s, i)
                for j in range(n * trips, count):
                    body(j, j % n, j // n, count - j)

            for t in range(T):
                pe.wait_ge(rows_ready, R0 + T + t + 1)
                turn_rows(hB[:, t, :])
            pe.wait_ge(gatew_loaded, 32)
            for t in range(T):
                project(XT2, t, rw_s, 0, E0, n + t + 1)
            n += T
            pe.wait_ge(rows_ready, R0 + 2 * T + 1)
            rank(msum[:, :, 0:E0], mcum[:, :, 0:E0], T * E0, (mcum[:, T - 1, 0:E0], msum[:, T - 1, 0:E0]))
            pe.wait_ge(product_read, n_mm[0])
            pe.wait_ge(turned_copied, n_turn[0])
            expert_tiles(ff0, NT0, up0, down0)
            pe.wait_ge(ff0.y_ready, NT0 + ff0.slots)
            pe.wait_ge(rows_ready, R0 + 1 + 2 * T + 1)
            turn_rows(hA[:, 0, :])
            pe.wait_ge(a1w_loaded, 48)
            for t in range(T):
                if t + 1 < T:
                    pe.wait_ge(rows_ready, R0 + 1 + 2 * T + t + 2)
                    turn_rows(hA[:, t + 1, :])
                for i in range(2):
                    project(XT, t, a1w_s, i * INNER, (i + 1) * INNER, n + t + 1)
            for t in range(T):
                project(XT, t, a1w_s, 2 * INNER, 3 * INNER, n + t + 1)
            n += T
            assert n_turn[0] == TURNED_1

            for t in range(T):
                pe.wait_ge(rows_ready, R0 + 1 + 3 * T + t + 1)
                sum_turned([weighted1[t % 3][:, i, :] for i in (0, 1, 4)], KI)
                if t >= 1:
                    project(OT, t - 1, a1wo_s, 0, C, n + t, KI)
            project(OT, T - 1, a1wo_s, 0, C, n + T, KI)
            n += T
            for t in range(T):
                pe.wait_ge(rows_ready, R0 + 1 + 4 * T + t + 1)
                turn_rows(hB[:, t, :])
            for t in range(T):
                project(XT, t, wg_s, 0, E1, n + t + 1)
            n += T
            pe.wait_ge(rows_ready, R0 + 1 + 5 * T + 1)
            rank(msum[:, 0, :], None, E1)
            pe.wait_ge(product_read, n_mm[0])
            pe.wait_ge(turned_copied, n_turn[0])
            expert_tiles(ff1, NPAIR, up1, down1)

        @block.scalar
        def _(act):
            step = Steps(act, act_step)
            for k in range(NCH):
                kn = P if k < NCH - 1 else KT
                act.wait_ge(setup_turned, k + 1)
                act.activation(convT[0:kn, k, :], bank[k % 2][0:kn, 0:C], ACT.Copy).then_inc(setup_copied, 1)
            act.wait_ge(setup_copied, NCH)
            for s in (conv_copied, kv_copied):
                act.sem_inc(s, CREDIT)
            for s in (patchT_ready, kvnT_ready):
                act.sem_inc(s, 1)
            for ff in (ff0, ff1):
                for s in (ff.xT_ready, ff.h_copied, ff.active):
                    act.sem_inc(s, ff.slots)

            def vec(v, k):
                return vecT[:, k, v:v + 1]

            def std(lo, hi, n):
                act.wait_ge(var_ready, n)
                act.activation(sd[:, lo:hi], mv[:, lo:hi, 1], ACT.Sqrt, bias=eps_sb[:, 0:1]).then_inc(std_ready, 1)

            def affine_turned(dst, src, g, b):
                for k in range(KC):
                    ins = act.activation(dst[:, k, :], src[:, k * P:(k + 1) * P], ACT.Identity,
                                         scale=vec(g, k), bias=vec(b, k))
                return ins

            std(0, 1, 1)

            def vectors_copied():
                act.wait_ge(setup_turned, NCH + 1)
                act.activation(vecT[:, :, :].rearrange("p k v -> p (k v)"), bank[4][:, 0:KC * 24], ACT.Copy).then_inc(setup_copied, 1)
                act.wait_ge(setup_turned, NCH + 2)
                act.activation(b1T[:, :, :].rearrange("p k v -> p (k v)"), bank[5][:, 0:FC * 24], ACT.Copy).then_inc(setup_copied, 1)
                act.wait_ge(setup_copied, NCH + 2)
                act.wait_ge(red_turned, 1)
                affine_turned(redT, b_q, 4, 5).then_inc(redT_ready, 1)

            def class_query_copied():
                act.wait_ge(q_ready, 1)
                act.activation(gq_sb[:, :], b_q[:, C:2 * C], ACT.Copy, scale=SCALE).then_inc(q_copied, 1)

            def patch_copied(w, p):
                act.wait_ge(patch_turned, w * NP + p + 1 + CREDIT)
                act.wait_ge(conv_ready, reuse(w, p, NP))
                act.activation(patchT[:, p % 2, 0:NCH - 1, :].rearrange("p k n -> p (k n)"), b_top[:, :], ACT.Copy)
                act.activation(patchT[0:KT, p % 2, NCH - 1, :], b_tail[0:KT, 0:P], ACT.Copy).then_inc(patchT_ready, 1)

            def raw_copied(w, p):
                act.wait_ge(conv_ready, w * NP + p + 1 + CREDIT)
                act.wait_ge(xhat_ready, w * NP + 1)
                act.activation(pe_raw[:, p, :], b_conv[p % 2][:, 0:C], ACT.Copy).then_inc(conv_copied, 1)

            def normed_copied(w, p):
                act.wait_ge(kvn_turned, w * NP + p + 1)
                act.wait_ge(kv_ready, reuse(w, p, NP))
                affine_turned(kvnT[:, p % 2], b_kvT, 2, 3).then_inc(kvnT_ready, 1)

            def kv_stored(w, p):
                act.wait_ge(kv_ready, w * NP + p + 1 + CREDIT)
                act.wait_ge(agg_ready, w + 1)
                act.activation(kvw[:, p, :], b_kv[p % 2][:, :], ACT.Copy).then_inc(kv_copied, 1)

            def window_exps(w):
                act.wait_ge(scores_shifted, w + 1)
                act.activation(ex[:, :, :], sc[:, :, :], ACT.Exp).then_inc(exps_ready, 1)

            def window(w, first=False, last=False):
                for p in range(NP):
                    if p + 1 < NP:
                        patch_copied(w, p + 1)
                    else:
                        normed_copied(w, 0)
                    raw_copied(w, p)
                    if p == 1 and not first:
                        window_exps(w - 1)
                    if p == 5 and first:
                        vectors_copied()
                    if p == 6 and first:
                        class_query_copied()
                    if p in (3, 6):
                        std(p - 3, p, w * 4 + p // 3 + 1)
                for p in range(NP):
                    if p + 1 < NP:
                        normed_copied(w, p + 1)
                    elif not last:
                        patch_copied(w + 1, 0)
                    if p == 0:
                        std(6, 9, w * 4 + 4)
                    kv_stored(w, p)
                    if p == 3:
                        std(0, 1, w * 4 + 5)
                    if p == 5:
                        act.wait_ge(red_turned, w + 2)
                        affine_turned(redT, b_q, 0, 1).then_inc(redT_ready, 1)
                    if p == 6:
                        act.wait_ge(q_ready, w + 2)
                        act.wait_ge(agg_ready, w + 1)
                        act.activation(q_sb, b_q[:, C:2 * C], ACT.Copy, scale=SCALE).then_inc(q_copied, 1)
            patch_copied(0, 0)
            window(0, first=True)
            with act.Fori(1, NW - 1) as w:
                window(w)
            window(NW - 1, last=True)
            window_exps(NW - 1)

            n_turn = [0]

            def rows_turned(dst, t, g=None, b=None, chunks=KC):
                n = n_turn[0]
                n_turn[0] += 1
                act.wait_ge(turned, n + 1)
                d = dst[:, :, t * P:(t + 1) * P]
                if g is None:
                    act.activation(d, b_turn[n % 2][:, 0:chunks * P].rearrange("p (k n) -> p k n", k=chunks), ACT.Copy)\
                        .then_inc(turned_copied, 1)
                else:
                    affine_turned(d, b_turn[n % 2], g, b).then_inc(turned_copied, 1)

            for n in range(NW):
                rows_turned(XT, n)
            for n in range(NW):
                rows_turned(XT2, n)
            std(0, NW, NW * 4 + 2)
            act.wait_ge(product_ready, NW)
            for n in range(NW):
                rows_turned(XT, n, 6, 7)
            act.wait_ge(scores_shifted, NW + 1)
            act.activation(ex[:, 0:NW, :], sc[:, 0:NW, :], ACT.Exp).then_inc(exps_ready, 1)
            act.wait_ge(product_ready, 3 * NW)
            for t in range(NW):
                rows_turned(XT2, t)
            rows_turned(XT, 0)
            rows_turned(XT2, NW)
            act.wait_ge(logits_shifted, 1)
            act.activation(S0[:, :, :, :], S0[:, :, :, :], ACT.Exp, scale=float(D0) ** -0.5).then_inc(attn_exps, 1)
            act.wait_ge(product_ready, 3 * NW + 5)
            for t in range(T):
                rows_turned(XT, t)
            for i in range(2):
                std(0, T, 4 * NW + 3 + i)
            act.wait_ge(product_ready, 3 * NW + 1 + 2 * T)
            for t in range(T):
                rows_turned(XT2, t)
            std(0, T, 4 * NW + 5)
            act.wait_ge(logits_shifted, 2)
            act.activation(gate[:, 1, :], gate[:, 0, :], ACT.Exp).then_inc(attn_exps, 1)

            def x_copied(ff, j, s, affine):
                act.wait_ge(ff.x_turned, j + 1 + ff.slots)
                act.wait_ge(ff.up_ready, j + 1)
                if affine:
                    act.wait_ge(ff.cur_ready, j + 1 + ff.slots)
                    for k in range(KC):
                        ins = act.activation(xTs[:, s, k, :], b_x[:, k * P:(k + 1) * P], ACT.Identity,
                                             scale=cur[:, s, k:k + 1], bias=cur[:, s, KC + k:KC + k + 1])
                else:
                    ins = act.activation(xTs[:, s, :, :].rearrange("p k n -> p (k n)"), b_x[:, 0:C], ACT.Copy)
                ins.then_inc(ff.xT_ready, 1)

            def h_stored(ff, j):
                act.wait_ge(ff.up_ready, j + 1 + ff.slots)
                act.wait_ge(ff.h_turned, j + ff.slots)
                for n in range(2):
                    ins = act.activation(h_sb[:, n * 512:(n + 1) * 512], b_h[n][:, :], ACT.Copy)
                ins.then_inc(ff.h_copied, 1)

            def activated(ff, j, func):
                act.wait_ge(ff.biased, j + 1 + ff.slots)
                act.wait_ge(ff.down_ready, j + ff.slots)
                act.activation(hTs.rearrange("p f n -> p (f n)"), hb, func).then_inc(ff.active, 1)

            def expert_tiles(ff, count, affine, func):
                n = ff.slots
                x_copied(ff, 0, 0, affine)
                h_stored(ff, 0)
                x_copied(ff, 1, 1, affine)
                activated(ff, 0, func)

                def body(j, s, left=3):
                    h_stored(ff, j + 1)
                    if left > 2:
                        x_copied(ff, j + 2, (s + 2) % n, affine)
                    activated(ff, j + 1, func)
                trips = (count - 2) // n
                with act.Fori(0, trips) as i:
                    for s in range(n):
                        body(i * n + s, s)
                for j in range(n * trips, count - 1):
                    body(j, j % n, count - j)

            expert_tiles(ff0, NT0, True, ACT.Gelu)
            n_std, n_mm = 4 * NW + 6, [PRODUCTS_1]

            def product_copied(dst):
                n = n_mm[0]
                n_mm[0] += 1
                act.wait_ge(product_ready, n + 1)
                act.activation(dst, b_mm[n % 4][:, :], ACT.Copy).then_inc(product_read, 1)
            std(0, 1, n_std)
            std(1, 2, n_std + 1)
            rows_turned(XT, 0)

            def squared(t):
                for h in range(2 * H1):
                    own = slice(h * D1, (h + 1) * D1)
                    ins = act.activation(squares[:, own], qkv1[:, t, own], ACT.Square, accum_out=ssq[:, t, h:h + 1])
                return ins
            for t in range(T):
                if t == 0:
                    std(2, 3, n_std + 2)
                if t + 1 < T:
                    rows_turned(XT, t + 1)
                if t == 1:
                    for i in range(3, T):
                        std(i, i + 1, n_std + i)
                for i in range(2):
                    product_copied(qkv1[:, t, i * INNER:(i + 1) * INNER])
                act.wait_ge(product_read, n_mm[0])
                if t >= 2:
                    squared(t - 2)
            for t in range(T):
                product_copied(qkv1[:, t, 2 * INNER:3 * INNER])
            step(squared(T - 2))
            squared(T - 1).then_inc(squares_ready, 1)
            act.wait_ge(squares_ready, 1)
            act.activation(rnorm[:, :, :], ssq[:, :, :], ACT.Sqrt).then_inc(norms_ready, 1)
            act.wait_ge(logits_shifted, 3)
            act.activation(S1[:, :, :, :], S1[:, :, :, :], ACT.Exp, scale=16.0, bias=neg16[:, 0:1]).then_inc(attn_exps, 1)
            for t in range(T):
                rows_turned(OT, t, chunks=KI)
            std(0, T, n_std + T)
            act.wait_ge(product_ready, n_mm[0] + T)
            for t in range(T):
                rows_turned(XT, t)
            act.wait_ge(logits_shifted, 4)
            act.activation(lg2[:, :, :], lg[:, :, :], ACT.Exp).then_inc(attn_exps, 1)
            expert_tiles(ff1, NPAIR, False, ACT.Relu)
            for t in range(T):
                std(t, t + 1, n_std + T + 1 + t)

        @block.vector
        def _(dve):
            step = Steps(dve, dve_step)

            def rstd(lo, hi, n):
                dve.wait_ge(std_ready, n)
                step(dve.reciprocal(rs[:, lo:hi], sd[:, lo:hi]))

            def normed(dst, src, i):
                return dve.tensor_scalar(dst, src, mv[:, i, 0:1], rs[:, i:i + 1], ALU.subtract, ALU.mult)

            dve.wait_ge(cls_loaded, 16)
            dve.wait_ge(consts_made, N_CONST)
            step(dve.bn_stats(stats[:, 0, :], cls_r))
            dve.bn_aggr(mv[:, 0, :], stats[:, 0, :]).then_inc(var_ready, 1)
            rstd(0, 1, 1)
            normed(redhat, cls_r, 0).then_inc(redhat_ready, 1)
            dve.sem_inc(xhat_ready, 1)
            dve.sem_inc(agg_ready, 1)
            for ff in (ff0, ff1):
                for s in (ff.cur_ready, ff.biased, ff.y_ready):
                    dve.sem_inc(s, ff.slots)

            def finish(lo, w):
                rstd(lo, lo + 3, w * 4 + lo // 3 + 2)
                for p in range(lo, lo + 3):
                    normed(xhat[:, p, :], pe_raw[:, p, :], p).then_inc(xhat_ready, 1)

            WEIGH_STEPS = 4

            def weigh_values(w):
                dve.wait_ge(exps_ready, w + 1)
                step(dve.tensor_reduce(hx[:, 1, :], ex[:, :, :].rearrange("p n h -> p h n"), AX.X, ALU.add))
                step(dve.reciprocal(hx[:, 2, :], hx[:, 1, :]))
                step(dve.tensor_tensor(ex[:, :, :], ex[:, :, :], hx[:, 2, :].unsqueeze(1).to_broadcast([P, NP, H8]), ALU.mult))
                vals = kvw[:, :, C:2 * C]
                step(dve.tensor_tensor(vals.rearrange("p n (h d) -> p n h d", h=H8), vals.rearrange("p n (h d) -> p n h d", h=H8),
                                       ex[:, :, :].unsqueeze(3).to_broadcast([P, NP, H8, DH]), ALU.mult))

            def sum_values(w):
                vals = kvw[:, :, C:2 * C]
                dve.tensor_reduce(agg[:, bass.ds(w, 1), :].rearrange("p a c -> p (a c)"), vals.rearrange("p n c -> p c n"),
                                  AX.X, ALU.add).then_inc(agg_ready, 1)

            def window(w, first=False):
                for p in range(NP):
                    dve.wait_ge(conv_copied, w * NP + p + 1 + CREDIT)
                    ins = dve.bn_stats(stats[:, p, :], pe_raw[:, p, :])
                    if p % 3 == 2:
                        step(ins)
                    if p in (5, 8):
                        finish(p - 5, w)
                    if p in (3, 5, 8):
                        batch = {3: 0, 5: 3, 8: 6}[p]
                        for i in range(batch, batch + 3):
                            ins = dve.bn_aggr(mv[:, i, :], stats[:, i, :])
                        ins.then_inc(var_ready, 1)
                    if not first and p == 1:
                        weigh_values(w - 1)
                    if not first and p == 3:
                        sum_values(w - 1)
                step(dve.tensor_reduce(redhat, pe_raw.rearrange("p n c -> p c n"), AX.X, ALU.add))
                finish(6, w)
                step(dve.tensor_scalar(red, redhat, 1.0 / NP, None, ALU.mult))
                dve.wait_ge(rows_loaded, 16 * N_ROWS)
                step(dve.bn_stats(stats[:, 0, :], red))
                dve.tensor_tensor(redb[:, bass.ds(w, 1), :].rearrange("p a c -> p (a c)"), red, projb_r, ALU.add)
                dve.bn_aggr(mv[:, 0, :], stats[:, 0, :]).then_inc(var_ready, 1)
                rstd(0, 1, w * 4 + 5)
                normed(redhat, red, 0).then_inc(redhat_ready, 1)
                dve.wait_ge(q_copied, w + 2)
                for r in range(3):
                    dve.wait_ge(kv_copied, w * NP + 3 * r + 3 + CREDIT)
                    keys = kvw[:, 3 * r:3 * r + 3, 0:C]
                    step(dve.tensor_tensor(keys, keys, q_sb.unsqueeze(1).to_broadcast([P, 3, C]), ALU.mult))
                    step(dve.tensor_reduce(sc[:, 3 * r:3 * r + 3, :],
                                           keys.rearrange("p n (h d) -> p n h d", h=H8), AX.X, ALU.add))
                step(dve.tensor_reduce(hx[:, 0, :], sc[:, :, :].rearrange("p n h -> p h n"), AX.X, ALU.max))
                dve.tensor_tensor(sc[:, :, :], sc[:, :, :], hx[:, 0, :].unsqueeze(1).to_broadcast([P, NP, H8]),
                                  ALU.subtract).then_inc(scores_shifted, 1)

            before = step.n
            window(0, first=True)
            base, per = step.n, step.n - before + WEIGH_STEPS
            with dve.Fori(1, NW) as w:
                step.loop(base, w - 1, per)
                window(w)
            step.loop(base, NW - 1, per)
            weigh_values(NW - 1)
            sum_values(NW - 1)

            n_mm = [0]

            def product():
                n = n_mm[0]
                n_mm[0] += 1
                dve.wait_ge(product_ready, n + 1)
                return b_mm[n % 4]

            for n in range(NW):
                b = product()
                dve.tensor_tensor(local[:, n, :], b[:, 0:C], redb[:, n, :], ALU.add).then_inc(product_read, 1)
                dve.wait_ge(product_read, n + 1)
                dve.bn_stats(stats[:, n, :], local[:, n, :]).then_inc(rows_ready, 1)
            dve.wait_ge(rows_ready, NW)
            for n in range(NW):
                ins = dve.bn_aggr(mv[:, n, :], stats[:, n, :])
            ins.then_inc(var_ready, 1)
            for n in range(NW):
                b = product()
                dve.tensor_tensor(hA[:, n, :], b[:, 0:C], modb_r, ALU.add).then_inc(product_read, 1)
            rstd(0, NW, NW * 4 + 2)
            for n in range(NW):
                normed(lhat[:, n, :], local[:, n, :], n).then_inc(rows_ready, 1)
            for n in range(NW):
                b = product()
                dve.tensor_copy(gkv[:, n, :], b[:, :]).then_inc(product_read, 1)
            dve.wait_ge(product_read, 3 * NW)
            step(dve.tensor_tensor(gprod, gkv[:, :, 0:C], gq_sb[:, :].unsqueeze(1).to_broadcast([P, NW, C]), ALU.mult))
            step(dve.tensor_reduce(sc[:, 0:NW, :], gprod.rearrange("p n (h d) -> p n h d", h=H8), AX.X, ALU.add))
            step(dve.tensor_reduce(hx[:, 0, :], sc[:, 0:NW, :].rearrange("p n h -> p h n"), AX.X, ALU.max))
            dve.tensor_tensor(sc[:, 0:NW, :], sc[:, 0:NW, :], hx[:, 0, :].unsqueeze(1).to_broadcast([P, NW, H8]),
                              ALU.subtract).then_inc(scores_shifted, 1)
            dve.wait_ge(exps_ready, NW + 1)
            step(dve.tensor_reduce(hx[:, 1, :], ex[:, 0:NW, :].rearrange("p n h -> p h n"), AX.X, ALU.add))
            step(dve.reciprocal(hx[:, 2, :], hx[:, 1, :]))
            step(dve.tensor_tensor(ex[:, 0:NW, :], ex[:, 0:NW, :], hx[:, 2, :].unsqueeze(1).to_broadcast([P, NW, H8]), ALU.mult))
            step(dve.tensor_tensor(gprod.rearrange("p n (h d) -> p n h d", h=H8),
                                   gkv[:, :, C:2 * C].rearrange("p n (h d) -> p n h d", h=H8),
                                   ex[:, 0:NW, :].unsqueeze(3).to_broadcast([P, NW, H8, DH]), ALU.mult))
            dve.tensor_reduce(gagg, gprod.rearrange("p n c -> p c n"), AX.X, ALU.add).then_inc(rows_ready, 1)
            dve.wait_ge(rows_ready, 2 * NW + 1)
            step(dve.tensor_tensor(gprod[:, 0, :], cls_r, gprojb_r, ALU.add))

            def read_product(dst, row_):
                b = product()
                width = dst.free_size()
                if row_ is None:
                    dve.tensor_copy(dst, b[:, 0:width]).then_inc(product_read, 1)
                else:
                    dve.tensor_tensor(dst, b[:, 0:width], row_, ALU.add).then_inc(product_read, 1)

            def qkv_read(t):
                read_product(qkv0[:, t, 0:2 * C], bqkv_r[:, 0:2 * C])
                read_product(qkv0[:, t, 2 * C:3 * C], bqkv_r[:, 2 * C:3 * C])

            def spread(a, n, where):
                shape = list(a.shape)
                shape.insert(where, n)
                return a.unsqueeze(where).to_broadcast(shape)

            def scores0(t):
                dve.wait_ge(product_read, n_mm[0])
                pr = prod0[:, 0:t + 1, :]
                step(dve.tensor_tensor(pr, qkv0[:, 0:t + 1, C:2 * C], spread(qkv0[:, t, 0:C], t + 1, 1), ALU.mult))
                step(dve.tensor_reduce(S0[:, t, :, 0:t + 1].rearrange("p h s -> p s h"),
                                       pr.rearrange("p s (h d) -> p s h d", h=H0), AX.X, ALU.add))
            qkv_read(0)
            qkv_read(1)
            b = product()
            dve.tensor_tensor(hA[:, NW, :], b[:, 0:C], gprod[:, 0, :], ALU.add).then_inc(product_read, 1)
            for t in range(T):
                if t == T - 1:
                    dve.wait_ge(product_read, n_mm[0])
                    dve.tensor_tensor(residual, hA, spread(beta_r, T, 1), ALU.add)
                if t >= 2:
                    qkv_read(t)
                scores0(t)
            flat0 = S0[:, :, :, :].rearrange("p t h s -> p (t h) s")
            step(dve.tensor_reduce(hs[:, 0, :], flat0, AX.X, ALU.max))
            dve.tensor_tensor(flat0, flat0, spread(hs[:, 0, :], T, 2), ALU.subtract).then_inc(logits_shifted, 1)
            dve.wait_ge(attn_exps, 1)
            step(dve.tensor_reduce(hs[:, 1, :], flat0, AX.X, ALU.add))
            step(dve.reciprocal(hs[:, 2, :], hs[:, 1, :]))
            step(dve.tensor_tensor(flat0, flat0, spread(hs[:, 2, :], T, 2), ALU.mult))
            for t in range(T):
                if t >= 3:
                    dve.wait_ge(turned, TURNED_0 + t - 2)
                dve.tensor_tensor(weighted0[t % 3][:, 0:t + 1, :].rearrange("p s (h d) -> p s h d", h=H0),
                                  qkv0[:, 0:t + 1, 2 * C:3 * C].rearrange("p s (h d) -> p s h d", h=H0),
                                  spread(S0[:, t, :, 0:t + 1].rearrange("p h s -> p s h"), D0, 3), ALU.mult)\
                    .then_inc(rows_ready, 1)

            n_std = [NW * 4 + 2]

            def row_stats(src):
                for t in range(T):
                    ins = dve.bn_stats(stats[:, t, :], src[:, t, :])
                step(ins)
                for t in range(T):
                    ins = dve.bn_aggr(mv[:, t, :], stats[:, t, :])
                ins.then_inc(var_ready, 1)
                n_std[0] += 1
                rstd(0, T, n_std[0])

            for t in range(T):
                read_product(yln[:, t, :], bo_r)
            dve.wait_ge(product_read, n_mm[0])
            row_stats(yln)
            for t in range(T):
                ins = dve.scalar_tensor_tensor(yln[:, t, :], yln[:, t, :], mv[:, t, 0:1], gamma_r, ALU.subtract, ALU.mult)
            step(ins)
            for t in range(T):
                ins = dve.scalar_tensor_tensor(yln[:, t, :], yln[:, t, :], rs[:, t:t + 1], residual[:, t, :], ALU.mult, ALU.add)
            step(ins)
            row_stats(yln)
            for t in range(T):
                normed(hB[:, t, :], yln[:, t, :], t).then_inc(rows_ready, 1)
            dve.wait_ge(rows_ready, R0 + 2 * T)
            row_stats(hB)
            for t in range(T):
                ins = normed(hX[:, t, :], hB[:, t, :], t)
            step(ins)
            for t in range(T):
                read_product(lg[:, t, 0:E0], rb_r)
            dve.wait_ge(product_read, n_mm[0])
            for t in range(T):
                ins = dve.max(best[:, t, :], lg[:, t, 0:E0])
            step(ins)
            for t in range(T):
                ins = dve.max_index(besti[:, t, :], best[:, t, :], lg[:, t, 0:E0])
            step(ins)
            dve.tensor_tensor(gate[:, 0, :], best[:, :, 1], best[:, :, 0], ALU.subtract).then_inc(logits_shifted, 1)
            step(dve.tensor_copy(bestf[:, :, :], besti[:, :, 0:2]))
            for k in range(2):
                step(dve.tensor_tensor(oh[:, k, :, 0:E0], spread(iota_e[:, 0:E0], T, 1),
                                       spread(bestf[:, :, k], E0, 2), ALU.is_equal))
            step(dve.tensor_tensor(msum[:, :, 0:E0], oh[:, 0, :, 0:E0], oh[:, 1, :, 0:E0], ALU.add))

            def tiles_before(width):
                step(dve.memset(mcum[:, 0, 0:width], 0.0))
                for t in range(1, T):
                    step(dve.tensor_tensor(mcum[:, t, 0:width], mcum[:, t - 1, 0:width],
                                           (msum if width == E0 else oh[:, 0])[:, t - 1, 0:width], ALU.add))
            tiles_before(E0)
            dve.sem_inc(rows_ready, 1)
            b = product()
            ins = dve.tensor_copy(cnt[:, :], b[:, 256:256 + E0])
            step(ins)
            dve.tensor_copy(rk[:, :, 0:E0], b[:, 0:T * E0].rearrange("p (t e) -> p t e", t=T)).then_inc(product_read, 1)
            step(dve.tensor_scalar(ntile[:, :], cnt[:, :], 0.0, None, ALU.is_gt))
            for i in range(1, T):
                step(dve.scalar_tensor_tensor(ntile[:, :], cnt[:, :], float(i * P), ntile[:, :], ALU.is_gt, ALU.add))
            step(dve.tensor_tensor_scan(incl[:, :], ones_sb[:, 0:E0], ntile[:, :], 0.0, ALU.mult, ALU.add))
            step(dve.tensor_tensor(basee[:, :], incl[:, :], ntile[:, :], ALU.subtract))
            step(dve.tensor_scalar(basee[:, :], basee[:, :], float(P), None, ALU.mult))
            dve.wait_ge(product_read, n_mm[0])
            step(dve.tensor_tensor(rk[:, :, 0:E0], rk[:, :, 0:E0], spread(basee[:, :], T, 1), ALU.add))
            for k in range(2):
                step(dve.tensor_tensor(oh[:, k, :, 0:E0], oh[:, k, :, 0:E0], rk[:, :, 0:E0], ALU.mult))
                step(dve.tensor_reduce(slotf[:, k, :], oh[:, k, :, 0:E0], AX.X, ALU.add))
            step(dve.tensor_copy(slotu[:, :, :], slotf[:, :, :]))
            step(dve.tensor_tensor(cmp_t[:, :, :], spread(iota_t[:, 0:NT0], E0, 2), spread(incl[0:1, :], NT0, 1), ALU.is_ge))
            step(dve.tensor_reduce(eidf[:, :], cmp_t[:, :, :], AX.X, ALU.add))
            step(dve.tensor_scalar(eidf[:, :], eidf[:, :], float(E0 - 1), None, ALU.min))
            dve.tensor_copy(eid[:, :], eidf[:, :]).then_inc(route_ready, 1)
            dve.wait_ge(setup_copied, NCH + 2)
            for k in range(KC):
                dve.tensor_copy(tab[:, :, k], vecT[:, k, 8:8 + E0])
                dve.tensor_copy(tab[:, :, KC + k], vecT[:, k, 16:16 + E0])
            step(dve.tensor_copy(tab[:, :, 2 * KC:].rearrange("p e f -> p f e"), b1T[:, :, 0:E0]))
            dve.wait_ge(attn_exps, 2)
            step(dve.tensor_scalar(gate[:, 0, :], gate[:, 1, :], 1.0, None, ALU.add))
            step(dve.reciprocal(gate[:, 2, :], gate[:, 0, :]))
            step(dve.tensor_tensor(gate[:, 3, :], gate[:, 1, :], gate[:, 2, :], ALU.mult))
            step(dve.tensor_tensor(gate[:, 0, :], gate[:, 2, :], gate[:, 3, :], ALU.add))
            step(dve.tensor_scalar(gate[:, 0, :], gate[:, 0, :], 1.0, None, ALU.add))
            dve.wait_ge(route_ready, 1)

            def biased0(ff, j, s):
                dve.wait_ge(ff.h_turned, j + 1 + ff.slots)
                dve.wait_ge(ff.active, j + ff.slots)
                for n in range(2):
                    ins = dve.tensor_tensor(hb[:, n * 512:(n + 1) * 512].rearrange("p (f n) -> p f n", f=4),
                                            b_hT[n][:, :].rearrange("p (f n) -> p f n", f=4),
                                            spread(cur[:, s, 2 * KC + 4 * n:2 * KC + 4 * n + 4], P, 2), ALU.add)
                ins.then_inc(ff.biased, 1)

            def biased1(ff, j, s):
                dve.wait_ge(ff.h_turned, j + 1 + ff.slots)
                dve.wait_ge(ff.active, j + ff.slots)
                for n in range(2):
                    bias = b1T[:, 4 * n:4 * n + 4, bass.ds(j * 2 + E0, 2)]
                    ins = dve.tensor_tensor(hb[:, n * 512:(n + 1) * 512].rearrange("p (f e n) -> p f e n", f=4, e=2),
                                            b_hT[n][:, :].rearrange("p (f e n) -> p f e n", f=4, e=2),
                                            spread(bias, SLOT, 3), ALU.add)
                ins.then_inc(ff.biased, 1)

            def y_read(ff, j, s, i, loads):
                dve.wait_ge(ff.down_ready, j + 1 + ff.slots)
                dve.wait_ge(ff.w2_loaded[s], i * (16 * loads) + 16 * loads)
                dve.wait_ge(ff.y_free, j + 1)
                dve.tensor_tensor(y_sb[:, s, :], b_y[:, 0:C], b2_r[:, s, :], ALU.add).then_inc(ff.y_ready, 1)

            def expert_tiles(ff, count, cur_read, biased, loads):
                n = ff.slots
                cur_read(0, 0)
                cur_read(1, 1)
                biased(ff, 0, 0)

                def body(j, s, i, left=3):
                    if left > 2:
                        cur_read(j + 2, (s + 2) % n)
                    y_read(ff, j, s, i, loads)
                    if left > 1:
                        biased(ff, j + 1, (s + 1) % n)
                trips = (count - 2) // n
                with dve.Fori(0, trips) as i:
                    for s in range(n):
                        body(i * n + s, s, i)
                for j in range(n * trips, count):
                    body(j, j % n, j // n, count - j)

            with dve.register("tile_expert") as expert:
                def cur_read(j, s):
                    dve.reg_load(expert, eid[0:1, bass.ds(j, 1)])
                    e = dve.snap(expert, min_val=0, max_val=E0 - 1)
                    dve.wait_ge(ff0.xT_ready, j + 1)
                    dve.wait_ge(ff0.biased, j + 1)
                    dve.tensor_copy(cur[:, s, :].unsqueeze(1), tab[:, bass.ds(e, 1), :]).then_inc(ff0.cur_ready, 1)
                expert_tiles(ff0, NT0, cur_read, biased0, 2)

            for t in range(T):
                ins = dve.tensor_scalar(hX[:, t, :], hB[:, t, :], gate[:, 0, t:t + 1], None, ALU.mult)
            step(ins)

            def combine(t):
                dve.wait_ge(gathered[t], 16 * 2)
                for k in range(2):
                    step(dve.scalar_tensor_tensor(hX[:, t, :], yg[:, k, t, :], gate[:, 2 + k, t:t + 1], hX[:, t, :],
                                                  ALU.mult, ALU.add))
                step(dve.bn_stats(stats[:, t, :], hX[:, t, :]))
                dve.bn_aggr(mv[:, t, :], stats[:, t, :]).then_inc(var_ready, 1)
            combine(0)
            for t in range(T):
                if t + 1 < T:
                    combine(t + 1)
                n_std[0] += 1
                rstd(t, t + 1, n_std[0])
                normed(hA[:, t, :], hX[:, t, :], t).then_inc(rows_ready, 1)

            copied = n_mm[0]
            n_mm[0] += 3 * T

            def scores(dst, n, a, b_):
                step(dve.tensor_tensor(prod1[:, 0:n, :], a, b_, ALU.mult))
                step(dve.tensor_reduce(dst, prod1[:, 0:n, :].rearrange("p s (h d) -> p s h d", h=H1), AX.X, ALU.add))
            for t in range(T):
                dve.wait_ge(product_read, copied + 2 * t + 2)
                scores(S1[:, t, :, 0:t + 1].rearrange("p h s -> p s h"), t + 1,
                       qkv1[:, 0:t + 1, INNER:2 * INNER], spread(qkv1[:, t, 0:INNER], t + 1, 1))
                if t:
                    scores(S1[:, 0:t, :, t], t, qkv1[:, 0:t, 0:INNER], spread(qkv1[:, t, INNER:2 * INNER], t, 1))
            dve.wait_ge(norms_ready, 1)
            step(dve.tensor_scalar(ssq[:, :, :], rnorm[:, :, :], 1e-12, None, ALU.max))
            step(dve.reciprocal(rnorm[:, :, :], ssq[:, :, :]))
            step(dve.tensor_tensor(S1[:, :, :, :], S1[:, :, :, :], spread(rnorm[:, :, 0:H1], T, 3), ALU.mult))
            dve.tensor_tensor(S1[:, :, :, :], S1[:, :, :, :], spread(rnorm[:, :, H1:].rearrange("p s h -> p h s"), T, 1),
                              ALU.mult).then_inc(logits_shifted, 1)
            dve.wait_ge(attn_exps, 3)
            flat1 = S1[:, :, :, :].rearrange("p t h s -> p (t h) s")
            hs1 = hs[:, :, 0:T * H1]
            step(dve.tensor_reduce(hs1[:, 0, :], flat1, AX.X, ALU.add))
            step(dve.tensor_scalar(hs1[:, 1, :], hs1[:, 0, :], 1e-6, None, ALU.max))
            step(dve.reciprocal(hs1[:, 2, :], hs1[:, 1, :]))
            step(dve.tensor_tensor(flat1, flat1, spread(hs1[:, 2, :], T, 2), ALU.mult))
            dve.wait_ge(product_read, n_mm[0])

            def attended(t):
                b = product()
                dve.tensor_tensor(hX[:, t, :], b[:, 0:C], hA[:, t, :], ALU.add).then_inc(product_read, 1)
                dve.wait_ge(product_read, n_mm[0])
                return dve.bn_stats(stats[:, t, :], hX[:, t, :])
            for t in range(T):
                pr = weighted1[t % 3]
                if t >= 3:
                    dve.wait_ge(turned, TURNED_1 + t - 2)
                step(dve.tensor_tensor(pr.rearrange("p s (h d) -> p s h d", h=H1),
                                       qkv1[:, :, 2 * INNER:].rearrange("p s (h d) -> p s h d", h=H1),
                                       spread(S1[:, t, :, :].rearrange("p h s -> p s h"), D1, 3), ALU.mult))
                dve.tensor_tensor(pr[:, 0:2, :], pr[:, 0:2, :], pr[:, 2:4, :], ALU.add).then_inc(rows_ready, 1)
                if t >= 2:
                    attended(t - 2)
            attended(T - 2)
            step(attended(T - 1))
            for t in range(T):
                ins = dve.bn_aggr(mv[:, t, :], stats[:, t, :])
            ins.then_inc(var_ready, 1)
            n_std[0] += 1
            rstd(0, T, n_std[0])
            for t in range(T):
                normed(hB[:, t, :], hX[:, t, :], t).then_inc(rows_ready, 1)

            for t in range(T):
                read_product(lg[:, t, :], bg_r)
            dve.wait_ge(product_read, n_mm[0])
            step(dve.tensor_reduce(gate[:, 0, :], lg[:, :, :], AX.X, ALU.max))
            dve.tensor_tensor(lg[:, :, :], lg[:, :, :], spread(gate[:, 0, :], E1, 2), ALU.subtract).then_inc(logits_shifted, 1)
            dve.wait_ge(attn_exps, 4)
            for t in range(T):
                ins = dve.max(best[:, t, :], lg2[:, t, :])
            step(ins)
            for t in range(T):
                ins = dve.max_index(besti[:, t, :], best[:, t, :], lg2[:, t, :])
            step(ins)
            step(dve.tensor_copy(bestf[:, :, :], besti[:, :, 0:2]))
            step(dve.tensor_tensor(oh[:, 0, :, :], spread(iota_e[:, :], T, 1), spread(bestf[:, :, 0], E1, 2), ALU.is_equal))
            dve.tensor_reduce(msum[:, 0, :], oh[:, 0, :, :].rearrange("p t e -> p e t"), AX.X, ALU.add).then_inc(rows_ready, 1)
            tiles_before(E1)
            step(dve.tensor_reduce(gate[:, 1, :], lg2[:, :, :], AX.X, ALU.add))
            step(dve.reciprocal(gate[:, 2, :], gate[:, 1, :]))
            b = product()
            dve.tensor_tensor(rk[:, :, :], mcum[:, :, :], spread(b[:, 0:E1], T, 1), ALU.add).then_inc(product_read, 1)
            dve.wait_ge(product_read, n_mm[0])
            step(dve.tensor_tensor(oh[:, 0, :, :], oh[:, 0, :, :], rk[:, :, :], ALU.mult))
            step(dve.tensor_reduce(slotf[:, 0, :], oh[:, 0, :, :], AX.X, ALU.add))
            step(dve.tensor_scalar(gate[:, 0, :], slotf[:, 0, :], float(CAP), None, ALU.is_lt))
            step(dve.tensor_scalar(slotf[:, 1, :], slotf[:, 0, :], float(CAP), None, ALU.min))
            step(dve.scalar_tensor_tensor(slotf[:, 1, :], bestf[:, :, 0], float(SLOT), slotf[:, 1, :], ALU.mult, ALU.add))
            step(dve.tensor_copy(gslotu[:, :], slotf[:, 1, :]))
            step(dve.tensor_tensor(slotf[:, 1, :], slotf[:, 1, :], trash[:, :], ALU.subtract))
            step(dve.tensor_tensor(slotf[:, 1, :], slotf[:, 1, :], gate[:, 0, :], ALU.mult))
            step(dve.tensor_tensor(slotf[:, 1, :], slotf[:, 1, :], trash[:, :], ALU.add))
            dve.tensor_copy(slotu[:, 0, :], slotf[:, 1, :]).then_inc(route_ready, 1)
            step(dve.tensor_tensor(gate[:, 3, :], gate[:, 0, :], gate[:, 2, :], ALU.mult))
            expert_tiles(ff1, NPAIR, lambda j, s: None, biased1, 3)

            def output_stats(t):
                dve.wait_ge(gathered[t], 16 * 3)
                step(dve.scalar_tensor_tensor(hX[:, t, :], yg[:, 0, t, :], gate[:, 3, t:t + 1], hB[:, t, :],
                                              ALU.mult, ALU.add))
                step(dve.bn_stats(stats[:, t, :], hX[:, t, :]))
                dve.bn_aggr(mv[:, t, :], stats[:, t, :]).then_inc(var_ready, 1)
            output_stats(0)
            for t in range(T):
                if t + 1 < T:
                    output_stats(t + 1)
                n_std[0] += 1
                rstd(t, t + 1, n_std[0])
                normed(hA[:, t, :], hX[:, t, :], t).then_inc(rows_ready, 1)


TOK, A0, FF0, A1, FF1 = "L0_tok_", "L0_attn_", "L0_ffn_", "L1_attn_", "L1_ffn_"


def kernel(**inputs):
    import numpy as _np
    import concourse.bacc as _bacc
    from concourse import mybir as _mybir
    from concourse.bass_utils import run_bass_kernel_spmd as _run

    nc = _bacc.Bacc("TRN2", target_bir_lowering=False, num_devices=1)
    arrays = {}

    def arg(name):
        a = _np.ascontiguousarray(inputs[name])
        arrays[f"in_{name}_dram"] = a
        return nc.dram_tensor(f"in_{name}_dram", a.shape, _mybir.dt.from_np(a.dtype), kind="ExternalInput").ap()

    vecs = [arg(TOK + n) for n in ("la_ln_q_g", "la_ln_q_b", "la_ln_kv_g", "la_ln_kv_b",
                                   "ga_ln_q_g", "ga_ln_q_b", "ga_ln_kv_g", "ga_ln_kv_b")]
    B, T, C = inputs["x"].shape[0], 5, inputs[A0 + "Wo"].shape[1]
    out = nc.dram_tensor("out_0_dram", (B, T, C), _mybir.dt.float32, kind="ExternalOutput").ap()
    build_program(
        nc, arg("x"), arg(TOK + "conv_w"), arg(TOK + "class_emb"), vecs, arg(TOK + "la_wq"), arg(TOK + "la_wkv"),
        arg(TOK + "la_proj_w"), arg(TOK + "la_proj_b"), arg(TOK + "ga_wq"), arg(TOK + "ga_wkv"),
        arg(TOK + "ga_proj_w"), arg(TOK + "ga_proj_b"), arg(TOK + "mod_w"), arg(TOK + "mod_b"),
        [arg(A0 + n) for n in ("Wq", "Wk", "Wv")], [arg(A0 + n) for n in ("bq", "bk", "bv")],
        arg(A0 + "Wo"), arg(A0 + "bo"), arg(A0 + "gamma"), arg(A0 + "beta"),
        arg(FF0 + "router_W"), arg(FF0 + "router_b"), arg(FF0 + "ln_g"), arg(FF0 + "ln_b"),
        arg(FF0 + "W1"), arg(FF0 + "b1"), arg(FF0 + "W2"), arg(FF0 + "b2"),
        arg(A1 + "Wq"), arg(A1 + "Wkv"), arg(A1 + "Wo"),
        arg(FF1 + "Wg"), arg(FF1 + "bg"), arg(FF1 + "W1"), arg(FF1 + "b1"), arg(FF1 + "W2"), arg(FF1 + "b2"), out)
    r = _run(nc, [arrays], core_ids=[0])
    return r.results[0]["out_0_dram"]
```

```python
from contextlib import ExitStack

import concourse.bass as bass
from concourse import mybir

ALU = mybir.AluOpType
ACT = mybir.ActivationFunctionType
AX = mybir.AxisListType
F32 = mybir.dt.float32
I32 = mybir.dt.int32
U32 = mybir.dt.uint32
P = 128


def reuse(w, p, per):
    n = w * per + p + CREDIT
    return n if p == 0 else n - 2 if p == 1 else n - 1


CREDIT = 3


class Steps:

    def __init__(self, eng, sem):
        self.eng, self.sem, self.n = eng, sem, 0

    def __call__(self, ins):
        ins.then_inc(self.sem, 1)
        self.n = self.n + 1
        self.eng.wait_ge(self.sem, self.n)

    def mark(self, ins):
        ins.then_inc(self.sem, 1)
        self.n = self.n + 1
        return self.n

    def after(self, n):
        self.eng.wait_ge(self.sem, n)

    def loop(self, base, trip, per):
        self.n = base + trip * per


def build_program(nc, x, conv_w, class_emb, tok_vecs, la_wq, la_wkv, la_proj_w, la_proj_b, ga_wq, ga_wkv,
                  ga_proj_w, ga_proj_b, mod_w, mod_b, a0_w, a0_b, a0_wo, a0_bo, a0_gamma, a0_beta,
                  f0_router_w, f0_router_b, f0_ln_g, f0_ln_b, f0_w1, f0_b1, f0_w2, f0_b2,
                  a1_wq, a1_wkv, a1_wo, f1_wg, f1_bg, f1_w1, f1_b1, f1_w2, f1_b2, out):
    B, CH, IH, IW = x.shape
    C, _, PS, _ = conv_w.shape
    assert B == P and C == 2 * P
    KC = C // P
    CS = 3
    G = IH // PS // CS
    NW = G * G
    NP = CS * CS
    T = NW + 1
    ROWS = G * CS * PS
    KP = CH * PS * PS
    NCH = -(-KP // P)
    KT = KP - (NCH - 1) * P
    H8 = 8
    DH = C // H8
    SCALE = float(C) ** -0.5
    LN_EPS = 1e-5

    H0 = 16
    D0 = C // H0
    E0, _, F0 = f0_w1.shape
    FC = F0 // P
    NT0 = (2 * T * P - E0) // P + E0
    H1 = 8
    INNER = a1_wq.shape[1]
    D1 = INNER // H1
    KI = INNER // P
    E1 = f1_w1.shape[0]
    CAP = -(-T * P // E1)
    SLOT = 64
    NPAIR = E1 // 2
    assert CAP < SLOT and F0 == f1_w1.shape[2]

    xs0 = nc.dram_tensor("xs0", [NT0 * P, C], F32, kind="Internal").ap()
    ys0 = nc.dram_tensor("ys0", [NT0 * P, C], F32, kind="Internal").ap()
    xs1 = nc.dram_tensor("xs1", [E1 * SLOT + T * P, C], F32, kind="Internal").ap()
    ys1 = nc.dram_tensor("ys1", [E1 * SLOT, C], F32, kind="Internal").ap()

    ctx = ExitStack()
    with ctx:
        def sb(name, shape, dt=F32):
            return ctx.enter_context(nc.sbuf_tensor(name, shape, dt))

        def sem(name):
            return ctx.enter_context(nc.semaphore(name))

        IMG = CH * ROWS * IW
        AR = 45400
        arena = sb("arena", [P, AR])

        def at(off, size, pat=None, /, **kw):
            a = arena[:, off:off + size]
            return a.rearrange(pat, **kw) if pat else a

        img = at(0, IMG, "p (c i j) -> p c i j", c=CH, i=ROWS)
        o = IMG
        packed = at(o, 2 * KP, "p (s k) -> p s k", s=2); o += 2 * KP
        patchT = at(o, 2 * NCH * P, "p (s k n) -> p s k n", s=2, k=NCH); o += 2 * NCH * P
        pe_raw = at(o, NP * C, "p (n c) -> p n c", n=NP); o += NP * C
        xhat = at(o, NP * C, "p (n c) -> p n c", n=NP); o += NP * C
        kvw = at(o, NP * 2 * C, "p (n c) -> p n c", n=NP)
        convw_raw = at(o, KC * KP, "p (h k) -> p h k", h=KC)
        vec_raw = at(o + KC * KP, C)
        b1_raw = at(o + KC * KP + C, F0); o += NP * 2 * C
        kvnT = at(o, 2 * KC * P, "p (s k n) -> p s k n", s=2, k=KC); o += 2 * KC * P
        redT = at(o, KC * P, "p (k n) -> p k n", k=KC); o += KC * P
        q_sb = at(o, C); o += C
        agg = at(o, NW * C, "p (n c) -> p n c", n=NW); o += NW * C
        redb = at(o, NW * C, "p (n c) -> p n c", n=NW); o += NW * C
        red = at(o, C); o += C
        redhat = at(o, C); o += C
        convT = at(o, NCH * C, "p (k c) -> p k c", k=NCH); o += NCH * C

        def wt(n):
            nonlocal o
            a = at(o, KC * n, "p (k n) -> p k n", k=KC)
            o += KC * n
            return a
        wq_s, wkv_s, proj_s, gwq_s, gwkv_s, gproj_s, mod_s = wt(C), wt(2 * C), wt(C), wt(C), wt(2 * C), wt(C), wt(C)
        assert o <= AR, o

        o = 0
        a0w_s = at(0, KC * 3 * C, "p (k n) -> p k n", k=KC); o += KC * 3 * C
        a0wo_s = at(o, KC * C, "p (k n) -> p k n", k=KC); o += KC * C
        qkv0 = at(o, T * 3 * C, "p (t n) -> p t n", t=T); o += T * 3 * C
        prod0 = at(o, T * C, "p (s c) -> p s c", s=T); o += T * C
        weighted0 = [prod0, qkv0[:, :, 0:C], qkv0[:, :, C:2 * C]]
        local = at(o, NW * C, "p (n c) -> p n c", n=NW); o += NW * C
        lhat = at(o, NW * C, "p (n c) -> p n c", n=NW); o += NW * C
        gkv = at(o, NW * 2 * C, "p (n c) -> p n c", n=NW); o += NW * 2 * C
        gprod = at(o, NW * C, "p (n c) -> p n c", n=NW); o += NW * C
        gagg = at(o, C); o += C
        residual = at(o, T * C, "p (t c) -> p t c", t=T); o += T * C
        yln = at(o, T * C, "p (t c) -> p t c", t=T); o += T * C
        assert o <= 16384, o
        PAIR = 2 * KC * F0
        up_at = [0, 2 * PAIR, 4 * PAIR]
        down_at = [o_ + PAIR for o_ in up_at]
        aggT = at(16384, KC * NW * P, "p (k n) -> p k n", k=KC)
        TILE = KC * F0
        SLOTS0 = 4
        w1_0 = [at(16384 + (i % 2 - i // 2 * 2) * 2 * TILE, TILE, "p (k f) -> p k f", k=KC) for i in range(SLOTS0)]
        w2_0 = [at(16384 + (i % 2 - i // 2 * 2) * 2 * TILE + TILE, TILE, "p (f c) -> p f c", f=FC) for i in range(SLOTS0)]
        assert TILE == FC * C
        o = 24576
        hB = at(o, T * C, "p (t c) -> p t c", t=T)
        squares = at(o, 2 * INNER); o += T * C
        assert 2 * INNER <= T * C
        down_at.append(o)
        hA = at(o, T * C, "p (t c) -> p t c", t=T); o += T * C
        hX = at(o, T * C, "p (t c) -> p t c", t=T)
        pool_at = [o]; o += T * C
        XT = at(o, KC * T * P, "p (k n) -> p k n", k=KC); o += KC * T * P
        pool_at.append(o)
        XT2 = at(o, KC * T * P, "p (k n) -> p k n", k=KC); o += KC * T * P
        OT = at(o - 2 * KC * T * P, KI * T * P, "p (k n) -> p k n", k=KI)
        assert KI == 2 * KC
        assert o - down_at[3] >= PAIR
        up_at.append(o)
        a1w_s = at(o, KC * 3 * INNER, "p (k n) -> p k n", k=KC); o += KC * 3 * INNER
        a1wo_s = at(o, KI * C, "p (k n) -> p k n", k=KI); o += KI * C
        assert o <= IMG + 2 * KP + 2 * NCH * P + 2 * NP * C + NP * 2 * C, o
        assert o - up_at[3] >= PAIR
        w1_1 = [at(i, PAIR, "p (e k f) -> p e k f", e=2, k=KC) for i in up_at]
        w2_1 = [at(i, PAIR, "p (e f c) -> p e f c", e=2, f=FC) for i in down_at]
        work = o
        qkv1 = at(o, T * 3 * INNER, "p (t n) -> p t n", t=T); o += T * 3 * INNER
        prod1 = at(o, T * INNER, "p (s c) -> p s c", s=T); o += T * INNER
        pool_prod = [at(i, 2 * INNER, "p (s c) -> p s c", s=2) for i in pool_at]
        last_squares = at(pool_at[(T - 2) % 2], 2 * INNER)
        weighted1 = [prod1, qkv1[:, :, 0:INNER], qkv1[:, :, INNER:2 * INNER]]
        assert o <= AR, o
        o = work
        SLOTS1 = 4
        xrow = at(o, SLOTS1 * C, "p (s c) -> p s c", s=SLOTS1); o += SLOTS1 * C
        xTs = at(o, SLOTS1 * KC * P, "p (s k n) -> p s k n", s=SLOTS1, k=KC); o += SLOTS1 * KC * P
        h_sb = at(o, F0); o += F0
        hb = at(o, F0); o += F0
        hTs = at(o, FC * P, "p (f n) -> p f n", f=FC); o += FC * P
        y_sb = at(o, SLOTS1 * C, "p (s c) -> p s c", s=SLOTS1); o += SLOTS1 * C
        b2_r = at(o, SLOTS1 * C, "p (s c) -> p s c", s=SLOTS1); o += SLOTS1 * C
        yg = at(o, 2 * T * C, "p (k t c) -> p k t c", k=2, t=T); o += 2 * T * C
        assert o <= AR, o

        rows_sb = sb("rows_sb", [P, 3 * C + 3 * C + 3 * C + C + E0 + E1])
        o = 0

        def row(n):
            nonlocal o
            o += n
            return rows_sb[:, o - n:o]
        projb_r, gprojb_r, modb_r, bqkv_r, bo_r, gamma_r, beta_r, cls_r, rb_r, bg_r = (
            row(C), row(C), row(C), row(3 * C), row(C), row(C), row(C), row(C), row(E0), row(E1))
        ident = sb("ident", [P, P])
        ones_sb = sb("ones_sb", [P, P])
        upper = sb("upper", [P, P])
        vecT = sb("vecT", [P, KC, 24])
        b1T = sb("b1T", [P, FC, 24])
        eps_sb = sb("eps_sb", [P, 1])
        gq_sb = sb("gq_sb", [P, C])
        stats = sb("stats", [P, NP, 6])
        mv = sb("mv", [P, NP, 2])
        sd = sb("sd", [P, NP])
        rs = sb("rs", [P, NP])
        sc = sb("sc", [P, NP, H8])
        ex = sb("ex", [P, NP, H8])
        hx = sb("hx", [P, 4, H8])

        zeros = sb("zeros", [P, C])
        S0 = sb("S0", [P, T, H0, T])
        S1 = sb("S1", [P, T, H1, T])
        hs = sb("hs", [P, 3, T * H0])
        ssq = sb("ssq", [P, T, 2 * H1])
        rnorm = sb("rnorm", [P, T, 2 * H1])
        neg16 = sb("neg16", [P, 1])
        rw_s = sb("rw_s", [P, KC, E0])
        wg_s = sb("wg_s", [P, KC, E1])
        iota_e = sb("iota_e", [P, E1])
        iota_t = sb("iota_t", [1, NT0 + 1])
        trash = sb("trash", [P, T])
        lg = sb("lg", [P, T, E1])
        lg2 = sb("lg2", [P, T, E1])
        best = sb("best", [P, T, 8])
        besti = sb("besti", [P, T, 8], U32)
        bestf = sb("bestf", [P, T, 2])
        oh = sb("oh", [P, 2, T, E1])
        msum = sb("msum", [P, T, E1])
        mcum = sb("mcum", [P, T, E1])
        rk = sb("rk", [P, T, E1])
        full = sb("full", [P, E0, T])
        tile_starts = sb("tile_starts", [P, T])
        ntile = sb("ntile", [P, E0])
        incl = sb("incl", [P, E0])
        basee = sb("basee", [P, E0])
        slotf = sb("slotf", [P, 2, T])
        slotu = sb("slotu", [P, 2, T], U32)
        gslotu = sb("gslotu", [P, T], U32)
        cmp_t = sb("cmp_t", [1, NT0, E0])
        eidf = sb("eidf", [1, NT0])
        eid = sb("eid", [1, NT0], I32)
        gate = sb("gate", [P, 4, T])
        tab = sb("tab", [P, E0, 2 * KC + FC])
        cur = sb("cur", [P, SLOTS0, 2 * KC + FC])

        bank = [ctx.enter_context(nc.psum_tensor(f"bank{i}", [P, 512], F32)) for i in range(8)]
        b_top, b_tail, b_conv, b_kvT, b_kv, b_q = bank[0], bank[1], bank[2:4], bank[4], bank[5:7], bank[7]
        b_turn, b_mm = bank[0:2], bank[2:6]
        b_x, b_h, b_hT, b_y = bank[0], bank[1:3], bank[3:5], bank[5]

        convw_loaded = sem("convw_loaded")
        img_rows = [sem(f"img_rows{i}") for i in range(CS)]
        vecs_loaded = sem("vecs_loaded")
        cls_loaded = sem("cls_loaded")
        gwq_loaded = sem("gwq_loaded")
        tokw_loaded = sem("tokw_loaded")
        rows_loaded = sem("rows_loaded")
        consts_made = sem("consts_made")
        setup_turned = sem("setup_turned")
        setup_copied = sem("setup_copied")
        patch_packed = sem("patch_packed")
        patch_turned = sem("patch_turned")
        patchT_ready = sem("patchT_ready")
        conv_ready = sem("conv_ready")
        conv_copied = sem("conv_copied")
        var_ready = sem("var_ready")
        std_ready = sem("std_ready")
        xhat_ready = sem("xhat_ready")
        kvn_turned = sem("kvn_turned")
        kvnT_ready = sem("kvnT_ready")
        kv_ready = sem("kv_ready")
        kv_copied = sem("kv_copied")
        redhat_ready = sem("redhat_ready")
        red_turned = sem("red_turned")
        redT_ready = sem("redT_ready")
        q_ready = sem("q_ready")
        q_copied = sem("q_copied")
        scores_shifted = sem("scores_shifted")
        exps_ready = sem("exps_ready")
        agg_ready = sem("agg_ready")
        dve_step = sem("dve_step")
        act_step = sem("act_step")
        pool_step = sem("pool_step")
        turned = sem("turned")
        turned_copied = sem("turned_copied")
        product_ready = sem("product_ready")
        product_read = sem("product_read")
        rows_ready = sem("rows_ready")
        out_stored = sem("out_stored")
        a0w_loaded = sem("a0w_loaded")
        a1w_loaded = sem("a1w_loaded")
        gatew_loaded = sem("gatew_loaded")
        scratch_zeroed = sem("scratch_zeroed")
        logits_shifted = sem("logits_shifted")
        attn_exps = sem("attn_exps")
        squares_ready = sem("squares_ready")
        norms_ready = sem("norms_ready")
        slots_ready = sem("slots_ready")
        pool_products = sem("pool_products")
        pool_products_used = sem("pool_products_used")
        route_ready = sem("route_ready")
        gathered = [sem(f"gathered{t}") for t in range(T)]

        class Ffn:

            def __init__(self, name, slots, scatters):
                self.slots = slots

                def s(what):
                    return sem(f"{name}_{what}")
                self.scattered = s("scattered")
                self.scatters = scatters
                self.x_loaded = [s(f"x_loaded{i}") for i in range(slots)]
                self.w1_loaded = [s(f"w1_loaded{i}") for i in range(slots)]
                self.w2_loaded = [s(f"w2_loaded{i}") for i in range(slots)]
                self.x_turned = s("x_turned")
                self.xT_ready = s("xT_ready")
                self.up_ready = s("up_ready")
                self.h_copied = s("h_copied")
                self.h_turned = s("h_turned")
                self.biased = s("biased")
                self.active = s("active")
                self.down_ready = s("down_ready")
                self.y_ready = s("y_ready")
                self.cur_ready = s("cur_ready")
                self.y_stored = [s(f"y_stored{i}") for i in range(slots)]
                self.y_free = s("y_free")
        ff0, ff1 = Ffn("ff0", SLOTS0, 2 * T), Ffn("ff1", SLOTS1, T)

        block = ctx.enter_context(nc.Block())

        def norm_n(which, t):
            first = NW * 4 + 3
            if which == 0:
                return first + (2 * t - 1 if t else 0)
            return first + (2 * t + 2 if t < T - 1 else 2 * T - 1)

        PRODUCTS_1 = 3 * NW + 1 + 2 * T + T + T + 1
        OUT_1 = PRODUCTS_1 + 4 * T
        TURNED_0 = 4 * NW + 2
        TURNED_1 = TURNED_0 + 3 * T
        N_VEC, N_TOKW, N_ROWS = 12, 6, 11
        N_CONST = 11
        R0 = 2 * NW + 1
        N_OUT = R0 + 2 + 6 * T
        def tiles(eng, lo, hi, slots, body):
            trips = (hi - 1 - lo) // slots
            if trips:
                with eng.Fori(0, trips) as i:
                    for s in range(slots):
                        body(i * slots + lo + s, s, i + lo // slots)
            for j in range(lo + trips * slots, hi):
                body(j, j % slots, j // slots)

        @block.sync
        def _(sp):
            sp.dma_start(convw_raw, conv_w.rearrange("(h p) c i j -> p h (c i j)", p=P)).then_inc(convw_loaded, 16)

            def image_rows(wr, pr):
                r = (wr * CS + pr) * PS
                if wr:
                    sp.wait_ge(img_rows[pr], 16 * wr)
                sp.dma_start(img[:, :, r:r + PS, :], x[:, :, r:r + PS, :]).then_inc(img_rows[pr], 16)
            sp.dma_start(cls_r, class_emb.partition_broadcast(P)).then_inc(cls_loaded, 16)
            image_rows(0, 0)
            sp.dma_start(gwq_s, ga_wq.rearrange("(k p) n -> p k n", p=P)).then_inc(gwq_loaded, 16)
            for i, v in enumerate(tok_vecs):
                sp.dma_start(vec_raw[i:i + 1, :], v.rearrange("(a c) -> a c", a=1)).then_inc(vecs_loaded, 16)
            sp.dma_start(vec_raw[8:16, :], f0_ln_g).then_inc(vecs_loaded, 16)
            sp.dma_start(vec_raw[16:24, :], f0_ln_b).then_inc(vecs_loaded, 16)
            sp.dma_start(b1_raw[0:E0, :], f0_b1).then_inc(vecs_loaded, 16)
            sp.dma_start(b1_raw[E0:E0 + E1, :], f1_b1).then_inc(vecs_loaded, 16)
            image_rows(0, 1)
            for dst, src in ((wq_s, la_wq), (wkv_s, la_wkv), (proj_s, la_proj_w),
                             (gwkv_s, ga_wkv), (gproj_s, ga_proj_w), (mod_s, mod_w)):
                sp.dma_start(dst, src.rearrange("(k p) n -> p k n", p=P)).then_inc(tokw_loaded, 16)
            image_rows(0, 2)
            for dst, src in ((projb_r, la_proj_b), (gprojb_r, ga_proj_b), (modb_r, mod_b),
                             (bqkv_r[:, 0:C], a0_b[0]), (bqkv_r[:, C:2 * C], a0_b[1]), (bqkv_r[:, 2 * C:3 * C], a0_b[2]),
                             (bo_r, a0_bo), (gamma_r, a0_gamma), (beta_r, a0_beta),
                             (rb_r, f0_router_b), (bg_r, f1_bg)):
                sp.dma_start(dst, src.partition_broadcast(P)).then_inc(rows_loaded, 16)
            for pr in range(CS):
                image_rows(1, pr)
            sp.dma_start(rw_s[:, :, :], f0_router_w.rearrange("(k p) e -> p k e", p=P)).then_inc(gatew_loaded, 16)
            sp.dma_start(wg_s[:, :, :], f1_wg.rearrange("(k p) e -> p k e", p=P)).then_inc(gatew_loaded, 16)
            sp.wait_ge(consts_made, N_CONST)
            for dst in (xs0, xs1):
                n = dst.shape[0] // P
                sp.dma_start(dst.rearrange("(n p) c -> p n c", p=P), zeros[:, :].unsqueeze(1).to_broadcast([P, n, C]))\
                    .then_inc(scratch_zeroed, 16)
            sp.wait_ge(patch_packed, NW * NP)
            for i in range(3):
                sp.dma_start(a0w_s[:, :, i * C:(i + 1) * C], a0_w[i].rearrange("(k p) n -> p k n", p=P)).then_inc(a0w_loaded, 16)
            sp.dma_start(a0wo_s, a0_wo.rearrange("(k p) n -> p k n", p=P)).then_inc(a0w_loaded, 16)
            sp.wait_ge(agg_ready, NW + 1)
            sp.dma_start(a1w_s[:, :, 0:INNER], a1_wq.rearrange("(k p) n -> p k n", p=P)).then_inc(a1w_loaded, 16)
            sp.dma_start(a1w_s[:, :, INNER:3 * INNER], a1_wkv.rearrange("(k p) n -> p k n", p=P)).then_inc(a1w_loaded, 16)
            sp.dma_start(a1wo_s, a1_wo.rearrange("(k p) n -> p k n", p=P)).then_inc(a1w_loaded, 16)

            def load_x(ff, j, s, xs):
                sp.wait_ge(ff.x_turned, j + 1)
                sp.dma_start(xrow[:, s, :], xs[bass.ds(j * P, P), :]).then_inc(ff.x_loaded[s], 16)

            def load_up(ff, j, s, w1, src):
                sp.wait_ge(ff.up_ready, j + 1)
                sp.dma_start(w1, src).then_inc(ff.w1_loaded[s], 16)

            def load_down(ff, j, s, w2, src):
                sp.wait_ge(ff.down_ready, j + 1)
                sp.dma_start(w2, src).then_inc(ff.w2_loaded[s], 16)

            def load_biases(ff, j, s, biases):
                sp.wait_ge(ff.y_ready, j + 1)
                for dst, src in biases:
                    sp.dma_start(dst, src).then_inc(ff.w2_loaded[s], 16)

            def load_tiles(ff, count, weights, xs, ahead):
                n = ff.slots
                for j in range(ahead):
                    up, down, biases = weights(j, j)
                    if ff is ff1 and j == n - 1:
                        sp.wait_ge(product_ready, OUT_1)
                    up(j)
                    if ff is ff1 and j == n - 1:
                        sp.wait_ge(product_ready, OUT_1 + T)
                    down(j)
                sp.wait_ge(ff.scattered, ff.scatters * 16)
                for j in range(ahead):
                    load_x(ff, j, j, xs)
                    weights(j, j)[2](j)
                for j in range(ahead, n):
                    up, down, biases = weights(j, j)
                    load_x(ff, j, j, xs)
                    up(j)
                    down(j)
                    biases(j)
                load_x(ff, n, 0, xs)

                def body(j, s, i):
                    up, down, biases = weights(j, s)
                    up(j)
                    if not isinstance(j, int) or j + 1 < count:
                        load_x(ff, j + 1, (s + 1) % n, xs)
                    down(j)
                    biases(j)
                tiles(sp, n, count, n, body)

            sp.wait_ge(route_ready, 1)
            with sp.register("tile_expert") as expert:
                def weights0(j, s):
                    sp.reg_load(expert, eid[0:1, bass.ds(j, 1)])
                    e = sp.snap(expert, min_val=0, max_val=E0 - 1)
                    up = f0_w1[bass.ds(e, 1)].rearrange("e (k p) f -> p (e k) f", p=P)
                    down = f0_w2[bass.ds(e, 1)].rearrange("e (f p) c -> p (e f) c", p=P)
                    bias = f0_b2[bass.ds(e, 1), :].rearrange("e c -> (e c)").partition_broadcast(P)
                    return (lambda j: load_up(ff0, j, s, w1_0[s], up),
                            lambda j: load_down(ff0, j, s, w2_0[s], down),
                            lambda j: load_biases(ff0, j, s, [(b2_r[:, s, :], bias)]))
                load_tiles(ff0, NT0, weights0, xs0, 1)
            sp.wait_ge(ff0.y_ready, NT0 + ff0.slots)
            for t in range(T):
                sp.wait_ge(gathered[t], 16 * 2)
            def weights1(j, s):
                up = f1_w1[bass.ds(j * 2, 2)].rearrange("e (k p) f -> p e k f", p=P)
                down = f1_w2[bass.ds(j * 2, 2)].rearrange("e (f p) c -> p e f c", p=P)
                biases = [(b2_r[e * SLOT:(e + 1) * SLOT, s, :],
                           f1_b2[bass.ds(j * 2 + e, 1), :].rearrange("e c -> (e c)").partition_broadcast(SLOT))
                          for e in range(2)]
                return (lambda j: load_up(ff1, j, s, w1_1[s], up),
                        lambda j: load_down(ff1, j, s, w2_1[s], down),
                        lambda j: load_biases(ff1, j, s, biases))
            load_tiles(ff1, NPAIR, weights1, xs1, ff1.slots)
            for t in range(T):
                sp.wait_ge(rows_ready, N_OUT - T + t + 1)
                sp.dma_start(out[:, t, :], hA[:, t, :]).then_inc(out_stored, 16)
            sp.wait_ge(out_stored, 16 * T)
        @block.gpsimd
        def _(pool):
            step = Steps(pool, pool_step)
            step(pool.memset(ident[:, :], 0.0))
            pool.affine_select(out=ident[:, :], in_=ident[:, :], compare_op=ALU.not_equal, fill=1.0, base=0,
                               pattern=[[-1, P]], channel_multiplier=1).then_inc(consts_made, 1)
            step(pool.memset(upper[:, :], 1.0))
            pool.affine_select(out=upper[:, :], in_=upper[:, :], compare_op=ALU.is_gt, fill=0.0, base=0,
                               pattern=[[1, P]], channel_multiplier=-1).then_inc(consts_made, 1)
            pool.memset(ones_sb[:, :], 1.0).then_inc(consts_made, 1)
            pool.memset(eps_sb[:, :], LN_EPS).then_inc(consts_made, 1)
            pool.memset(neg16[:, :], -16.0).then_inc(consts_made, 1)
            pool.memset(zeros[:, :], 0.0).then_inc(consts_made, 1)
            pool.memset(S0[:, :, :, :], -1e30).then_inc(consts_made, 1)
            pool.iota(iota_e[:, :], [[1, E1]], base=0, channel_multiplier=0,
                      allow_small_or_imprecise_dtypes=True).then_inc(consts_made, 1)
            pool.iota(iota_t[:, :], [[1, NT0 + 1]], base=0, channel_multiplier=0,
                      allow_small_or_imprecise_dtypes=True).then_inc(consts_made, 1)
            pool.iota(trash[:, :], [[P, T]], base=E1 * SLOT, channel_multiplier=1,
                      allow_small_or_imprecise_dtypes=True).then_inc(consts_made, 1)
            pool.iota(tile_starts[:, :], [[P, T]], base=0, channel_multiplier=0,
                      allow_small_or_imprecise_dtypes=True).then_inc(consts_made, 1)
            with pool.Fori(0, G) as wr:
                with pool.Fori(0, G) as wc:
                    w = wr * G + wc
                    for p in range(NP):
                        pr, pc = divmod(p, CS)
                        pool.wait_ge(img_rows[pr], wr * 16 + 16)
                        pool.wait_ge(patch_turned, reuse(w, p, NP))
                        src = img[:, :, bass.ds(wr * (CS * PS) + pr * PS, PS), bass.ds(wc * (CS * PS) + pc * PS, PS)]
                        pool.tensor_copy(packed[:, p % 2, :].rearrange("p (c i j) -> p c i j", c=CH, i=PS), src)\
                            .then_inc(patch_packed, 1)

            def store_tiles(ff, ys, count):
                n = ff.slots

                def store(j, s, i):
                    if not isinstance(j, int) or j:
                        pool.wait_ge(ff.y_stored[(s - 1) % n], i * 16 + (16 if s else 0))
                        pool.sem_inc(ff.y_free, 1)
                    pool.wait_ge(ff.y_ready, j + 1 + n)
                    pool.dma_start(ys[bass.ds(j * P, P), :], y_sb[:, s, :]).then_inc(ff.y_stored[s], 16)
                for j in range(n):
                    store(j, j, 0)
                tiles(pool, n, count, n, store)
                pool.wait_ge(ff.y_stored[(count - 1) % n], (count - 1) // n * 16 + 16)

            for ff in (ff0, ff1):
                pool.sem_inc(ff.y_free, ff.slots)
            pool.wait_ge(slots_ready, 1)
            pool.wait_ge(scratch_zeroed, 32)
            for k in range(2):
                for t in range(T):
                    pool.indirect_dma_start(xs0, bass.IndirectOffsetOnAxis(ap=slotu[:, k, t:t + 1], axis=0),
                                            hX[:, t, :], None).then_inc(ff0.scattered, 16)
            store_tiles(ff0, ys0, NT0)
            for t in range(T):
                for k in range(2):
                    pool.indirect_dma_start(yg[:, k, t, :], None, ys0,
                                            bass.IndirectOffsetOnAxis(ap=slotu[:, k, t:t + 1], axis=0)).then_inc(gathered[t], 16)
            pool.wait_ge(rows_ready, R0 + 1 + 3 * T)
            for t in range(1, T):
                pool.wait_ge(product_read, PRODUCTS_1 + 2 * t + 2)
                if t >= 3:
                    pool.wait_ge(pool_products_used, t - 2)
                n = min(t, 2)
                pool.tensor_tensor(pool_prod[t % 2][:, 0:n, :], qkv1[:, 0:n, 0:INNER],
                                   qkv1[:, t, INNER:2 * INNER].unsqueeze(1).to_broadcast([P, n, INNER]),
                                   ALU.mult).then_inc(pool_products, 1)
            pool.wait_ge(slots_ready, 2)
            for t in range(T):
                pool.indirect_dma_start(xs1, bass.IndirectOffsetOnAxis(ap=slotu[:, 0, t:t + 1], axis=0),
                                        hB[:, t, :], None).then_inc(ff1.scattered, 16)
            store_tiles(ff1, ys1, NPAIR)
            for t in range(T):
                pool.indirect_dma_start(yg[:, 0, t, :], None, ys1,
                                        bass.IndirectOffsetOnAxis(ap=gslotu[:, t:t + 1], axis=0)).then_inc(gathered[t], 16)

        @block.tensor
        def _(pe):
            pe.wait_ge(consts_made, N_CONST)
            pe.wait_ge(convw_loaded, 16)
            for k in range(NCH):
                kn = P if k < NCH - 1 else KT
                if k >= 2:
                    pe.wait_ge(setup_copied, k - 1)
                for h in range(KC):
                    ins = pe.transpose(bank[k % 2][0:kn, h * P:(h + 1) * P], convw_raw[:, h, k * P:k * P + kn], ident[:, :])
                ins.then_inc(setup_turned, 1)
            pe.wait_ge(setup_copied, NCH)
            for s in (patch_turned, conv_ready, kv_ready):
                pe.sem_inc(s, CREDIT)
            for ff in (ff0, ff1):
                for s in (ff.x_turned, ff.up_ready, ff.h_turned, ff.down_ready):
                    pe.sem_inc(s, ff.slots)

            def turn_patch(w, p):
                g = w * NP + p
                pe.wait_ge(patch_packed, g + 1)
                pe.wait_ge(patchT_ready, g + 1)
                for k in range(NCH - 1):
                    pe.transpose(b_top[:, k * P:(k + 1) * P], packed[:, p % 2, k * P:(k + 1) * P], ident[:, :])
                pe.transpose(b_tail[0:KT, 0:P], packed[:, p % 2, (NCH - 1) * P:KP], ident[:, :]).then_inc(patch_turned, 1)

            def project_patch(w, p):
                pe.wait_ge(patchT_ready, w * NP + p + 2)
                pe.wait_ge(conv_copied, reuse(w, p, NP))
                for k in range(NCH):
                    kn = P if k < NCH - 1 else KT
                    ins = pe.matmul(b_conv[p % 2][:, 0:C], patchT[0:kn, p % 2, k, :], convT[0:kn, k, :],
                                    start=(k == 0), stop=(k == NCH - 1))
                ins.then_inc(conv_ready, 1)

            def turn_normed(w, p):
                g = w * NP + p
                pe.wait_ge(xhat_ready, g + 2)
                pe.wait_ge(kvnT_ready, g + 1)
                for k in range(KC):
                    ins = pe.transpose(b_kvT[:, k * P:(k + 1) * P], xhat[:, p, k * P:(k + 1) * P], ident[:, :])
                ins.then_inc(kvn_turned, 1)

            def key_value(w, p):
                pe.wait_ge(kvnT_ready, w * NP + p + 2)
                pe.wait_ge(kv_copied, reuse(w, p, NP))
                for k in range(KC):
                    ins = pe.matmul(b_kv[p % 2][:, :], kvnT[:, p % 2, k, :], wkv_s[:, k, :],
                                    start=(k == 0), stop=(k == KC - 1))
                ins.then_inc(kv_ready, 1)

            def turn_vectors():
                pe.wait_ge(vecs_loaded, 16 * N_VEC)
                for k in range(KC):
                    ins = pe.transpose(bank[4][:, k * 24:(k + 1) * 24], vec_raw[0:24, k * P:(k + 1) * P], ident[0:24, 0:24])
                ins.then_inc(setup_turned, 1)
                for f in range(FC):
                    ins = pe.transpose(bank[5][:, f * 24:(f + 1) * 24], b1_raw[0:24, f * P:(f + 1) * P], ident[0:24, 0:24])
                ins.then_inc(setup_turned, 1)
                pe.wait_ge(redhat_ready, 1)
                for k in range(KC):
                    ins = pe.transpose(b_q[:, k * P:(k + 1) * P], redhat[:, k * P:(k + 1) * P], ident[:, :])
                ins.then_inc(red_turned, 1)

            def class_query():
                pe.wait_ge(redT_ready, 1)
                pe.wait_ge(gwq_loaded, 16)
                for k in range(KC):
                    ins = pe.matmul(b_q[:, C:2 * C], redT[:, k, :], gwq_s[:, k, :], start=(k == 0), stop=(k == KC - 1))
                ins.then_inc(q_ready, 1)

            def window(w, first=False, last=False):
                for p in range(NP):
                    if p + 1 < NP:
                        turn_patch(w, p + 1)
                    else:
                        if first:
                            pe.wait_ge(setup_copied, NCH + 2)
                        turn_normed(w, 0)
                    project_patch(w, p)
                    if first and p == 5:
                        turn_vectors()
                    if first and p == 6:
                        class_query()
                pe.wait_ge(tokw_loaded, 16 * N_TOKW)
                for p in range(NP):
                    if p + 1 < NP:
                        turn_normed(w, p + 1)
                    elif not last:
                        turn_patch(w + 1, 0)
                    key_value(w, p)
                    if p == 5:
                        pe.wait_ge(redhat_ready, w + 2)
                        pe.wait_ge(q_copied, w + 1)
                        for k in range(KC):
                            ins = pe.transpose(b_q[:, k * P:(k + 1) * P], redhat[:, k * P:(k + 1) * P], ident[:, :])
                        ins.then_inc(red_turned, 1)
                    if p == 6:
                        pe.wait_ge(redT_ready, w + 2)
                        for k in range(KC):
                            ins = pe.matmul(b_q[:, C:2 * C], redT[:, k, :], wq_s[:, k, :],
                                            start=(k == 0), stop=(k == KC - 1))
                        ins.then_inc(q_ready, 1)
            turn_patch(0, 0)
            window(0, first=True)
            with pe.Fori(1, NW - 1) as w:
                window(w)
            window(NW - 1, last=True)
            pe.wait_ge(kv_copied, NW * NP + CREDIT)
            pe.wait_ge(q_copied, NW + 1)

            n_turn, n_mm = [0], [0]

            def turn_rows(src, chunks=KC):
                n = n_turn[0]
                n_turn[0] += 1
                if n >= 2:
                    pe.wait_ge(turned_copied, n - 1)
                for k in range(chunks):
                    ins = pe.transpose(b_turn[n % 2][:, k * P:(k + 1) * P], src[:, k * P:(k + 1) * P], ident[:, :])
                ins.then_inc(turned, 1)

            def project(xt, t, w_s, lo, hi, copied, chunks=KC, bias=None):
                n = n_mm[0]
                n_mm[0] += 1
                pe.wait_ge(turned_copied, copied)
                if n >= 4:
                    pe.wait_ge(product_read, n - 3)
                for k in range(chunks):
                    ins = pe.matmul(b_mm[n % 4][:, 0:hi - lo], xt[:, k, t * P:(t + 1) * P], w_s[:, k, lo:hi],
                                    start=(k == 0), stop=(k == chunks - 1 and bias is None))
                if bias is not None:
                    ins = pe.matmul(b_mm[n % 4][:, 0:hi - lo], ones_sb[0:1, :], bias[0:1, :], start=False, stop=True)
                ins.then_inc(product_ready, 1)

            def sum_turned(parts, chunks):
                m = n_turn[0]
                n_turn[0] += 1
                pe.wait_ge(turned_copied, m - 1)
                for k in range(chunks):
                    for i, part in enumerate(parts):
                        ins = pe.matmul(b_turn[m % 2][:, k * P:(k + 1) * P], part[:, k * P:(k + 1) * P], ident[:, :],
                                        start=(i == 0), stop=(i == len(parts) - 1))
                ins.then_inc(turned, 1)

            for n in range(NW - 1):
                pe.wait_ge(agg_ready, n + 2)
                turn_rows(agg[:, n, :])
            for n in range(NW - 1):
                project(aggT, n, proj_s, 0, C, n + 1)
            pe.wait_ge(agg_ready, NW + 1)
            turn_rows(agg[:, NW - 1, :])
            project(aggT, NW - 1, proj_s, 0, C, NW)
            for n in range(NW):
                pe.wait_ge(rows_ready, n + 1)
                turn_rows(local[:, n, :])
            for n in range(NW):
                project(XT2, n, mod_s, 0, C, NW + n + 1)
            for n in range(NW):
                pe.wait_ge(rows_ready, NW + n + 1)
                turn_rows(lhat[:, n, :])
            for n in range(NW):
                project(XT, n, gwkv_s, 0, 2 * C, 2 * NW + n + 1)
            n = 3 * NW
            pe.wait_ge(product_read, 2 * NW)
            for t in range(NW):
                turn_rows(hA[:, t, :])
            pe.wait_ge(a0w_loaded, 64)
            for t in range(2):
                project(XT2, t, a0w_s, 0, 2 * C, n + t + 1)
                project(XT2, t, a0w_s, 2 * C, 3 * C, n + t + 1)
            pe.wait_ge(rows_ready, 2 * NW + 1)
            turn_rows(gagg)
            project(XT, 0, gproj_s, 0, C, n + NW + 1)
            for t in range(2, NW):
                project(XT2, t, a0w_s, 0, 2 * C, n + t + 1)
                project(XT2, t, a0w_s, 2 * C, 3 * C, n + t + 1)
            pe.wait_ge(product_read, 3 * NW + 5)
            turn_rows(hA[:, NW, :])
            n += NW + 2
            project(XT2, NW, a0w_s, 0, 2 * C, n)
            project(XT2, NW, a0w_s, 2 * C, 3 * C, n)
            assert n_turn[0] == TURNED_0
            for t in range(T):
                pe.wait_ge(rows_ready, R0 + t + 1)
                sum_turned([weighted0[t % 3][:, i, :] for i in range(t + 1) if i not in (2, 3) or t < 3], KC)
                if t >= 1:
                    project(XT, t - 1, a0wo_s, 0, C, n + t, bias=bo_r)
            project(XT, T - 1, a0wo_s, 0, C, n + T, bias=bo_r)
            n += T

            def rank(rhs_own, rhs_all, width, totals=None):
                m = n_mm[0]
                n_mm[0] += 1
                pe.wait_ge(product_read, m - 3)
                b = b_mm[m % 4]
                ins = pe.matmul(b[:, 0:width], upper[:, :], rhs_own, start=True, stop=rhs_all is None)
                if rhs_all is not None:
                    ins = pe.matmul(b[:, 0:width], ones_sb[:, :], rhs_all, start=False, stop=True)
                if totals is not None:
                    for i, r in enumerate(totals):
                        ins = pe.matmul(b[:, 256:256 + E0], ones_sb[:, :], r, start=(i == 0), stop=(i == len(totals) - 1))
                ins.then_inc(product_ready, 1)

            def turn_x(ff, j, s, i):
                pe.wait_ge(ff.x_loaded[s], i * 16 + 16)
                pe.wait_ge(ff.xT_ready, j + ff.slots)
                for k in range(KC):
                    ins = pe.transpose(b_x[:, k * P:(k + 1) * P], xrow[:, s, k * P:(k + 1) * P], ident[:, :])
                ins.then_inc(ff.x_turned, 1)

            def turn_h(ff, j):
                pe.wait_ge(ff.h_copied, j + 1 + ff.slots)
                pe.wait_ge(ff.biased, (j + ff.slots) * 2)
                for f in range(FC):
                    ins = pe.transpose(b_hT[f // 4][:, f % 4 * P:(f % 4 + 1) * P], h_sb[:, f * P:(f + 1) * P], ident[:, :])
                ins.then_inc(ff.h_turned, 1)

            def before_up(ff, j, s, i):
                pe.wait_ge(ff.xT_ready, j + 1 + ff.slots)
                pe.wait_ge(ff.w1_loaded[s], i * 16 + 16)
                pe.wait_ge(ff.h_copied, j + ff.slots)

            def before_down(ff, j, s, i, loads):
                pe.wait_ge(ff.active, (j + ff.slots) * 2 + 1)
                pe.wait_ge(ff.w2_loaded[s], i * (16 * loads) + 16 * loads)
                pe.wait_ge(ff.y_ready, j + ff.slots)

            def up0(j, s, i):
                before_up(ff0, j, s, i)
                for n in range(2):
                    for k in range(KC):
                        ins = pe.matmul(b_h[n][:, :], xTs[:, s, k, :], w1_0[s][:, k, n * 512:(n + 1) * 512],
                                        start=(k == 0), stop=(k == KC - 1))
                ins.then_inc(ff0.up_ready, 1)

            def down0(j, s, i):
                before_down(ff0, j, s, i, 2)
                for f in range(FC):
                    if f == FC // 2:
                        pe.wait_ge(ff0.active, (j + ff0.slots) * 2 + 2)
                    ins = pe.matmul(b_y[:, 0:C], hTs[:, f, :], w2_0[s][:, f, :], start=(f == 0), stop=(f == FC - 1))
                ins.then_inc(ff0.down_ready, 1)

            def up1(j, s, i):
                before_up(ff1, j, s, i)
                for n in range(2):
                    for k in range(KC):
                        for e in range(2):
                            own = slice(e * SLOT, (e + 1) * SLOT)
                            ins = pe.matmul(b_h[n][own, :], xTs[:, s, k, own], w1_1[s][:, e, k, n * 512:(n + 1) * 512],
                                            start=(k == 0), stop=(k == KC - 1))
                ins.then_inc(ff1.up_ready, 1)

            def down1(j, s, i):
                before_down(ff1, j, s, i, 3)
                for f in range(FC):
                    if f == FC // 2:
                        pe.wait_ge(ff1.active, (j + ff1.slots) * 2 + 2)
                    for e in range(2):
                        own = slice(e * SLOT, (e + 1) * SLOT)
                        ins = pe.matmul(b_y[own, 0:C], hTs[:, f, own], w2_1[s][:, e, f, :], start=(f == 0), stop=(f == FC - 1))
                ins.then_inc(ff1.down_ready, 1)

            def expert_tiles(ff, count, up, down):
                n = ff.slots
                turn_x(ff, 0, 0, 0)
                up(0, 0, 0)
                turn_x(ff, 1, 1, 0)
                turn_h(ff, 0)

                def body(j, s, i, left=3):
                    if left > 1:
                        up(j + 1, (s + 1) % n, i + (s + 1) // n)
                    if left > 2:
                        turn_x(ff, j + 2, (s + 2) % n, i + (s + 2) // n)
                    down(j, s, i)
                    if left > 1:
                        turn_h(ff, j + 1)
                trips = (count - 2) // n
                with pe.Fori(0, trips) as i:
                    for s in range(n):
                        body(i * n + s, s, i)
                for j in range(n * trips, count):
                    body(j, j % n, j // n, count - j)

            pe.wait_ge(gatew_loaded, 32)
            for t in range(T):
                pe.wait_ge(rows_ready, R0 + T + t + 1)
                turn_rows(hB[:, t, :])
                if t:
                    project(XT2, t - 1, rw_s, 0, E0, n + t)
            project(XT2, T - 1, rw_s, 0, E0, n + T)
            n += T
            pe.wait_ge(rows_ready, R0 + 2 * T + 1)
            rank(msum[:, :, 0:E0], mcum[:, :, 0:E0], T * E0, (mcum[:, T - 1, 0:E0], msum[:, T - 1, 0:E0]))
            pe.wait_ge(product_read, n_mm[0])
            pe.wait_ge(turned_copied, n_turn[0])
            expert_tiles(ff0, NT0, up0, down0)
            pe.wait_ge(ff0.y_ready, NT0 + ff0.slots)
            pe.wait_ge(rows_ready, R0 + 1 + 2 * T + 1)
            turn_rows(hA[:, 0, :])
            pe.wait_ge(a1w_loaded, 48)
            for t in range(T):
                if t + 1 < T:
                    pe.wait_ge(rows_ready, R0 + 1 + 2 * T + t + 2)
                    turn_rows(hA[:, t + 1, :])
                for i in range(2):
                    project(XT, t, a1w_s, i * INNER, (i + 1) * INNER, n + t + 1)
            for t in range(T):
                project(XT, t, a1w_s, 2 * INNER, 3 * INNER, n + t + 1)
            n += T
            assert n_turn[0] == TURNED_1

            for t in range(T):
                pe.wait_ge(rows_ready, R0 + 1 + 3 * T + t + 1)
                sum_turned([weighted1[t % 3][:, i, :] for i in (0, 1, 4)], KI)
                if t >= 1:
                    project(OT, t - 1, a1wo_s, 0, C, n + t, KI)
            project(OT, T - 1, a1wo_s, 0, C, n + T, KI)
            n += T
            for t in range(T):
                pe.wait_ge(rows_ready, R0 + 1 + 4 * T + t + 1)
                turn_rows(hB[:, t, :])
            for t in range(T):
                project(XT, t, wg_s, 0, E1, n + t + 1)
            n += T
            pe.wait_ge(rows_ready, R0 + 1 + 5 * T + 1)
            rank(msum[:, 0, :], None, E1)
            pe.wait_ge(product_read, n_mm[0])
            pe.wait_ge(turned_copied, n_turn[0])
            expert_tiles(ff1, NPAIR, up1, down1)

        @block.scalar
        def _(act):
            step = Steps(act, act_step)
            for k in range(NCH):
                kn = P if k < NCH - 1 else KT
                act.wait_ge(setup_turned, k + 1)
                act.activation(convT[0:kn, k, :], bank[k % 2][0:kn, 0:C], ACT.Copy).then_inc(setup_copied, 1)
            act.wait_ge(setup_copied, NCH)
            for s in (conv_copied, kv_copied):
                act.sem_inc(s, CREDIT)
            for s in (patchT_ready, kvnT_ready):
                act.sem_inc(s, 1)
            for ff in (ff0, ff1):
                for s in (ff.xT_ready, ff.h_copied):
                    act.sem_inc(s, ff.slots)
                act.sem_inc(ff.active, ff.slots * 2)

            def vec(v, k):
                return vecT[:, k, v:v + 1]

            def std(lo, hi, n):
                act.wait_ge(var_ready, n)
                act.activation(sd[:, lo:hi], mv[:, lo:hi, 1], ACT.Sqrt, bias=eps_sb[:, 0:1]).then_inc(std_ready, 1)

            def affine_turned(dst, src, g, b):
                for k in range(KC):
                    ins = act.activation(dst[:, k, :], src[:, k * P:(k + 1) * P], ACT.Identity,
                                         scale=vec(g, k), bias=vec(b, k))
                return ins

            std(0, 1, 1)

            def vectors_copied():
                act.wait_ge(setup_turned, NCH + 1)
                act.activation(vecT[:, :, :].rearrange("p k v -> p (k v)"), bank[4][:, 0:KC * 24], ACT.Copy).then_inc(setup_copied, 1)
                act.wait_ge(setup_turned, NCH + 2)
                act.activation(b1T[:, :, :].rearrange("p k v -> p (k v)"), bank[5][:, 0:FC * 24], ACT.Copy).then_inc(setup_copied, 1)
                act.wait_ge(setup_copied, NCH + 2)
                act.wait_ge(red_turned, 1)
                affine_turned(redT, b_q, 4, 5).then_inc(redT_ready, 1)

            def class_query_copied():
                act.wait_ge(q_ready, 1)
                act.activation(gq_sb[:, :], b_q[:, C:2 * C], ACT.Copy, scale=SCALE).then_inc(q_copied, 1)

            def patch_copied(w, p):
                act.wait_ge(patch_turned, w * NP + p + 1 + CREDIT)
                act.wait_ge(conv_ready, reuse(w, p, NP))
                act.activation(patchT[:, p % 2, 0:NCH - 1, :].rearrange("p k n -> p (k n)"), b_top[:, :], ACT.Copy)
                act.activation(patchT[0:KT, p % 2, NCH - 1, :], b_tail[0:KT, 0:P], ACT.Copy).then_inc(patchT_ready, 1)

            def raw_copied(w, p):
                act.wait_ge(conv_ready, w * NP + p + 1 + CREDIT)
                act.wait_ge(xhat_ready, w * NP + 1)
                act.activation(pe_raw[:, p, :], b_conv[p % 2][:, 0:C], ACT.Copy).then_inc(conv_copied, 1)

            def normed_copied(w, p):
                act.wait_ge(kvn_turned, w * NP + p + 1)
                act.wait_ge(kv_ready, reuse(w, p, NP))
                affine_turned(kvnT[:, p % 2], b_kvT, 2, 3).then_inc(kvnT_ready, 1)

            def kv_stored(w, p):
                act.wait_ge(kv_ready, w * NP + p + 1 + CREDIT)
                act.wait_ge(agg_ready, w + 1)
                act.activation(kvw[:, p, :], b_kv[p % 2][:, :], ACT.Copy).then_inc(kv_copied, 1)

            def window_exps(w):
                act.wait_ge(scores_shifted, w + 1)
                act.activation(ex[:, :, :], sc[:, :, :], ACT.Exp).then_inc(exps_ready, 1)

            def window(w, first=False, last=False):
                for p in range(NP):
                    if p + 1 < NP:
                        patch_copied(w, p + 1)
                    else:
                        normed_copied(w, 0)
                    raw_copied(w, p)
                    if p == 1 and not first:
                        window_exps(w - 1)
                    if p == 5 and first:
                        vectors_copied()
                    if p == 6 and first:
                        class_query_copied()
                    if p in (3, 6):
                        std(p - 3, p, w * 4 + p // 3 + 1)
                for p in range(NP):
                    if p + 1 < NP:
                        normed_copied(w, p + 1)
                    elif not last:
                        patch_copied(w + 1, 0)
                    if p == 0:
                        std(6, 9, w * 4 + 4)
                    kv_stored(w, p)
                    if p == 3:
                        std(0, 1, w * 4 + 5)
                    if p == 5:
                        act.wait_ge(red_turned, w + 2)
                        affine_turned(redT, b_q, 0, 1).then_inc(redT_ready, 1)
                    if p == 6:
                        act.wait_ge(q_ready, w + 2)
                        act.wait_ge(agg_ready, w + 1)
                        act.activation(q_sb, b_q[:, C:2 * C], ACT.Copy, scale=SCALE).then_inc(q_copied, 1)
            patch_copied(0, 0)
            window(0, first=True)
            with act.Fori(1, NW - 1) as w:
                window(w)
            window(NW - 1, last=True)

            n_turn = [0]

            def rows_turned(dst, t, g=None, b=None, chunks=KC):
                n = n_turn[0]
                n_turn[0] += 1
                act.wait_ge(turned, n + 1)
                d = dst[:, :, t * P:(t + 1) * P]
                if g is None:
                    act.activation(d, b_turn[n % 2][:, 0:chunks * P].rearrange("p (k n) -> p k n", k=chunks), ACT.Copy)\
                        .then_inc(turned_copied, 1)
                else:
                    affine_turned(d, b_turn[n % 2], g, b).then_inc(turned_copied, 1)

            for n in range(NW - 1):
                rows_turned(aggT, n)
            window_exps(NW - 1)
            rows_turned(aggT, NW - 1)
            for n in range(NW):
                rows_turned(XT2, n)
            std(0, NW, NW * 4 + 2)
            act.wait_ge(product_ready, NW)
            for n in range(NW):
                rows_turned(XT, n, 6, 7)
            act.wait_ge(product_ready, 3 * NW)
            for t in range(NW):
                rows_turned(XT2, t)
            act.wait_ge(scores_shifted, NW + 1)
            act.activation(ex[:, 0:NW, :], sc[:, 0:NW, :], ACT.Exp).then_inc(exps_ready, 1)
            rows_turned(XT, 0)
            rows_turned(XT2, NW)
            act.wait_ge(logits_shifted, 1)
            act.activation(S0[:, :, :, :], S0[:, :, :, :], ACT.Exp, scale=float(D0) ** -0.5).then_inc(attn_exps, 1)
            act.wait_ge(product_ready, 3 * NW + 5)
            for i in range(T + 2):
                if i < T:
                    rows_turned(XT, i)
                if 1 <= i < T + 1:
                    std(i - 1, i, norm_n(0, i - 1))
                if i == T:
                    act.wait_ge(product_ready, 3 * NW + 1 + 2 * T)
                    rows_turned(XT2, 0)
                if i == T + 1:
                    rows_turned(XT2, 1)
                    rows_turned(XT2, 2)
                if i >= 2:
                    std(i - 2, i - 1, norm_n(1, i - 2))
            for t in range(3, T):
                rows_turned(XT2, t)
            std(0, T, 4 * NW + 2 + 2 * T + 1)
            act.wait_ge(logits_shifted, 2)
            act.activation(gate[:, 1, :], gate[:, 0, :], ACT.Exp).then_inc(attn_exps, 1)

            def x_copied(ff, j, s, affine):
                act.wait_ge(ff.x_turned, j + 1 + ff.slots)
                act.wait_ge(ff.up_ready, j + 1)
                if affine:
                    act.wait_ge(ff.cur_ready, j + 1 + ff.slots)
                    for k in range(KC):
                        ins = act.activation(xTs[:, s, k, :], b_x[:, k * P:(k + 1) * P], ACT.Identity,
                                             scale=cur[:, s, k:k + 1], bias=cur[:, s, KC + k:KC + k + 1])
                else:
                    ins = act.activation(xTs[:, s, :, :].rearrange("p k n -> p (k n)"), b_x[:, 0:C], ACT.Copy)
                ins.then_inc(ff.xT_ready, 1)

            def h_stored(ff, j):
                act.wait_ge(ff.up_ready, j + 1 + ff.slots)
                act.wait_ge(ff.h_turned, j + ff.slots)
                for n in range(2):
                    ins = act.activation(h_sb[:, n * 512:(n + 1) * 512], b_h[n][:, :], ACT.Copy)
                ins.then_inc(ff.h_copied, 1)

            def activated(ff, j, func):
                act.wait_ge(ff.down_ready, j + ff.slots)
                for n in range(2):
                    act.wait_ge(ff.biased, (j + ff.slots) * 2 + n + 1)
                    act.activation(hTs.rearrange("p f n -> p (f n)")[:, n * 512:(n + 1) * 512], hb[:, n * 512:(n + 1) * 512],
                                   func).then_inc(ff.active, 1)

            def expert_tiles(ff, count, affine, func):
                n = ff.slots
                x_copied(ff, 0, 0, affine)
                h_stored(ff, 0)
                x_copied(ff, 1, 1, affine)
                activated(ff, 0, func)

                def body(j, s, left=3):
                    h_stored(ff, j + 1)
                    if left > 2:
                        x_copied(ff, j + 2, (s + 2) % n, affine)
                    activated(ff, j + 1, func)
                trips = (count - 2) // n
                with act.Fori(0, trips) as i:
                    for s in range(n):
                        body(i * n + s, s)
                for j in range(n * trips, count - 1):
                    body(j, j % n, count - j)

            expert_tiles(ff0, NT0, True, ACT.Gelu)
            n_std, n_mm = 4 * NW + 2 + 2 * T + 2, [PRODUCTS_1]

            def product_copied(dst):
                n = n_mm[0]
                n_mm[0] += 1
                act.wait_ge(product_ready, n + 1)
                act.activation(dst, b_mm[n % 4][:, :], ACT.Copy).then_inc(product_read, 1)
            std(0, 1, n_std)
            std(1, 2, n_std + 1)
            rows_turned(XT, 0)

            def squared(t):
                for h in range(2 * H1):
                    own = slice(h * D1, (h + 1) * D1)
                    ins = act.activation(squares[:, own], qkv1[:, t, own], ACT.Square, accum_out=ssq[:, t, h:h + 1])
                return ins
            for t in range(T):
                if t == 0:
                    std(2, 3, n_std + 2)
                if t + 1 < T:
                    rows_turned(XT, t + 1)
                if t == 1:
                    for i in range(3, T):
                        std(i, i + 1, n_std + i)
                for i in range(2):
                    product_copied(qkv1[:, t, i * INNER:(i + 1) * INNER])
                act.wait_ge(product_read, n_mm[0])
                if t >= 2:
                    squared(t - 2)
            for t in range(T):
                product_copied(qkv1[:, t, 2 * INNER:3 * INNER])
            act.wait_ge(pool_products_used, T - 2)
            act.activation(last_squares, qkv1[:, T - 1, 0:2 * INNER], ACT.Square).then_inc(squares_ready, 1)
            step(squared(T - 2))
            act.wait_ge(norms_ready, 1)
            act.activation(rnorm[:, :, :], ssq[:, :, :], ACT.Sqrt).then_inc(norms_ready, 1)
            act.wait_ge(logits_shifted, 3)
            act.activation(S1[:, :, :, :], S1[:, :, :, :], ACT.Exp, scale=16.0, bias=neg16[:, 0:1]).then_inc(attn_exps, 1)
            for t in range(T):
                rows_turned(OT, t, chunks=KI)
            std(0, T, n_std + T)
            act.wait_ge(product_ready, n_mm[0] + T)
            for t in range(T):
                rows_turned(XT, t)
            act.wait_ge(logits_shifted, 4)
            act.activation(lg2[:, :, :], lg[:, :, :], ACT.Exp).then_inc(attn_exps, 1)
            expert_tiles(ff1, NPAIR, False, ACT.Relu)
            for t in range(T):
                std(t, t + 1, n_std + T + 1 + t)

        @block.vector
        def _(dve):
            step = Steps(dve, dve_step)

            def rstd(lo, hi, n):
                dve.wait_ge(std_ready, n)
                step(dve.reciprocal(rs[:, lo:hi], sd[:, lo:hi]))

            def normed(dst, src, i):
                return dve.tensor_scalar(dst, src, mv[:, i, 0:1], rs[:, i:i + 1], ALU.subtract, ALU.mult)

            dve.wait_ge(cls_loaded, 16)
            dve.wait_ge(consts_made, N_CONST)
            step(dve.bn_stats(stats[:, 0, :], cls_r))
            dve.bn_aggr(mv[:, 0, :], stats[:, 0, :]).then_inc(var_ready, 1)
            rstd(0, 1, 1)
            normed(redhat, cls_r, 0).then_inc(redhat_ready, 1)
            dve.sem_inc(xhat_ready, 1)
            dve.sem_inc(agg_ready, 1)
            for ff in (ff0, ff1):
                for s in (ff.cur_ready, ff.y_ready):
                    dve.sem_inc(s, ff.slots)
                dve.sem_inc(ff.biased, ff.slots * 2)

            def finish(lo, w):
                rstd(lo, lo + 3, w * 4 + lo // 3 + 2)
                for p in range(lo, lo + 3):
                    normed(xhat[:, p, :], pe_raw[:, p, :], p).then_inc(xhat_ready, 1)

            WEIGH_STEPS = 4

            def weigh_values(w):
                dve.wait_ge(exps_ready, w + 1)
                step(dve.tensor_reduce(hx[:, 1, :], ex[:, :, :].rearrange("p n h -> p h n"), AX.X, ALU.add))
                step(dve.reciprocal(hx[:, 2, :], hx[:, 1, :]))
                step(dve.tensor_tensor(ex[:, :, :], ex[:, :, :], hx[:, 2, :].unsqueeze(1).to_broadcast([P, NP, H8]), ALU.mult))
                vals = kvw[:, :, C:2 * C]
                step(dve.tensor_tensor(vals.rearrange("p n (h d) -> p n h d", h=H8), vals.rearrange("p n (h d) -> p n h d", h=H8),
                                       ex[:, :, :].unsqueeze(3).to_broadcast([P, NP, H8, DH]), ALU.mult))

            def sum_values(w):
                vals = kvw[:, :, C:2 * C]
                dve.tensor_reduce(agg[:, bass.ds(w, 1), :].rearrange("p a c -> p (a c)"), vals.rearrange("p n c -> p c n"),
                                  AX.X, ALU.add).then_inc(agg_ready, 1)

            def window(w, first=False):
                for p in range(NP):
                    dve.wait_ge(conv_copied, w * NP + p + 1 + CREDIT)
                    ins = dve.bn_stats(stats[:, p, :], pe_raw[:, p, :])
                    if p % 3 == 2:
                        step(ins)
                    if p in (5, 8):
                        finish(p - 5, w)
                    if p in (3, 5, 8):
                        batch = {3: 0, 5: 3, 8: 6}[p]
                        for i in range(batch, batch + 3):
                            ins = dve.bn_aggr(mv[:, i, :], stats[:, i, :])
                        ins.then_inc(var_ready, 1)
                    if not first and p == 1:
                        weigh_values(w - 1)
                    if not first and p == 3:
                        sum_values(w - 1)
                step(dve.tensor_reduce(redhat, pe_raw.rearrange("p n c -> p c n"), AX.X, ALU.add))
                finish(6, w)
                step(dve.tensor_scalar(red, redhat, 1.0 / NP, None, ALU.mult))
                dve.wait_ge(rows_loaded, 16 * N_ROWS)
                step(dve.bn_stats(stats[:, 0, :], red))
                dve.tensor_tensor(redb[:, bass.ds(w, 1), :].rearrange("p a c -> p (a c)"), red, projb_r, ALU.add)
                dve.bn_aggr(mv[:, 0, :], stats[:, 0, :]).then_inc(var_ready, 1)
                rstd(0, 1, w * 4 + 5)
                normed(redhat, red, 0).then_inc(redhat_ready, 1)
                dve.wait_ge(q_copied, w + 2)
                for lo, hi in ((0, 4), (4, NP - 1), (NP - 1, NP)):
                    dve.wait_ge(kv_copied, w * NP + hi + CREDIT)
                    keys = kvw[:, lo:hi, 0:C]
                    step(dve.tensor_tensor(keys, keys, q_sb.unsqueeze(1).to_broadcast([P, hi - lo, C]), ALU.mult))
                    step(dve.tensor_reduce(sc[:, lo:hi, :],
                                           keys.rearrange("p n (h d) -> p n h d", h=H8), AX.X, ALU.add))
                step(dve.tensor_reduce(hx[:, 0, :], sc[:, :, :].rearrange("p n h -> p h n"), AX.X, ALU.max))
                dve.tensor_tensor(sc[:, :, :], sc[:, :, :], hx[:, 0, :].unsqueeze(1).to_broadcast([P, NP, H8]),
                                  ALU.subtract).then_inc(scores_shifted, 1)

            before = step.n
            window(0, first=True)
            base, per = step.n, step.n - before + WEIGH_STEPS
            with dve.Fori(1, NW) as w:
                step.loop(base, w - 1, per)
                window(w)
            step.loop(base, NW - 1, per)
            weigh_values(NW - 1)
            sum_values(NW - 1)

            n_mm = [0]

            def product():
                n = n_mm[0]
                n_mm[0] += 1
                dve.wait_ge(product_ready, n + 1)
                return b_mm[n % 4]

            for n in range(NW):
                b = product()
                dve.tensor_tensor(local[:, n, :], b[:, 0:C], redb[:, n, :], ALU.add).then_inc(product_read, 1)
                dve.wait_ge(product_read, n + 1)
                dve.bn_stats(stats[:, n, :], local[:, n, :]).then_inc(rows_ready, 1)
            dve.wait_ge(rows_ready, NW)
            for n in range(NW):
                ins = dve.bn_aggr(mv[:, n, :], stats[:, n, :])
            ins.then_inc(var_ready, 1)
            for n in range(NW):
                b = product()
                dve.tensor_tensor(hA[:, n, :], b[:, 0:C], modb_r, ALU.add).then_inc(product_read, 1)
            rstd(0, NW, NW * 4 + 2)
            for n in range(NW):
                normed(lhat[:, n, :], local[:, n, :], n).then_inc(rows_ready, 1)
            for n in range(NW):
                b = product()
                scored = step.mark(dve.tensor_tensor(gprod[:, n, :], b[:, 0:C], gq_sb[:, :], ALU.mult))
                dve.tensor_copy(gkv[:, n, C:2 * C], b[:, C:2 * C]).then_inc(product_read, 1)
                step.after(scored)
                ins = dve.tensor_reduce(sc[:, n, :], gprod[:, n, :].rearrange("p (h d) -> p h d", h=H8), AX.X, ALU.add)
            step(ins)
            dve.wait_ge(product_read, 3 * NW)
            step(dve.tensor_reduce(hx[:, 0, :], sc[:, 0:NW, :].rearrange("p n h -> p h n"), AX.X, ALU.max))
            dve.tensor_tensor(sc[:, 0:NW, :], sc[:, 0:NW, :], hx[:, 0, :].unsqueeze(1).to_broadcast([P, NW, H8]),
                              ALU.subtract).then_inc(scores_shifted, 1)
            dve.wait_ge(exps_ready, NW + 1)
            step(dve.tensor_reduce(hx[:, 1, :], ex[:, 0:NW, :].rearrange("p n h -> p h n"), AX.X, ALU.add))
            step(dve.reciprocal(hx[:, 2, :], hx[:, 1, :]))
            step(dve.tensor_tensor(ex[:, 0:NW, :], ex[:, 0:NW, :], hx[:, 2, :].unsqueeze(1).to_broadcast([P, NW, H8]), ALU.mult))
            step(dve.tensor_tensor(gprod.rearrange("p n (h d) -> p n h d", h=H8),
                                   gkv[:, :, C:2 * C].rearrange("p n (h d) -> p n h d", h=H8),
                                   ex[:, 0:NW, :].unsqueeze(3).to_broadcast([P, NW, H8, DH]), ALU.mult))
            dve.tensor_reduce(gagg, gprod.rearrange("p n c -> p c n"), AX.X, ALU.add).then_inc(rows_ready, 1)
            dve.wait_ge(rows_ready, 2 * NW + 1)
            step(dve.tensor_tensor(gprod[:, 0, :], cls_r, gprojb_r, ALU.add))

            def read_product(dst, row_):
                b = product()
                width = dst.free_size()
                if row_ is None:
                    dve.tensor_copy(dst, b[:, 0:width]).then_inc(product_read, 1)
                else:
                    dve.tensor_tensor(dst, b[:, 0:width], row_, ALU.add).then_inc(product_read, 1)

            def qkv_read(t):
                read_product(qkv0[:, t, 0:2 * C], bqkv_r[:, 0:2 * C])
                read_product(qkv0[:, t, 2 * C:3 * C], bqkv_r[:, 2 * C:3 * C])

            def spread(a, n, where):
                shape = list(a.shape)
                shape.insert(where, n)
                return a.unsqueeze(where).to_broadcast(shape)

            def scores0(t):
                dve.wait_ge(product_read, n_mm[0])
                pr = prod0[:, 0:t + 1, :]
                step(dve.tensor_tensor(pr, qkv0[:, 0:t + 1, C:2 * C], spread(qkv0[:, t, 0:C], t + 1, 1), ALU.mult))
                step(dve.tensor_reduce(S0[:, t, :, 0:t + 1].rearrange("p h s -> p s h"),
                                       pr.rearrange("p s (h d) -> p s h d", h=H0), AX.X, ALU.add))
            qkv_read(0)
            qkv_read(1)
            b = product()
            dve.tensor_tensor(hA[:, NW, :], b[:, 0:C], gprod[:, 0, :], ALU.add).then_inc(product_read, 1)
            for t in range(T):
                if t >= 2:
                    qkv_read(t)
                scores0(t)
            flat0 = S0[:, :, :, :].rearrange("p t h s -> p (t h) s")
            step(dve.tensor_reduce(hs[:, 0, :], flat0, AX.X, ALU.max))
            dve.tensor_tensor(flat0, flat0, spread(hs[:, 0, :], T, 2), ALU.subtract).then_inc(logits_shifted, 1)
            dve.wait_ge(attn_exps, 1)
            step(dve.tensor_reduce(hs[:, 1, :], flat0, AX.X, ALU.add))
            step(dve.reciprocal(hs[:, 2, :], hs[:, 1, :]))
            step(dve.tensor_tensor(flat0, flat0, spread(hs[:, 2, :], T, 2), ALU.mult))
            for t in range(T):
                if t >= 3:
                    dve.wait_ge(turned, TURNED_0 + t - 2)
                pr = weighted0[t % 3]
                ins = dve.tensor_tensor(pr[:, 0:t + 1, :].rearrange("p s (h d) -> p s h d", h=H0),
                                        qkv0[:, 0:t + 1, 2 * C:3 * C].rearrange("p s (h d) -> p s h d", h=H0),
                                        spread(S0[:, t, :, 0:t + 1].rearrange("p h s -> p s h"), D0, 3), ALU.mult)
                if t >= 3:
                    step(ins)
                    ins = dve.tensor_tensor(pr[:, 0:2, :], pr[:, 0:2, :], pr[:, 2:4, :], ALU.add)
                ins.then_inc(rows_ready, 1)

            n_std = [NW * 4 + 2]

            dve.tensor_tensor(residual, hA, spread(beta_r, T, 1), ALU.add)
            banks = []
            for i in range(1, T + 3):
                ta, tb, tc = i - 1, i - 2, i - 3
                has_a, has_b, has_c = ta < T, 0 <= tb < T, 0 <= tc
                if has_c:
                    dve.wait_ge(std_ready, norm_n(1, tc))
                    inv_c = step.mark(dve.reciprocal(rs[:, tc:tc + 1], sd[:, tc:tc + 1]))
                if has_b:
                    dve.wait_ge(std_ready, norm_n(0, tb))
                    step.mark(dve.reciprocal(rs[:, tb:tb + 1], sd[:, tb:tb + 1]))
                    centred = step.mark(dve.scalar_tensor_tensor(yln[:, tb, :], banks[tb][:, 0:C], mv[:, tb, 0:1], gamma_r,
                                                                 ALU.subtract, ALU.mult))
                if has_c:
                    step.after(inv_c)
                    normed(hB[:, tc, :], yln[:, tc, :], tc).then_inc(rows_ready, 1)
                if has_b:
                    step.after(centred)
                    summed = step.mark(dve.scalar_tensor_tensor(yln[:, tb, :], yln[:, tb, :], rs[:, tb:tb + 1],
                                                                residual[:, tb, :], ALU.mult, ALU.add))
                if has_a:
                    banks.append(product())
                    stats_a = step.mark(dve.bn_stats(stats[:, ta, :], banks[ta][:, 0:C]))
                if has_b:
                    step.after(summed)
                    stats_b = step.mark(dve.bn_stats(stats[:, tb, :], yln[:, tb, :]))
                if has_a:
                    step.after(stats_a)
                    dve.bn_aggr(mv[:, ta, :], stats[:, ta, :]).then_inc(var_ready, 1)
                if has_b:
                    step.after(stats_b)
                    dve.bn_aggr(mv[:, tb, :], stats[:, tb, :]).then_inc(var_ready, 1)
                    dve.sem_inc(product_read, 1)
            n_std[0] += 2 * T
            dve.wait_ge(rows_ready, R0 + 2 * T)
            for t in range(T):
                ins = dve.bn_stats(stats[:, t, :], hB[:, t, :])
            step(ins)
            for t in range(T):
                ins = dve.bn_aggr(mv[:, t, :], stats[:, t, :])
            ins.then_inc(var_ready, 1)
            for t in range(T):
                read_product(lg[:, t, 0:E0], rb_r)
            dve.wait_ge(product_read, n_mm[0])
            for t in range(T):
                ins = dve.max(best[:, t, :], lg[:, t, 0:E0])
            step(ins)
            for t in range(T):
                ins = dve.max_index(besti[:, t, :], best[:, t, :], lg[:, t, 0:E0])
            step(ins)
            dve.tensor_tensor(gate[:, 0, :], best[:, :, 1], best[:, :, 0], ALU.subtract).then_inc(logits_shifted, 1)
            step(dve.tensor_copy(bestf[:, :, :], besti[:, :, 0:2]))
            step(dve.tensor_tensor(oh[:, :, :, 0:E0], spread(spread(iota_e[:, 0:E0], T, 1), 2, 1),
                                   spread(bestf[:, :, :].rearrange("p t k -> p k t"), E0, 3), ALU.is_equal))
            step(dve.tensor_tensor(msum[:, :, 0:E0], oh[:, 0, :, 0:E0], oh[:, 1, :, 0:E0], ALU.add))

            def tiles_before(width):
                step(dve.memset(mcum[:, 0, 0:width], 0.0))
                for t in range(1, T):
                    step(dve.tensor_tensor(mcum[:, t, 0:width], mcum[:, t - 1, 0:width],
                                           (msum if width == E0 else oh[:, 0])[:, t - 1, 0:width], ALU.add))
            tiles_before(E0)
            dve.sem_inc(rows_ready, 1)
            n_std[0] += 1
            rstd(0, T, n_std[0])
            for t in range(T):
                ins = normed(hX[:, t, :], hB[:, t, :], t)
            step(ins)
            b = product()
            step(dve.tensor_tensor(full[:, :, :], spread(b[:, 256:256 + E0], T, 2), spread(tile_starts[:, :], E0, 1), ALU.is_gt))
            step(dve.tensor_reduce(ntile[:, :], full[:, :, :], AX.X, ALU.add))
            step(dve.tensor_tensor_scan(incl[:, :], ones_sb[:, 0:E0], ntile[:, :], 0.0, ALU.mult, ALU.add))
            step(dve.tensor_tensor(basee[:, :], incl[:, :], ntile[:, :], ALU.subtract))
            dve.scalar_tensor_tensor(rk[:, :, 0:E0], spread(basee[:, :], T, 1), float(P),
                                     b[:, 0:T * E0].rearrange("p (t e) -> p t e", t=T), ALU.mult, ALU.add).then_inc(product_read, 1)
            dve.wait_ge(product_read, n_mm[0])
            step(dve.tensor_tensor(oh[:, :, :, 0:E0], oh[:, :, :, 0:E0], spread(rk[:, :, 0:E0], 2, 1), ALU.mult))
            step(dve.tensor_reduce(slotf[:, :, :], oh[:, :, :, 0:E0], AX.X, ALU.add))
            dve.tensor_copy(slotu[:, :, :], slotf[:, :, :]).then_inc(slots_ready, 1)
            step(dve.tensor_tensor(cmp_t[:, :, :], spread(iota_t[:, 0:NT0], E0, 2), spread(incl[0:1, :], NT0, 1), ALU.is_ge))
            step(dve.tensor_reduce(eidf[:, :], cmp_t[:, :, :], AX.X, ALU.add))
            step(dve.tensor_scalar(eidf[:, :], eidf[:, :], float(E0 - 1), None, ALU.min))
            dve.tensor_copy(eid[:, :], eidf[:, :]).then_inc(route_ready, 1)
            dve.wait_ge(setup_copied, NCH + 2)
            for k in range(KC):
                dve.tensor_copy(tab[:, :, k], vecT[:, k, 8:8 + E0])
                dve.tensor_copy(tab[:, :, KC + k], vecT[:, k, 16:16 + E0])
            step(dve.tensor_copy(tab[:, :, 2 * KC:].rearrange("p e f -> p f e"), b1T[:, :, 0:E0]))
            dve.wait_ge(attn_exps, 2)
            step(dve.tensor_scalar(gate[:, 0, :], gate[:, 1, :], 1.0, None, ALU.add))
            step(dve.reciprocal(gate[:, 2, :], gate[:, 0, :]))
            step(dve.tensor_tensor(gate[:, 3, :], gate[:, 1, :], gate[:, 2, :], ALU.mult))
            step(dve.tensor_tensor(gate[:, 0, :], gate[:, 2, :], gate[:, 3, :], ALU.add))
            step(dve.tensor_scalar(gate[:, 0, :], gate[:, 0, :], 1.0, None, ALU.add))
            dve.wait_ge(route_ready, 1)

            def biased0(ff, j, s):
                dve.wait_ge(ff.h_turned, j + 1 + ff.slots)
                dve.wait_ge(ff.active, (j + ff.slots) * 2)
                for n in range(2):
                    ins = dve.tensor_tensor(hb[:, n * 512:(n + 1) * 512].rearrange("p (f n) -> p f n", f=4),
                                            b_hT[n][:, :].rearrange("p (f n) -> p f n", f=4),
                                            spread(cur[:, s, 2 * KC + 4 * n:2 * KC + 4 * n + 4], P, 2), ALU.add)
                    ins.then_inc(ff.biased, 1)

            def biased1(ff, j, s):
                dve.wait_ge(ff.h_turned, j + 1 + ff.slots)
                dve.wait_ge(ff.active, (j + ff.slots) * 2)
                for n in range(2):
                    bias = b1T[:, 4 * n:4 * n + 4, bass.ds(j * 2 + E0, 2)]
                    ins = dve.tensor_tensor(hb[:, n * 512:(n + 1) * 512].rearrange("p (f e n) -> p f e n", f=4, e=2),
                                            b_hT[n][:, :].rearrange("p (f e n) -> p f e n", f=4, e=2),
                                            spread(bias, SLOT, 3), ALU.add)
                    ins.then_inc(ff.biased, 1)

            def y_read(ff, j, s, i, loads):
                dve.wait_ge(ff.down_ready, j + 1 + ff.slots)
                dve.wait_ge(ff.w2_loaded[s], i * (16 * loads) + 16 * loads)
                dve.wait_ge(ff.y_free, j + 1)
                dve.tensor_tensor(y_sb[:, s, :], b_y[:, 0:C], b2_r[:, s, :], ALU.add).then_inc(ff.y_ready, 1)

            def expert_tiles(ff, count, cur_read, biased, loads):
                n = ff.slots
                cur_read(0, 0)
                cur_read(1, 1)
                biased(ff, 0, 0)

                def body(j, s, i, left=3):
                    if left > 2:
                        cur_read(j + 2, (s + 2) % n)
                    y_read(ff, j, s, i, loads)
                    if left > 1:
                        biased(ff, j + 1, (s + 1) % n)
                trips = (count - 2) // n
                with dve.Fori(0, trips) as i:
                    for s in range(n):
                        body(i * n + s, s, i)
                for j in range(n * trips, count):
                    body(j, j % n, j // n, count - j)

            with dve.register("tile_expert") as expert:
                def cur_read(j, s):
                    dve.reg_load(expert, eid[0:1, bass.ds(j, 1)])
                    e = dve.snap(expert, min_val=0, max_val=E0 - 1)
                    dve.wait_ge(ff0.xT_ready, j + 1)
                    dve.wait_ge(ff0.biased, j * 2 + 2)
                    dve.tensor_copy(cur[:, s, :].unsqueeze(1), tab[:, bass.ds(e, 1), :]).then_inc(ff0.cur_ready, 1)
                expert_tiles(ff0, NT0, cur_read, biased0, 2)

            for t in range(T):
                ins = dve.tensor_scalar(hX[:, t, :], hB[:, t, :], gate[:, 0, t:t + 1], None, ALU.mult)
            step(ins)

            def normed_tiles(first, second, dst):
                for t in range(T + 1):
                    more = t < T
                    if more:
                        made = step.mark(first(t))
                    if t:
                        n_std[0] += 1
                        dve.wait_ge(std_ready, n_std[0])
                        inv = step.mark(dve.reciprocal(rs[:, t - 1:t], sd[:, t - 1:t]))
                    if more and second is not None:
                        step.after(made)
                        made = step.mark(second(t))
                    if t:
                        step.after(inv)
                        normed(dst[:, t - 1, :], hX[:, t - 1, :], t - 1).then_inc(rows_ready, 1)
                    if more:
                        step.after(made)
                        step(dve.bn_stats(stats[:, t, :], hX[:, t, :]))
                        dve.bn_aggr(mv[:, t, :], stats[:, t, :]).then_inc(var_ready, 1)

            def add_expert(k):
                def add(t):
                    if k == 0:
                        dve.wait_ge(gathered[t], 16 * 2)
                    return dve.scalar_tensor_tensor(hX[:, t, :], yg[:, k, t, :], gate[:, 2 + k, t:t + 1], hX[:, t, :],
                                                    ALU.mult, ALU.add)
                return add
            normed_tiles(add_expert(0), add_expert(1), hA)

            copied = n_mm[0]
            n_mm[0] += 3 * T

            def scores(dst, n, a, b_):
                step(dve.tensor_tensor(prod1[:, 0:n, :], a, b_, ALU.mult))
                step(dve.tensor_reduce(dst, prod1[:, 0:n, :].rearrange("p s (h d) -> p s h d", h=H1), AX.X, ALU.add))
            for t in range(T):
                dve.wait_ge(product_read, copied + 2 * t + 2)
                scores(S1[:, t, :, 0:t + 1].rearrange("p h s -> p s h"), t + 1,
                       qkv1[:, 0:t + 1, INNER:2 * INNER], spread(qkv1[:, t, 0:INNER], t + 1, 1))
                if t > 2:
                    scores(S1[:, 2:t, :, t], t - 2, qkv1[:, 2:t, 0:INNER], spread(qkv1[:, t, INNER:2 * INNER], t - 2, 1))
                if t:
                    n = min(t, 2)
                    dve.wait_ge(pool_products, t)
                    dve.tensor_reduce(S1[:, 0:n, :, t], pool_prod[t % 2][:, 0:n, :].rearrange("p s (h d) -> p s h d", h=H1),
                                      AX.X, ALU.add).then_inc(pool_products_used, 1)
            dve.wait_ge(squares_ready, 1)
            dve.tensor_reduce(ssq[:, T - 1, :], last_squares.rearrange("p (h d) -> p h d", h=2 * H1), AX.X, ALU.add)\
                .then_inc(norms_ready, 1)
            dve.wait_ge(pool_products_used, T - 1)
            dve.wait_ge(norms_ready, 2)
            step(dve.tensor_scalar(ssq[:, :, :], rnorm[:, :, :], 1e-12, None, ALU.max))
            step(dve.reciprocal(rnorm[:, :, :], ssq[:, :, :]))
            step(dve.tensor_tensor(S1[:, :, :, :], S1[:, :, :, :], spread(rnorm[:, :, 0:H1], T, 3), ALU.mult))
            dve.tensor_tensor(S1[:, :, :, :], S1[:, :, :, :], spread(rnorm[:, :, H1:].rearrange("p s h -> p h s"), T, 1),
                              ALU.mult).then_inc(logits_shifted, 1)
            dve.wait_ge(attn_exps, 3)
            flat1 = S1[:, :, :, :].rearrange("p t h s -> p (t h) s")
            hs1 = hs[:, :, 0:T * H1]
            step(dve.tensor_reduce(hs1[:, 0, :], flat1, AX.X, ALU.add))
            step(dve.tensor_scalar(hs1[:, 1, :], hs1[:, 0, :], 1e-6, None, ALU.max))
            step(dve.reciprocal(hs1[:, 2, :], hs1[:, 1, :]))
            step(dve.tensor_tensor(flat1, flat1, spread(hs1[:, 2, :], T, 2), ALU.mult))
            dve.wait_ge(product_read, n_mm[0])

            def attended(t):
                b = product()
                dve.tensor_tensor(hX[:, t, :], b[:, 0:C], hA[:, t, :], ALU.add).then_inc(product_read, 1)
                dve.wait_ge(product_read, n_mm[0])
                return dve.bn_stats(stats[:, t, :], hX[:, t, :])
            for t in range(T):
                pr = weighted1[t % 3]
                if t >= 3:
                    dve.wait_ge(turned, TURNED_1 + t - 2)
                step(dve.tensor_tensor(pr.rearrange("p s (h d) -> p s h d", h=H1),
                                       qkv1[:, :, 2 * INNER:].rearrange("p s (h d) -> p s h d", h=H1),
                                       spread(S1[:, t, :, :].rearrange("p h s -> p s h"), D1, 3), ALU.mult))
                dve.tensor_tensor(pr[:, 0:2, :], pr[:, 0:2, :], pr[:, 2:4, :], ALU.add).then_inc(rows_ready, 1)
                if t >= 2:
                    attended(t - 2)
            attended(T - 2)
            step(attended(T - 1))
            for t in range(T):
                ins = dve.bn_aggr(mv[:, t, :], stats[:, t, :])
            ins.then_inc(var_ready, 1)
            n_std[0] += 1
            rstd(0, T, n_std[0])
            for t in range(T):
                normed(hB[:, t, :], hX[:, t, :], t).then_inc(rows_ready, 1)

            for t in range(T):
                read_product(lg[:, t, :], bg_r)
            dve.wait_ge(product_read, n_mm[0])
            step(dve.tensor_reduce(gate[:, 0, :], lg[:, :, :], AX.X, ALU.max))
            dve.tensor_tensor(lg[:, :, :], lg[:, :, :], spread(gate[:, 0, :], E1, 2), ALU.subtract).then_inc(logits_shifted, 1)
            dve.wait_ge(attn_exps, 4)
            for t in range(T):
                ins = dve.max(best[:, t, :], lg2[:, t, :])
            step(ins)
            for t in range(T):
                ins = dve.max_index(besti[:, t, :], best[:, t, :], lg2[:, t, :])
            step(ins)
            step(dve.tensor_copy(bestf[:, :, :], besti[:, :, 0:2]))
            step(dve.tensor_tensor(oh[:, 0, :, :], spread(iota_e[:, :], T, 1), spread(bestf[:, :, 0], E1, 2), ALU.is_equal))
            dve.tensor_reduce(msum[:, 0, :], oh[:, 0, :, :].rearrange("p t e -> p e t"), AX.X, ALU.add).then_inc(rows_ready, 1)
            tiles_before(E1)
            step(dve.tensor_reduce(gate[:, 1, :], lg2[:, :, :], AX.X, ALU.add))
            step(dve.reciprocal(gate[:, 2, :], gate[:, 1, :]))
            step(dve.scalar_tensor_tensor(slotf[:, 1, :], bestf[:, :, 0], float(SLOT), trash[:, :], ALU.mult, ALU.subtract))
            b = product()
            dve.tensor_tensor(rk[:, :, :], mcum[:, :, :], spread(b[:, 0:E1], T, 1), ALU.add).then_inc(product_read, 1)
            dve.wait_ge(product_read, n_mm[0])
            step(dve.tensor_tensor(oh[:, 0, :, :], oh[:, 0, :, :], rk[:, :, :], ALU.mult))
            step(dve.tensor_reduce(slotf[:, 0, :], oh[:, 0, :, :], AX.X, ALU.add))
            dve.tensor_scalar(gate[:, 0, :], slotf[:, 0, :], float(CAP), None, ALU.is_lt)
            step(dve.tensor_tensor(slotf[:, 1, :], slotf[:, 0, :], slotf[:, 1, :], ALU.add))
            step(dve.tensor_tensor(slotf[:, 1, :], slotf[:, 1, :], gate[:, 0, :], ALU.mult))
            step(dve.tensor_tensor(slotf[:, 1, :], slotf[:, 1, :], trash[:, :], ALU.add))
            dve.tensor_copy(slotu[:, 0, :], slotf[:, 1, :]).then_inc(slots_ready, 1)
            step(dve.tensor_scalar(slotf[:, 0, :], slotf[:, 0, :], float(CAP), None, ALU.min))
            step(dve.scalar_tensor_tensor(slotf[:, 0, :], bestf[:, :, 0], float(SLOT), slotf[:, 0, :], ALU.mult, ALU.add))
            dve.tensor_copy(gslotu[:, :], slotf[:, 0, :])
            step(dve.tensor_tensor(gate[:, 3, :], gate[:, 0, :], gate[:, 2, :], ALU.mult))
            expert_tiles(ff1, NPAIR, lambda j, s: None, biased1, 3)

            def expert_row(t):
                dve.wait_ge(gathered[t], 16 * 3)
                return dve.scalar_tensor_tensor(hX[:, t, :], yg[:, 0, t, :], gate[:, 3, t:t + 1], hB[:, t, :],
                                                ALU.mult, ALU.add)
            normed_tiles(expert_row, None, hA)


TOK, A0, FF0, A1, FF1 = "L0_tok_", "L0_attn_", "L0_ffn_", "L1_attn_", "L1_ffn_"


def kernel(**inputs):
    import numpy as _np
    import concourse.bacc as _bacc
    from concourse import mybir as _mybir
    from concourse.bass_utils import run_bass_kernel_spmd as _run

    nc = _bacc.Bacc("TRN2", target_bir_lowering=False, num_devices=1)
    arrays = {}

    def arg(name):
        a = _np.ascontiguousarray(inputs[name])
        arrays[f"in_{name}_dram"] = a
        return nc.dram_tensor(f"in_{name}_dram", a.shape, _mybir.dt.from_np(a.dtype), kind="ExternalInput").ap()

    vecs = [arg(TOK + n) for n in ("la_ln_q_g", "la_ln_q_b", "la_ln_kv_g", "la_ln_kv_b",
                                   "ga_ln_q_g", "ga_ln_q_b", "ga_ln_kv_g", "ga_ln_kv_b")]
    B, T, C = inputs["x"].shape[0], 5, inputs[A0 + "Wo"].shape[1]
    out = nc.dram_tensor("out_0_dram", (B, T, C), _mybir.dt.float32, kind="ExternalOutput").ap()
    build_program(
        nc, arg("x"), arg(TOK + "conv_w"), arg(TOK + "class_emb"), vecs, arg(TOK + "la_wq"), arg(TOK + "la_wkv"),
        arg(TOK + "la_proj_w"), arg(TOK + "la_proj_b"), arg(TOK + "ga_wq"), arg(TOK + "ga_wkv"),
        arg(TOK + "ga_proj_w"), arg(TOK + "ga_proj_b"), arg(TOK + "mod_w"), arg(TOK + "mod_b"),
        [arg(A0 + n) for n in ("Wq", "Wk", "Wv")], [arg(A0 + n) for n in ("bq", "bk", "bv")],
        arg(A0 + "Wo"), arg(A0 + "bo"), arg(A0 + "gamma"), arg(A0 + "beta"),
        arg(FF0 + "router_W"), arg(FF0 + "router_b"), arg(FF0 + "ln_g"), arg(FF0 + "ln_b"),
        arg(FF0 + "W1"), arg(FF0 + "b1"), arg(FF0 + "W2"), arg(FF0 + "b2"),
        arg(A1 + "Wq"), arg(A1 + "Wkv"), arg(A1 + "Wo"),
        arg(FF1 + "Wg"), arg(FF1 + "bg"), arg(FF1 + "W1"), arg(FF1 + "b1"), arg(FF1 + "W2"), arg(FF1 + "b2"), out)
    r = _run(nc, [arrays], core_ids=[0])
    return r.results[0]["out_0_dram"]
```
